# Optimizing a Trainium2 kernel written in Bass

```python
import numpy as np
import jax
import jax.numpy as jnp

def _softmax(x, axis=-1):
    return jax.nn.softmax(x, axis=axis)

def _gelu(x):
    return jax.nn.gelu(x, approximate=True)

def _silu(x):
    return jax.nn.silu(x)

def _sigmoid(x):
    return jax.nn.sigmoid(x)

def _layernorm(x, axis=-1, eps=1e-05):
    m = jnp.mean(x, axis=axis, keepdims=True)
    v = jnp.var(x, axis=axis, keepdims=True)
    return (x - m) / jnp.sqrt(v + eps)

def _scatter_add(tgt, idx, src, axis=0):
    return tgt.at[idx].add(src)

def _segment_sum(src, seg, n):
    return jax.ops.segment_sum(src, seg, n)
kernel_name = 'mk_adaln_ffn_d2_seqx_r8_63d281'

def setup_inputs(seed: int=0):
    np.random.seed(seed)
    _w = jnp.asarray

    def _rec_inputs():
        import jax
        import jax.numpy as jnp
        _rk = jax.random.key(seed)
        x = -0.000125 + 0.9999 * jax.random.normal(jax.random.fold_in(_rk, 1), (64, 32, 512), jnp.float32)
        _lenS = 32 - jax.random.randint(jax.random.fold_in(_rk, 7), (64,), 0, max(1, 32 // 4) + 1, jnp.int32)
        _lenS2 = 32 - jax.random.randint(jax.random.fold_in(_rk, 8), (64,), 0, max(1, 32 // 4) + 1, jnp.int32)
        itok_B_3_7 = jax.random.randint(jax.random.fold_in(_rk, 11), (64,), 3, 8, jnp.int32)
        itok_Bx16_0_63 = jax.random.randint(jax.random.fold_in(_rk, 12), (64, 16), 0, 64, jnp.int32)
        itok_B_207_1644 = jax.random.randint(jax.random.fold_in(_rk, 13), (64,), 207, 1645, jnp.int32)
        return (x, itok_B_3_7, itok_Bx16_0_63, itok_B_207_1644)
    x, itok_B_3_7, itok_Bx16_0_63, itok_B_207_1644 = _rec_inputs()

    def _L0_cond_setup():
        import jax, jax.numpy as jnp
        import numpy as np
        MAX_LORAS, OUT, IN = (8, 512, 512)
        B, S = (4, 256)
        key = jax.random.key(seed)
        k1, k2, k3 = jax.random.split(key, 3)
        x = jax.random.normal(k1, (B, S, IN), dtype=jnp.float32)
        weight = jax.random.normal(k2, (MAX_LORAS, OUT, IN), dtype=jnp.float32) * 0.02
        adapter_ids = jax.random.randint(k3, (B,), 0, MAX_LORAS, dtype=jnp.int32)
        return {'x': x, 'weight': weight, 'adapter_ids': adapter_ids}
    _L0_cond_all = _L0_cond_setup()
    _L0_cond_in = {k: v for k, v in _L0_cond_all.items() if k in ('weight',)}
    del _L0_cond_all

    def _L0_ffn_setup():
        import jax, jax.numpy as jnp
        import numpy as np
        R = 16
        ALPHA = 32
        SCALING = ALPHA / R
        E = 8
        TOP_K = 2
        key = jax.random.key(seed)
        ks = jax.random.split(key, 5)
        B, S, D = (4, 256, 512)
        x = jax.random.normal(ks[0], (B, S, D), dtype=jnp.float32)
        base_W = jax.random.normal(ks[1], (D, D), dtype=jnp.float32) * 0.02
        router_W = jax.random.normal(ks[2], (E, D), dtype=jnp.float32) * 0.02
        lora_A = jax.random.normal(ks[3], (E, D, R), dtype=jnp.float32) * 0.02
        lora_B = jax.random.normal(ks[4], (E, R, D), dtype=jnp.float32) * 0.02
        return {'x': x, 'base_W': base_W, 'router_W': router_W, 'lora_A': lora_A, 'lora_B': lora_B}
    _L0_ffn_all = _L0_ffn_setup()
    _L0_ffn_in = {k: v for k, v in _L0_ffn_all.items() if k in ('base_W', 'router_W', 'lora_A', 'lora_B')}
    del _L0_ffn_all

    def _L1_cond_setup():
        import jax, jax.numpy as jnp
        import numpy as np
        B, S, HID = (4, 128, 512)
        D, HQ, HK = (128, 32, 8)
        PAGES, PSIZE, NPP = (64, 32, 16)
        THETA = 10000.0
        EPS = 1e-06
        SCALE = 1.0 / float(np.sqrt(D))

        def _rmsnorm(t, w):
            var = jnp.mean(t * t, axis=-1, keepdims=True)
            return t * jax.lax.rsqrt(var + EPS) * w

        def _rope(t, pos):
            inv_freq = 1.0 / THETA ** (jnp.arange(0, D, 2, dtype=jnp.float32) / D)
            freqs = pos[..., None].astype(jnp.float32) * inv_freq
            cos = jnp.cos(freqs)[:, :, None, :]
            sin = jnp.sin(freqs)[:, :, None, :]
            t1, t2 = (t[..., :D // 2], t[..., D // 2:])
            return jnp.concatenate([t1 * cos - t2 * sin, t2 * cos + t1 * sin], axis=-1)
        key = jax.random.key(seed)
        ks = jax.random.split(key, 10)
        x = jax.random.normal(ks[0], (B, S, HID), jnp.float32)
        Wq = jax.random.normal(ks[1], (HQ * D, HID), jnp.float32) * 0.02
        Wk = jax.random.normal(ks[2], (HK * D, HID), jnp.float32) * 0.02
        Wv = jax.random.normal(ks[3], (HK * D, HID), jnp.float32) * 0.02
        Wo = jax.random.normal(ks[4], (HID, HQ * D), jnp.float32) * 0.02
        q_norm_w = jax.random.uniform(ks[5], (D,), jnp.float32)
        k_norm_w = jax.random.uniform(ks[6], (D,), jnp.float32)
        k_cache = jax.random.normal(ks[7], (PAGES, PSIZE, HK, D), jnp.float32)
        v_cache = jax.random.normal(ks[8], (PAGES, PSIZE, HK, D), jnp.float32)
        block_table = jnp.arange(B * NPP, dtype=jnp.int32).reshape(B, NPP)
        cache_seqlens = jax.random.randint(ks[9], (B,), 0, 475).astype(jnp.int32)
        return dict(x=x, Wq=Wq, Wk=Wk, Wv=Wv, Wo=Wo, q_norm_w=q_norm_w, k_norm_w=k_norm_w, k_cache=k_cache, v_cache=v_cache, block_table=block_table, cache_seqlens=cache_seqlens)
    _L1_cond_all = _L1_cond_setup()
    _L1_cond_in = {k: v for k, v in _L1_cond_all.items() if k in ('Wq', 'Wk', 'Wv', 'Wo', 'q_norm_w', 'k_norm_w', 'k_cache', 'v_cache')}
    del _L1_cond_all

    def _L1_ffn_setup():
        import jax, jax.numpy as jnp
        import numpy as np
        H = 512
        I = 1376
        CS = 8
        CB = 8192

        def _dequant(codebook, idx):
            return codebook[idx].reshape(idx.shape[0], -1)
        key = jax.random.key(seed)
        k0, k1, k2, k3, k4 = jax.random.split(key, 5)
        x = jax.random.normal(k0, (4, 256, H), dtype=jnp.float32)
        codebook = jax.random.normal(k1, (CB, CS), dtype=jnp.float32)
        idx_gate = jax.random.randint(k2, (I, H // CS), 0, CB, dtype=jnp.int32)
        idx_up = jax.random.randint(k3, (I, H // CS), 0, CB, dtype=jnp.int32)
        idx_down = jax.random.randint(k4, (H, I // CS), 0, CB, dtype=jnp.int32)
        return {'x': x, 'codebook': codebook, 'idx_gate': idx_gate, 'idx_up': idx_up, 'idx_down': idx_down}
    _L1_ffn_all = _L1_ffn_setup()
    _L1_ffn_in = {k: v for k, v in _L1_ffn_all.items() if k in ('codebook', 'idx_gate', 'idx_up', 'idx_down')}
    del _L1_ffn_all
    return {'x': x, 'itok_B_3_7': itok_B_3_7, 'itok_Bx16_0_63': itok_Bx16_0_63, 'itok_B_207_1644': itok_B_207_1644, 'L0_cond_weight': _L0_cond_in['weight'], 'L0_ffn_base_W': _L0_ffn_in['base_W'], 'L0_ffn_router_W': _L0_ffn_in['router_W'], 'L0_ffn_lora_A': _L0_ffn_in['lora_A'], 'L0_ffn_lora_B': _L0_ffn_in['lora_B'], 'L1_cond_Wq': _L1_cond_in['Wq'], 'L1_cond_Wk': _L1_cond_in['Wk'], 'L1_cond_Wv': _L1_cond_in['Wv'], 'L1_cond_Wo': _L1_cond_in['Wo'], 'L1_cond_q_norm_w': _L1_cond_in['q_norm_w'], 'L1_cond_k_norm_w': _L1_cond_in['k_norm_w'], 'L1_cond_k_cache': _L1_cond_in['k_cache'], 'L1_cond_v_cache': _L1_cond_in['v_cache'], 'L1_ffn_codebook': _L1_ffn_in['codebook'], 'L1_ffn_idx_gate': _L1_ffn_in['idx_gate'], 'L1_ffn_idx_up': _L1_ffn_in['idx_up'], 'L1_ffn_idx_down': _L1_ffn_in['idx_down']}

def reference(x, itok_B_3_7, itok_Bx16_0_63, itok_B_207_1644, L0_cond_weight, L0_ffn_base_W, L0_ffn_router_W, L0_ffn_lora_A, L0_ffn_lora_B, L1_cond_Wq, L1_cond_Wk, L1_cond_Wv, L1_cond_Wo, L1_cond_q_norm_w, L1_cond_k_norm_w, L1_cond_k_cache, L1_cond_v_cache, L1_ffn_codebook, L1_ffn_idx_gate, L1_ffn_idx_up, L1_ffn_idx_down):
    import jax
    import jax.numpy as jnp

    def _L0_cond_ref(x, weight, adapter_ids):
        import jax, jax.numpy as jnp
        import numpy as np
        MAX_LORAS, OUT, IN = (8, 512, 512)
        B, S = (4, 256)
        w = weight[adapter_ids]
        return jnp.einsum('bsi,boi->bso', x, w)

    def _L0_ffn_ref(x, base_W, router_W, lora_A, lora_B):
        import jax, jax.numpy as jnp
        import numpy as np
        R = 16
        ALPHA = 32
        SCALING = ALPHA / R
        E = 8
        TOP_K = 2
        base = jnp.einsum('bsd,od->bso', x, base_W)
        logits = jnp.einsum('bsd,ed->bse', x, router_W)
        probs = jax.nn.softmax(logits.astype(jnp.float32), axis=-1)
        top_vals, top_idx = jax.lax.top_k(probs, TOP_K)
        rw = top_vals / jnp.sum(top_vals, axis=-1, keepdims=True)
        w_dense = jnp.sum(jax.nn.one_hot(top_idx, E, dtype=rw.dtype) * rw[..., None], axis=-2).astype(x.dtype)
        mid = jnp.einsum('bsd,edr->bser', x, lora_A)
        mid = mid * w_dense[..., None]
        inc = jnp.einsum('bser,erd->bsd', mid, lora_B)
        return base + inc * SCALING

    def _L1_cond_ref(x, Wq, Wk, Wv, Wo, q_norm_w, k_norm_w, k_cache, v_cache, block_table, cache_seqlens):
        import jax, jax.numpy as jnp
        import numpy as np
        B, S, HID = (4, 128, 512)
        D, HQ, HK = (128, 32, 8)
        PAGES, PSIZE, NPP = (64, 32, 16)
        THETA = 10000.0
        EPS = 1e-06
        SCALE = 1.0 / float(np.sqrt(D))

        def _rmsnorm(t, w):
            var = jnp.mean(t * t, axis=-1, keepdims=True)
            return t * jax.lax.rsqrt(var + EPS) * w

        def _rope(t, pos):
            inv_freq = 1.0 / THETA ** (jnp.arange(0, D, 2, dtype=jnp.float32) / D)
            freqs = pos[..., None].astype(jnp.float32) * inv_freq
            cos = jnp.cos(freqs)[:, :, None, :]
            sin = jnp.sin(freqs)[:, :, None, :]
            t1, t2 = (t[..., :D // 2], t[..., D // 2:])
            return jnp.concatenate([t1 * cos - t2 * sin, t2 * cos + t1 * sin], axis=-1)
        bsz, seqlen, _ = x.shape
        q = jnp.einsum('bsd,ed->bse', x, Wq).reshape(bsz, seqlen, HQ, D)
        k = jnp.einsum('bsd,ed->bse', x, Wk).reshape(bsz, seqlen, HK, D)
        v = jnp.einsum('bsd,ed->bse', x, Wv).reshape(bsz, seqlen, HK, D)
        q = _rmsnorm(q, q_norm_w)
        k = _rmsnorm(k, k_norm_w)
        pos = cache_seqlens[:, None] + jnp.arange(seqlen)[None, :]
        q = _rope(q, pos)
        k = _rope(k, pos)
        L = NPP * PSIZE
        kc = k_cache[block_table].reshape(bsz, L, HK, D)
        vc = v_cache[block_table].reshape(bsz, L, HK, D)
        k_all = jnp.concatenate([kc, k], axis=1)
        v_all = jnp.concatenate([vc, v], axis=1)
        valid_c = jnp.arange(L)[None, :] < cache_seqlens[:, None]
        valid = jnp.concatenate([valid_c, jnp.ones((bsz, seqlen), dtype=bool)], axis=1)
        rep = HQ // HK
        k_all = jnp.repeat(k_all, rep, axis=2)
        v_all = jnp.repeat(v_all, rep, axis=2)
        scores = jnp.einsum('bqhd,bkhd->bhqk', q, k_all) * SCALE
        scores = jnp.where(valid[:, None, None, :], scores, -1e+30)
        probs = jax.nn.softmax(scores, axis=-1)
        o = jnp.einsum('bhqk,bkhd->bqhd', probs, v_all)
        o = o.reshape(bsz, seqlen, HQ * D)
        return jnp.einsum('bse,de->bsd', o, Wo)

    def _L1_ffn_ref(x, codebook, idx_gate, idx_up, idx_down):
        import jax, jax.numpy as jnp
        import numpy as np
        H = 512
        I = 1376
        CS = 8
        CB = 8192

        def _dequant(codebook, idx):
            return codebook[idx].reshape(idx.shape[0], -1)
        Wg = _dequant(codebook, idx_gate)
        Wu = _dequant(codebook, idx_up)
        Wd = _dequant(codebook, idx_down)
        g = jnp.einsum('bsh,ih->bsi', x, Wg)
        u = jnp.einsum('bsh,ih->bsi', x, Wu)
        h = jax.nn.silu(g) * u
        return jnp.einsum('bsi,hi->bsh', h, Wd)
    x = x + _L0_ffn_ref(_L0_cond_ref(x, L0_cond_weight, itok_B_3_7), L0_ffn_base_W, L0_ffn_router_W, L0_ffn_lora_A, L0_ffn_lora_B)
    x = x + _L1_ffn_ref(_L1_cond_ref(x, L1_cond_Wq, L1_cond_Wk, L1_cond_Wv, L1_cond_Wo, L1_cond_q_norm_w, L1_cond_k_norm_w, L1_cond_k_cache, L1_cond_v_cache, itok_Bx16_0_63, itok_B_207_1644), L1_ffn_codebook, L1_ffn_idx_gate, L1_ffn_idx_up, L1_ffn_idx_down)
    return x

_drawn_inputs = setup_inputs


def setup_inputs(seed=0):
    import zlib

    import numpy as np

    out = dict(_drawn_inputs(seed))
    spreads = {}
    factors = {'L0_ffn_router_W': 3.304, 'L0_ffn_lora_A': 2.857, 'L0_ffn_lora_B': 2.852}
    for name, (base, spread) in spreads.items():
        noise = np.random.default_rng([zlib.crc32(name.encode()), seed]).standard_normal(out[name].shape)
        drawn = base * np.exp(spread * noise) if base else spread * noise
        out[name] = jnp.asarray(drawn.astype(out[name].dtype))
    for name, factor in factors.items():
        out[name] = (out[name] * factor).astype(out[name].dtype)
    return out
```

```python
from contextlib import ExitStack

import concourse.bass as bass
from concourse import mybir

F32 = mybir.dt.float32
I32 = mybir.dt.int32
ALU = mybir.AluOpType
ACT = mybir.ActivationFunctionType
AX = mybir.AxisListType
PE_, DVE_, SP_ = mybir.EngineType.PE, mybir.EngineType.DVE, mybir.EngineType.SP

P = 128
S = 32
TB = P // S
D = 512
KC = D // P
NE, RANK = 8, 16
NHALF = 2
PG = 16
PSZ = 32
L = PG * PSZ
HD = 128
REP = 4
HK2 = 4
HQ2 = REP * HK2
NP = TB * HK2
BIG = 1e30
SCALE = HD ** -0.5
EPS = 1e-6
MAGIC = 12582912.0
TWO_PI = 6.283185307179586
PI1 = 6.28125
PI2 = 0.0019350051879882812
PI3 = TWO_PI - PI1 - PI2
RSQRT_BITS = 1597463007.0
ROPE_UNITS = 5
ROPE_OPS = 4 * ROPE_UNITS + 13 + 2
CHUNK = 43
RED_OPS = 1 + TB + 1 + 1 + 2 + 3 + 1
TAB_OPS = RED_OPS + 3 + 8
RT_OPS = 13
FILL = {0: 0, 2: 1, 4: 2, 6: 3, 8: 4}


def adaln_ffn_kernel(nc, x, ids, table, seqlens, w_cond, base_w, router_w, lora_a, lora_b,
                     wq, wk, wv, wo, qnw, knw, k_cache, v_cache, codebook, idx_all,
                     con_a, con_b, out):
    NB = x.shape[0]
    NT = NB * S // P
    NPAGES = k_cache.shape[0]
    NID = w_cond.shape[0]
    NG = idx_all.shape[1]
    CW = codebook.shape[1]
    I = NG * P * CW // (3 * D)
    NI = -(-I // P)
    ILAST = I - (NI - 1) * P
    ROUNDS = NG // CHUNK // 2
    assert NB * S == NT * P and NG % (2 * CHUNK) == 0
    GT = 4
    NGRP = NT // GT

    x_t = x.rearrange("(t b) s d -> t (b s) d", b=TB)
    out_t = out.rearrange("(t b) s d -> t (b s) d", b=TB)
    x1_d = nc.dram_tensor("x1_d", (NT, P, D), F32).ap()
    x1t_d = nc.dram_tensor("x1t_d", (NT + 1, P, D), F32).ap()
    tab_d = nc.dram_tensor("tab_d", (NT + 1, P, 4 * HD), F32).ap()
    a_d = nc.dram_tensor("a_d", (NT, P, D), F32).ap()
    w_d = nc.dram_tensor("w_d", (P, NG * CW), F32).ap()

    with ExitStack() as ctx:
        def sem(name):
            return ctx.enter_context(nc.semaphore(name))

        bank = [ctx.enter_context(nc.psum_tensor(f"bank{i}", [P, 512], F32)) for i in range(8)]

        base = (nc.sbuf_base + 63) // 64 * 64
        at = [base]

        def sb(name, shape, dt=F32):
            t = nc.alloc_sbuf_tensor_at(name, shape, dt, offset=at[0])
            n = 4
            for s in shape[1:]:
                n *= s
            at[0] += (n + 31) // 32 * 32
            return t

        ident = sb("ident", [P, P])
        keyidx = sb("keyidx", [P, L])
        pages = sb("pages", [1, NB * PG], I32)
        seqf = sb("seqf", [P, NB])
        gidx = [sb(f"gidx{u}", [P, CHUNK], I32) for u in range(2)]
        stage = [sb(f"stage{u}", [P, CHUNK, CW]) for u in range(2)]
        nat = [sb(f"nat{j}", [P, 512]) for j in range(4)]
        nat_at = at[0] - 4 * 2048
        phase_at = at[0]

        wt_all = sb("wt_all", [P, NID, KC, D])
        w_base = sb("w_base", [P, KC, D + NE + NE * RANK])
        lorab = sb("lorab", [P, D])
        routn = sb("routn", [NE, D])
        idb = sb("idb", [1, NB], I32)
        con2 = sb("con2", [P, con_b.shape[1]])
        seqi = sb("seqi", [P, NB], I32)
        qkw = sb("qkw", [P, 2, HD])
        pos = sb("pos", [P, NT])
        ang = sb("ang", [P, NT, HD // 2])
        red = sb("red", [P, NT, HD // 2])
        sin_ = sb("sin_", [P, NT, HD // 2])
        cos_ = sb("cos_", [P, NT, HD // 2])
        tabs = sb("tabs", [P, NT, 4, HD])
        zero = sb("zero", [P, D])
        xn = sb("xn", [P, D])
        xtz = sb("xtz", [P, KC, 5 * P])
        cn = sb("cn", [P, D])
        ct = sb("ct", [P, D])
        mm = sb("mm", [P, NE, RANK])
        mt = sb("mt", [P, P])
        xres = sb("xres", [P, D])
        x1n = sb("x1n", [P, D])
        x1t = sb("x1t", [P, D])
        nmx = sb("nmx", [P, 1])
        rex = sb("rex", [P, NE])
        rsm = sb("rsm", [P, 4])
        prb = sb("prb", [P, NE])
        cmp_ = sb("cmp_", [P, NE, NE])
        eq = sb("eq", [P, NE, NE])
        rank = sb("rank", [P, NE])
        sel = sb("sel", [P, NE])
        wgt = sb("wgt", [P, NE])
        end0 = at[0]

        at[0] = nat_at
        ots = sb("ots", [P, HQ2, P])
        assert at[0] == phase_at
        wqt = sb("wqt", [P, KC, HQ2 * HD])
        wkvt = sb("wkvt", [P, KC, 2 * HK2 * HD])
        wot = sb("wot", [P, HQ2, D])
        ktall = sb("ktall", [P, NPAGES, HK2, PSZ])
        vg = [sb(f"vg{i}", [P, KC, HK2 * HD]) for i in range(2)]
        kg = [sb(f"kg{i}", [P, HK2, PG, PSZ]) for i in range(2)]
        sm = [sb(f"sm{i}", [P, L]) for i in range(2)]
        pts = [sb(f"pts{i}", [P, KC, P]) for i in range(2)]
        pz = sb("pz", [P, TB, HK2, P])
        pnt = sb("pnt", [P, HK2, P])
        sn = sb("sn", [P, NP, S])
        qt = sb("qt", [P, TB, HK2, REP, S])
        ktn = sb("ktn", [P, HK2, P])
        vn = sb("vn", [P, HK2 * HD])
        qkf = sb("qkf", [P, ROPE_UNITS, REP, HD])
        qn = sb("qn", [P, REP, HD])
        qb = sb("qb", [P, REP, HD])
        xt = sb("xt", [P, KC, P])
        tab = sb("tab", [P, 4, HD])
        on = sb("on", [P, HK2, HD])
        an = sb("an", [P, D])
        mask = sb("mask", [P, L])
        ssq = sb("ssq", [P, 20])
        xs = sb("xs", [P, 20])
        xh = sb("xh", [P, 20])
        yy = sb("yy", [P, 20])
        y2 = sb("y2", [P, 20])
        y3 = sb("y3", [P, 20])
        yi = sb("yi", [P, 20], I32)
        mp = sb("mp", [P, NP])
        mnew = sb("mnew", [P, NP])
        sumc = sb("sumc", [P, NP])
        sumn = sb("sumn", [P, NP])
        rsum = sb("rsum", [P, NP])
        rinv = sb("rinv", [P, NP])
        end1 = at[0]

        at[0] = phase_at
        wgt_t = [sb(f"w{n}t", [P, KC, I]) for n in "gu"]
        wdt = sb("wdt", [P, NI, D])
        an4 = sb("an4", [P, GT, D])
        at4 = sb("at4", [P, KC, GT * P])
        ht = sb("ht", [P, NI, GT * P])
        sg = [sb(f"sg{i}", [P, GT * P]) for i in range(2)]
        x1b = [sb(f"x1b{i}", [P, D]) for i in range(2)]
        ob = [sb(f"ob{i}", [P, D]) for i in range(2)]
        assert max(end0, end1, at[0]) <= 229344, (end0, end1, at[0])

        c_ld = sem("c_ld")
        c2_ld = sem("c2_ld")
        nat_full = [sem(f"nat_full{j}") for j in range(4)]
        prep_tr = [sem(f"prep_tr{j}") for j in range(4)]
        prep_ev = [sem(f"prep_ev{j}") for j in range(4)]
        phase = sem("phase")
        gate = {e: sem(f"gate_{e}") for e in ("pool", "act", "dve", "sp", "pe")}
        rtab = sem("rtab")
        trig = sem("trig")
        tab_st = sem("tab_st")
        zeroed = sem("zeroed")
        x_ld = sem("x_ld")
        xres_ld = sem("xres_ld")
        pe_xt, xtz_ev = sem("pe_xt"), sem("xtz_ev")
        pe_cond, c_ev = sem("pe_cond"), sem("c_ev")
        pe_ct, ct_ev = sem("pe_ct"), sem("ct_ev")
        pe_mid, rt = sem("pe_mid"), sem("rt")
        rexp = sem("rexp")
        pe_mt, mt_ev = sem("pe_mt"), sem("mt_ev")
        pe_y0, x1_rdy = sem("pe_y0"), sem("x1_rdy")
        pe_x1t, x1t_ev = sem("pe_x1t"), sem("x1t_ev")
        x1_st, x1t_st = sem("x1_st"), sem("x1t_st")
        pe_r, r_ev = sem("pe_r"), sem("r_ev")
        pz_zero = sem("pz_zero")
        xt_ld, tab_ld = sem("xt_ld"), sem("tab_ld")
        v_ld = [sem(f"v_ld{i}") for i in range(2)]
        a_ld, a_st = sem("a_ld"), sem("a_st")
        unit_mm, unit_cp, unit_ev = sem("unit_mm"), sem("unit_cp"), sem("unit_ev")
        rope = sem("rope")
        pe_v, v_ev = sem("pe_v"), sem("v_ev")
        pe_qt, qt_a, qt_d = sem("pe_qt"), sem("qt_a"), sem("qt_d")
        pe_kt, kt_ev = sem("pe_kt"), sem("kt_ev")
        pe_sn, sn_ev, mn = sem("pe_sn"), sem("sn_ev"), sem("mn")
        kg_rdy, mk = sem("kg_rdy"), sem("mk")
        s_mm, ttr = sem("s_mm"), sem("ttr")
        ex, exn = sem("ex"), sem("exn")
        pe_t, pt_d, pt_a = sem("pe_t"), sem("pt_d"), sem("pt_a")
        pe_tn, tn_ev = sem("pe_tn"), sem("tn_ev")
        pe_o, osum, on_rdy = sem("pe_o"), sem("osum"), sem("on_rdy")
        pe_ot, ot_ev = sem("pe_ot"), sem("ot_ev")
        pe_op, op_ev = sem("pe_op"), sem("op_ev")
        gi_ld = [sem(f"gi_ld{u}") for u in range(2)]
        gat = [sem(f"gat{u}") for u in range(2)]
        g_st = [sem(f"g_st{u}") for u in range(2)]
        an_ld, pe_at, at_ev = sem("an_ld"), sem("pe_at"), sem("at_ev")
        pe_gu, silu, hm = sem("pe_gu"), sem("silu"), sem("hm")
        pe_dn, out_add = sem("pe_dn"), sem("out_add")
        x1b_ld = [sem(f"x1b_ld{i}") for i in range(2)]
        o_st = [sem(f"o_st{i}") for i in range(2)]

        R_BASE = NID
        R_HALF = NID + 1
        HALF_ROUNDS = 4 + 1 + 1 + 4 + NPAGES // 16
        R_FFN = R_HALF + NHALF * HALF_ROUNDS

        def regs(engine, ap):
            return nc.values_load_multi_w_load_instructions(
                ap, engines=[engine], min_val=0, max_val=63,
                skip_runtime_bounds_check_because="they index a table of 64 pages or fewer")[1]

        def cols(j):
            return bank[j][:].rearrange("p (k c) -> p k c", k=4)

        def cond_dst(i, j):
            return wt_all[:, bass.ds(i, 1), :, j * P:(j + 1) * P].rearrange("p a k c -> p (a k) c"), cols(j)

        def base_dst(j):
            return w_base[:, :, j * P:(j + 1) * P], cols(j)

        def wq_dst(i, j):
            return wqt[:, :, bass.ds(i * 512 + j * P, P)], cols(j)

        def kv_dst(v, j):
            return wkvt[:, :, v * 512 + j * P:v * 512 + (j + 1) * P], cols(j)

        def wo_dst(i, j):
            return wot[:, bass.ds(i * 4 + j, 1), :].rearrange("p a d -> p (a d)"), bank[j][:]

        def kt_dst(i, j):
            return (ktall[:, bass.ds(i * 16 + j * 4, 4)].rearrange("p g h s -> p h g s"),
                    bank[j][:].rearrange("p (h g s) -> p h g s", h=HK2, g=4))

        def ffn_dst(u):
            m, c = divmod(u, NI)
            n = P if c < NI - 1 else ILAST
            if m < 2:
                return wgt_t[m][:, :, c * P:c * P + n], cols(u % 4)[:, :, 0:n]
            return wdt[0:n, c, :], bank[u % 4][0:n, :]

        def xtz_diag(b):
            return xtz[:, :, b * (P + S):b * (P + S) + S]

        block = ctx.enter_context(nc.Block())

        @block.sync
        def _(sp):
            def nat_round(rnd, srcs, whole=False):
                for j, (dst, src) in enumerate(srcs):
                    if not (isinstance(rnd, int) and rnd == 0):
                        sp.wait_ge(prep_tr[3 if whole else j], rnd)
                    sp.dma_start(dst, src).then_inc(nat_full[j], 16)

            sp.dma_start(ident[:], con_a[:, 0:P]).then_inc(c_ld, 16)
            nat_round(0, [(nat[j][:], w_cond[0, j * P:(j + 1) * P, :]) for j in range(4)])
            sp.dma_start(keyidx[:], con_a[:, P:]).then_inc(c_ld, 16)
            sp.dma_start(con2[:], con_b).then_inc(c2_ld, 16)
            sp.dma_start(seqi[:], seqlens.partition_broadcast(P)).then_inc(c2_ld, 16)
            sp.dma_start(qkw[:, 0, :], qnw.partition_broadcast(P)).then_inc(c2_ld, 16)
            sp.dma_start(qkw[:, 1, :], knw.partition_broadcast(P)).then_inc(c2_ld, 16)
            sp.dma_start(pages[:], table.rearrange("(a b) c -> a (b c)", a=1)).then_inc(c_ld, 16)
            sp.dma_start(idb[:], ids.rearrange("(a b) -> a b", a=1)).then_inc(c_ld, 16)
            sp.dma_start(routn[:], router_w).then_inc(c_ld, 16)
            sp.dma_start(lorab[:], lora_b.rearrange("e r d -> (e r) d")).then_inc(c_ld, 16)
            for kc in range(KC):
                sp.dma_start(w_base[:, kc, D + NE:].rearrange("p (e r) -> p e r", e=NE),
                             lora_a[:, kc * P:(kc + 1) * P, :].rearrange("e p r -> p e r")).then_inc(c_ld, 16)
            sp.dma_start(xn[:], x_t[0]).then_inc(x_ld, 16)
            with sp.Fori(1, NID) as i:
                nat_round(i, [(nat[j][:], w_cond[bass.ds(i, 1), j * P:(j + 1) * P, :]
                               .rearrange("a p d -> (a p) d")) for j in range(4)])
            nat_round(R_BASE, [(nat[j][:], base_w[j * P:(j + 1) * P, :]) for j in range(4)])
            sp.wait_ge(zeroed, 1)
            sp.dma_start(a_d.rearrange("t p d -> p t d"),
                         zero[:].unsqueeze(1).to_broadcast([P, NT, D])).then_inc(a_st, 16)
            sp.wait_ge(rtab, TAB_OPS)
            sp.dma_start(tab_d[0:NT].rearrange("t p c -> p t c"),
                         tabs[:].rearrange("p t a c -> p t (a c)")).then_inc(tab_st, 16)
            sp.dma_start(tab_d[NT], tabs[:, NT - 1].rearrange("p a c -> p (a c)")).then_inc(tab_st, 16)

            def l0(t, load, res, pad=False):
                if load:
                    sp.wait_ge(pe_xt, t + 1)
                    sp.dma_start(xn[:], x_t[bass.ds(t + 1, 1)].rearrange("a p d -> (a p) d")).then_inc(x_ld, 16)
                if res:
                    if not isinstance(t, int) or t > 1:
                        sp.wait_ge(x1_rdy, t - 1)
                    sp.dma_start(xres[:], x_t[bass.ds(t - 1, 1)].rearrange("a p d -> (a p) d")).then_inc(xres_ld, 16)
                    sp.wait_ge(x1_rdy, t)
                    sp.dma_start(x1_d[bass.ds(t - 1, 1)].rearrange("a p d -> (a p) d"), x1n[:]).then_inc(x1_st, 16)
                    sp.wait_ge(x1t_ev, t)
                    sp.dma_start(x1t_d[bass.ds(t - 1, 1)].rearrange("a p d -> (a p) d"), x1t[:]).then_inc(x1t_st, 16)
                    if pad:
                        sp.dma_start(x1t_d[NT], x1t[:]).then_inc(x1t_st, 16)

            l0(0, True, False)
            l0(1, True, True)
            with sp.Fori(2, NT - 1) as t:
                l0(t, True, True)
            l0(NT - 1, False, True)
            l0(NT, False, True, pad=True)
            sp.wait_ge(x1_st, 16 * NT)
            sp.wait_ge(x1t_st, 16 * (NT + 1))
            sp.wait_ge(tab_st, 32)

            with sp.Fori(0, NHALF) as h:
                sp.drain().then_inc(phase, 1)
                sp.wait_ge(phase, 4 * h + 4)
                sp.sem_inc(gate["sp"], 1)
                r0 = h * HALF_ROUNDS + R_HALF
                with sp.Fori(0, 4) as i:
                    nat_round(r0 + i, [(nat[j][:], wq[bass.ds(h * (HQ2 * HD) + i * 512 + j * P, P), :]) for j in range(4)])
                nat_round(r0 + 4, [(nat[j][:], wk[bass.ds(h * (HK2 * HD) + j * P, P), :]) for j in range(4)])
                nat_round(r0 + 5, [(nat[j][:], wv[bass.ds(h * (HK2 * HD) + j * P, P), :]) for j in range(4)])
                with sp.Fori(0, 4) as i:
                    nat_round(r0 + 6 + i, [(nat[j][:], wo[j * P:(j + 1) * P, bass.ds(h * (HQ2 * HD) + i * 512, 512)])
                                           for j in range(4)], whole=True)
                with sp.Fori(0, NPAGES // 16) as i:
                    nat_round(r0 + 10 + i, [(nat[j][:].rearrange("p (h d) -> p h d", h=HK2),
                                             k_cache[bass.ds(i * 16 + j * 4, 4), :, bass.ds(h * HK2, HK2), :]
                                             .rearrange("a s h d -> (a s) h d")) for j in range(4)], whole=True)

                def v_load(n, par):
                    pg = regs(SP_, pages[0:1, bass.ds(n * PG, PG)])
                    for j in range(PG):
                        q = j % 4
                        sp.dma_start(vg[par][PSZ * q:PSZ * (q + 1), j // 4, :],
                                     v_cache[bass.ds(pg[j], 1), :, bass.ds(h * HK2, HK2), :]
                                     .rearrange("a s h d -> (a s) (h d)")).then_inc(v_ld[par], 16)

                def xt_load(t):
                    sp.dma_start(xt[:].rearrange("p k c -> p (k c)"),
                                 x1t_d[bass.ds(t, 1)].rearrange("a p d -> (a p) d")).then_inc(xt_ld, 16)

                def tab_load(t):
                    sp.dma_start(tab[:].rearrange("p k c -> p (k c)"),
                                 tab_d[bass.ds(t, 1)].rearrange("a p d -> (a p) d")).then_inc(tab_ld, 16)

                xt_load(0)
                tab_load(0)
                v_load(0, 0)
                v_load(1, 1)
                j = h * NT
                sp.wait_ge(rope, j * ROPE_OPS + 4 * ROPE_UNITS)
                tab_load(1)
                sp.wait_ge(pe_v, j + 1)
                xt_load(1)

                def tile(t, last):
                    g = h * NT + t
                    j = g + 1
                    sp.wait_ge(a_st, g * 16 + 16)
                    sp.dma_start(an[:], a_d[bass.ds(t, 1)].rearrange("a p d -> (a p) d")).then_inc(a_ld, 16)
                    for b in range(TB):
                        if not (last and b >= 2):
                            sp.wait_ge(pe_o, g * TB + b + 1)
                            sp.sem_inc(gate["sp"], 1)
                            v_load(t * TB + b + 2, b % 2)
                        if b == 2 and not last:
                            sp.wait_ge(rope, j * ROPE_OPS + 4 * ROPE_UNITS)
                            tab_load(t + 2)
                    if not last:
                        sp.wait_ge(pe_v, j + 1)
                        xt_load(t + 2)
                    sp.wait_ge(op_ev, g + 1)
                    sp.dma_start(a_d[bass.ds(t, 1)].rearrange("a p d -> (a p) d"), an[:]).then_inc(a_st, 16)

                with sp.Fori(0, NT - 1) as t:
                    tile(t, False)
                tile(NT - 1, True)

            sp.drain().then_inc(phase, 1)
            sp.wait_ge(phase, 4 * NHALF + 4)
            sp.wait_ge(a_st, 16 * (NHALF * NT + 1))
            for u in range(2):
                sp.wait_ge(g_st[u], 16 * ROUNDS)
            flat = w_d.rearrange("p c -> (p c)")
            wrow = [flat[m * I * D:(m + 1) * I * D].rearrange("(i j) -> i j", j=D) for m in range(2)]
            wdrow = flat[2 * I * D:].rearrange("(i j) -> i j", j=I)
            for u in range(3 * NI):
                m, c = divmod(u, NI)
                n = P if c < NI - 1 else ILAST
                r, j = R_FFN + u // 4, u % 4
                sp.wait_ge(prep_tr[j], r)
                if m < 2:
                    sp.dma_start(nat[j][0:n, :], wrow[m][c * P:c * P + n, :]).then_inc(nat_full[j], 16)
                else:
                    sp.dma_start(nat[j][:].rearrange("p (o c) -> p o c", o=4)[:, :, 0:n],
                                 wdrow[:, c * P:c * P + n].rearrange("(o p) c -> p o c", p=P)).then_inc(nat_full[j], 16)

            def an_load(n):
                sp.dma_start(an4[:], a_d[bass.ds(n * GT, GT)].rearrange("t p d -> p t d")).then_inc(an_ld, 16)

            an_load(0)

            def group(n, last):
                if not last:
                    sp.wait_ge(pe_at, (n + 1) * 4)
                    an_load(n + 1)
                for i in range(GT):
                    sp.wait_ge(out_add, n * GT + i + 1)
                    sp.dma_start(x1b[i % 2][:], x1_d[bass.ds(n * GT + i, 1)].rearrange("a p d -> (a p) d")).then_inc(x1b_ld[i % 2], 16)
                    if i >= 1:
                        sp.wait_ge(out_add, n * GT + i + 2)
                        sp.dma_start(out_t[bass.ds(n * GT + i - 1, 1)].rearrange("a p d -> (a p) d"), ob[(i - 1) % 2][:]).then_inc(o_st[(i - 1) % 2], 16)
                sp.wait_ge(out_add, n * GT + GT + 2)
                sp.dma_start(out_t[bass.ds(n * GT + GT - 1, 1)].rearrange("a p d -> (a p) d"), ob[(GT - 1) % 2][:]).then_inc(o_st[(GT - 1) % 2], 16)

            with sp.Fori(0, NGRP - 1) as n:
                group(n, False)
            group(NGRP - 1, True)
            for i in range(2):
                sp.wait_ge(o_st[i], 16 * (NT // 2))

        @block.gpsimd
        def _(pool):
            def load_numbers(r, u):
                pool.dma_start(gidx[u][:], idx_all[:, bass.ds((r * 2 + u) * CHUNK, CHUNK)]).then_inc(gi_ld[u], 16)

            def store(r, u, more):
                pool.wait_ge(gat[u], (r + 1) * (16 * CHUNK))
                pool.sem_inc(gate["pool"], 1)
                pool.dma_start(w_d[:, bass.ds((r * 2 + u) * (CHUNK * CW), CHUNK * CW)],
                               stage[u][:].rearrange("p n c -> p (n c)")).then_inc(g_st[u], 16)
                if more:
                    load_numbers(r + 1, u)

            def round_(r, first, last):
                for u in range(2):
                    pool.wait_ge(gi_ld[u], (r + 1) * 16)
                    pool.sem_inc(gate["pool"], 1)
                    if not first:
                        pool.wait_ge(g_st[u], r * 16)
                        pool.sem_inc(gate["pool"], 1)
                    for n in range(CHUNK):
                        if n == 8:
                            if u:
                                store(r, 0, not last)
                            elif not first:
                                store(r - 1, 1, True)
                        pool.indirect_dma_start(
                            out=stage[u][:, n, :], out_offset=None, in_=codebook,
                            in_offset=bass.IndirectOffsetOnAxis(ap=gidx[u][:, n:n + 1], axis=0)).then_inc(gat[u], 16)

            load_numbers(0, 0)
            load_numbers(0, 1)
            round_(0, True, False)
            with pool.Fori(1, ROUNDS - 1) as r:
                round_(r, False, False)
            round_(ROUNDS - 1, False, True)
            store(ROUNDS - 1, 1, False)

        @block.scalar
        def _(act):
            def copy(dst, src):
                return nc.scalar.activation(dst, src, ACT.Copy)

            def prep(rnd, dst):
                for j in (0, 2):
                    act.wait_ge(prep_tr[j], rnd + 1)
                    act.sem_inc(gate["act"], 1)
                    o, i = dst(j)
                    copy(o, i).then_inc(prep_ev[j], 1)

            prep(0, lambda j: cond_dst(0, j))
            act.wait_ge(rtab, RED_OPS)
            nc.scalar.activation(sin_[:].rearrange("p a b -> p (a b)"), red[:].rearrange("p a b -> p (a b)"), ACT.Sin).then_inc(trig, 1)
            nc.scalar.activation(cos_[:].rearrange("p a b -> p (a b)"), red[:].rearrange("p a b -> p (a b)"), ACT.Sin, scale=0.5).then_inc(trig, 1)
            with act.Fori(1, NID) as i:
                prep(i, lambda j: cond_dst(i, j))
            prep(R_BASE, base_dst)
            act.wait_ge(zeroed, 2)
            act.wait_ge(pe_xt, 1)
            for b in range(TB):
                ins = copy(xtz_diag(b), bank[0][:].rearrange("p (k c) -> p k c", k=KC)[:, :, b * S:(b + 1) * S])
            ins.then_inc(xtz_ev, 1)

            def l0(t, cond, nxt, prev):
                if prev:
                    act.wait_ge(rt, (t - 1) * RT_OPS + 1)
                    nc.scalar.activation(rex[:], bank[4][:, 0:NE], ACT.Exp, bias=nmx[:], accum_out=rsm[:, 0:1]).then_inc(rexp, 1)
                if cond:
                    act.wait_ge(pe_cond, t + 1)
                    copy(cn[:], bank[1][:]).then_inc(c_ev, 1)
                if nxt:
                    act.wait_ge(pe_xt, t + 2)
                    for b in range(TB):
                        ins = copy(xtz_diag(b), bank[0][:].rearrange("p (k c) -> p k c", k=KC)[:, :, b * S:(b + 1) * S])
                    ins.then_inc(xtz_ev, 1)
                if prev:
                    act.wait_ge(pe_mt, t)
                    copy(mt[:], bank[5][:, 0:P]).then_inc(mt_ev, 1)
                if cond:
                    act.wait_ge(pe_ct, t + 1)
                    copy(ct[:], bank[2][:]).then_inc(ct_ev, 1)
                if prev:
                    act.wait_ge(pe_x1t, t)
                    if not isinstance(t, int) or t > 1:
                        act.wait_ge(x1t_st, (t - 1) * 16)
                    copy(x1t[:], bank[6][:]).then_inc(x1t_ev, 1)

            l0(0, True, True, False)
            l0(1, True, True, True)
            with act.Fori(2, NT - 1) as t:
                l0(t, True, True, True)
            l0(NT - 1, True, False, True)
            l0(NT, False, False, True)

            with act.Fori(0, NHALF) as h:
                act.drain().then_inc(phase, 1)
                act.wait_ge(phase, 4 * h + 4)
                act.sem_inc(gate["act"], 1)
                r0 = h * HALF_ROUNDS + R_HALF
                with act.Fori(0, 4) as i:
                    prep(r0 + i, lambda j: wq_dst(i, j))
                prep(r0 + 4, lambda j: kv_dst(0, j))
                prep(r0 + 5, lambda j: kv_dst(1, j))
                with act.Fori(0, 4) as i:
                    prep(r0 + 6 + i, lambda j: wo_dst(i, j))
                with act.Fori(0, NPAGES // 16) as i:
                    prep(r0 + 10 + i, lambda j: kt_dst(i, j))

                def unit(j, u):
                    act.wait_ge(unit_mm, j * ROPE_UNITS + u + 1)
                    if u:
                        act.wait_ge(rope, j * ROPE_OPS + 4 * u - 1)
                    copy(qn[:].rearrange("p r d -> p (r d)"), bank[7][:]).then_inc(unit_cp, 1)
                    act.wait_ge(unit_cp, j * ROPE_UNITS + u + 1)
                    for i in range(REP):
                        ins = nc.scalar.activation(bank[7][:, i * HD:(i + 1) * HD], bank[7][:, i * HD:(i + 1) * HD], ACT.Square,
                                                   scale=HD ** -0.5, accum_out=ssq[:, 4 * u + i:4 * u + i + 1])
                    ins.then_inc(unit_ev, 1)

                def tail(j):
                    act.wait_ge(pe_v, j + 1)
                    copy(vn[:], bank[7][:]).then_inc(v_ev, 1)
                    for k in range(2):
                        act.wait_ge(pe_qt, j * 4 + k + 1)
                        copy(qt[:, :, k], bank[k][:].rearrange("p (r b s) -> p b r s", r=REP, b=TB)).then_inc(qt_a, 1)
                    act.wait_ge(pe_kt, j + 1)
                    copy(ktn[:].rearrange("p h c -> p (h c)"), bank[7][:]).then_inc(kt_ev, 1)

                def tail_sn(j):
                    act.wait_ge(pe_sn, j + 1)
                    copy(sn[:].rearrange("p n s -> p (n s)"), bank[7][:]).then_inc(sn_ev, 1)

                def softmax(g, p):
                    b, hh = divmod(p, HK2)
                    act.wait_ge(ttr, g * NP + p + 1)
                    nc.scalar.activation(sm[p % 2][:], sm[p % 2][:], ACT.Exp, bias=mp[:, p:p + 1], scale=-1.0,
                                         accum_out=sumc[:, p:p + 1]).then_inc(ex, 1)
                    nc.scalar.activation(pz[:, b, hh, b * S:(b + 1) * S], sn[:, p, :], ACT.Exp, bias=mp[:, p:p + 1], scale=-1.0,
                                         accum_out=sumn[:, p:p + 1]).then_inc(exn, 1)

                def ot_out(g, b):
                    act.wait_ge(pe_ot, g * TB + b + 1)
                    copy(ots[:, :, b * S:(b + 1) * S], bank[6][:].rearrange("p (h s) -> p h s", s=S)).then_inc(ot_ev, 1)

                j0 = h * NT
                for u in range(ROPE_UNITS):
                    unit(j0, u)
                tail(j0)
                tail_sn(j0)
                act.wait_ge(pz_zero, h + 1)
                act.sem_inc(gate["act"], 1)

                def tile(t, last):
                    g = h * NT + t
                    j = g + 1
                    act.wait_ge(sn_ev, g + 1)
                    softmax(g, 0)
                    for p in range(NP):
                        if p + 1 < NP:
                            softmax(g, p + 1)
                        if p in FILL and not last:
                            unit(j, FILL[p])
                        if p % 4 == 2 and p >= 6:
                            ot_out(g, (p - 6) // 4)
                        if p % 2:
                            act.wait_ge(pe_t, g * NP + p + 1)
                            copy(pts[1][:].rearrange("p k c -> p (k c)"), bank[3][:]).then_inc(pt_a, 1)
                        if p % 4 == 3:
                            act.wait_ge(pe_tn, g * TB + p // 4 + 1)
                            copy(pnt[:].rearrange("p h c -> p (h c)"), bank[6][:]).then_inc(tn_ev, 1)
                    if not last:
                        tail(j)
                    ot_out(g, 3)
                    if not last:
                        tail_sn(j)

                with act.Fori(0, NT - 1) as t:
                    tile(t, False)
                tile(NT - 1, True)

            act.drain().then_inc(phase, 1)
            act.wait_ge(phase, 4 * NHALF + 4)
            for u in range(3 * NI):
                if u % 2 == 0:
                    act.wait_ge(prep_tr[u % 4], R_FFN + u // 4 + 1)
                    o, i = ffn_dst(u)
                    copy(o, i).then_inc(prep_ev[u % 4], 1)

            def at_out(n):
                for k in range(KC):
                    act.wait_ge(pe_at, n * KC + k + 1)
                    copy(at4[:, k, :], bank[6 + k % 2][:]).then_inc(at_ev, 1)

            at_out(0)

            def group(n, last):
                for c in range(NI):
                    m = P if c < NI - 1 else ILAST
                    act.wait_ge(pe_gu, n * NI + c + 1)
                    if c >= 2:
                        act.wait_ge(hm, n * NI + c - 1)
                    nc.scalar.activation(sg[c % 2][0:m, :], bank[c % 2][0:m, :], ACT.Silu).then_inc(silu, 1)
                if not last:
                    at_out(n + 1)

            with act.Fori(0, NGRP - 1) as n:
                group(n, False)
            group(NGRP - 1, True)

        @block.tensor
        def _(pe):
            def prep(rnd, cols=4):
                for j in range(4):
                    pe.wait_ge(nat_full[j], (rnd + 1) * 16)
                    if not (isinstance(rnd, int) and rnd == 0):
                        pe.wait_ge(prep_ev[j], rnd)
                    for k in range(4):
                        ins = nc.tensor.transpose(bank[j][:, k * P:(k + 1) * P], nat[j][:, k * P:(k + 1) * P], ident[:])
                    ins.then_inc(prep_tr[j], 1)

            def prep_wo(rnd):
                for j in range(4):
                    pe.wait_ge(nat_full[j], (rnd + 1) * 16)
                    pe.wait_ge(prep_ev[j], rnd)
                for j in range(4):
                    for k in range(4):
                        ins = nc.tensor.transpose(bank[j][:, k * P:(k + 1) * P], nat[k][:, j * P:(j + 1) * P], ident[:])
                    ins.then_inc(prep_tr[j], 1)

            def block_t(dst, src, done):
                for k in range(4):
                    ins = nc.tensor.transpose(dst[:, k * P:(k + 1) * P], src[:, k * P:(k + 1) * P], ident[:])
                ins.then_inc(done, 1)

            pe.wait_ge(c_ld, 16 * 10)
            prep(0)
            with pe.Fori(1, NID) as i:
                prep(i)
            prep(R_BASE)
            for k in range(KC):
                ins = nc.tensor.transpose(bank[7][:, k * NE:(k + 1) * NE], routn[:, k * P:(k + 1) * P], ident[0:NE, 0:NE])
            ins.then_inc(pe_r, 1)
            for j in range(4):
                pe.wait_ge(prep_ev[j], R_BASE + 1)
            pe.wait_ge(r_ev, 1)
            pe.wait_ge(x_ld, 16)
            block_t(bank[0], xn, pe_xt)

            def l0(t, cond, nxt, prev):
                if cond:
                    wid = nc.values_load_multi_w_load_instructions(
                        idb[0:1, bass.ds(t * TB, TB)], engines=[PE_], min_val=0, max_val=NID - 1,
                        skip_runtime_bounds_check_because="adapter numbers are below the adapters' count")[1]
                    pe.wait_ge(xtz_ev, t + 1)
                    for b in range(TB):
                        for k in range(KC):
                            ins = nc.tensor.matmul(bank[1][:], xtz[:, k, b * P:(b + 1) * P],
                                                   wt_all[:, bass.ds(wid[b], 1), k, :].rearrange("p a d -> p (a d)"),
                                                   start=(b == 0 and k == 0), stop=(b == TB - 1 and k == KC - 1))
                    ins.then_inc(pe_cond, 1)
                if nxt:
                    pe.wait_ge(x_ld, (t + 2) * 16)
                    block_t(bank[0], xn, pe_xt)
                if prev:
                    pe.wait_ge(rt, t * RT_OPS)
                    nc.tensor.transpose(bank[5][:, 0:P], mm[:].rearrange("p e r -> p (e r)"), ident[:]).then_inc(pe_mt, 1)
                    pe.wait_ge(mt_ev, t)
                    nc.tensor.matmul(bank[3][:], mt[:], lorab[:], start=False, stop=True).then_inc(pe_y0, 1)
                if cond:
                    pe.wait_ge(c_ev, t + 1)
                    block_t(bank[2], cn, pe_ct)
                if prev:
                    pe.wait_ge(x1_rdy, t)
                    if not isinstance(t, int) or t > 1:
                        pe.wait_ge(x1t_ev, t - 1)
                    block_t(bank[6], x1n, pe_x1t)
                if cond:
                    pe.wait_ge(ct_ev, t + 1)
                    for k in range(KC):
                        nc.tensor.matmul(bank[3][:], ct[:, k * P:(k + 1) * P], w_base[:, k, 0:D], start=(k == 0), stop=False)
                    for k in range(KC):
                        ins = nc.tensor.matmul(bank[4][:, 0:NE + P], ct[:, k * P:(k + 1) * P], w_base[:, k, D:],
                                               start=(k == 0), stop=(k == KC - 1))
                    ins.then_inc(pe_mid, 1)

            l0(0, True, True, False)
            l0(1, True, True, True)
            with pe.Fori(2, NT - 1) as t:
                l0(t, True, True, True)
            l0(NT - 1, True, False, True)
            l0(NT, False, False, True)

            with pe.Fori(0, NHALF) as h:
                pe.drain().then_inc(phase, 1)
                pe.wait_ge(phase, 4 * h + 4)
                pe.sem_inc(gate["pe"], 1)
                r0 = h * HALF_ROUNDS + R_HALF
                with pe.Fori(0, 4) as i:
                    prep(r0 + i)
                prep(r0 + 4)
                prep(r0 + 5)
                with pe.Fori(0, 4) as i:
                    prep_wo(r0 + 6 + i)
                with pe.Fori(0, NPAGES // 16) as i:
                    prep(r0 + 10 + i)
                for k in range(4):
                    pe.wait_ge(prep_ev[k], r0 + HALF_ROUNDS)

                def unit(t, j, u, first=False):
                    if u == 0:
                        pe.wait_ge(xt_ld, (h * (NT + 1) + t + 1) * 16)
                        if not first:
                            pe.wait_ge(sn_ev, j)
                    else:
                        pe.wait_ge(unit_ev, j * ROPE_UNITS + u)
                    for k in range(KC):
                        w = wkvt[:, k, 0:512] if u == 0 else wqt[:, k, (u - 1) * 512:u * 512]
                        ins = nc.tensor.matmul(bank[7][:], xt[:, k, :], w, start=(k == 0), stop=(k == KC - 1))
                    ins.then_inc(unit_mm, 1)

                def tail(j):
                    pe.wait_ge(unit_ev, j * ROPE_UNITS + ROPE_UNITS)
                    for k in range(KC):
                        ins = nc.tensor.matmul(bank[7][:], xt[:, k, :], wkvt[:, k, 512:1024], start=(k == 0), stop=(k == KC - 1))
                    ins.then_inc(pe_v, 1)
                    pe.wait_ge(rope, j * ROPE_OPS + ROPE_OPS)
                    for k in range(4):
                        block_t(bank[k], qkf[:, k + 1].rearrange("p r d -> p (r d)"), pe_qt)
                    pe.wait_ge(v_ev, j + 1)
                    block_t(bank[7], qkf[:, 0].rearrange("p r d -> p (r d)"), pe_kt)

                def tail_sn(j):
                    pe.wait_ge(kt_ev, j + 1)
                    pe.wait_ge(qt_a, j * 2 + 2)
                    pe.wait_ge(qt_d, j * 2 + 2)
                    for p in range(NP):
                        b, hh = divmod(p, HK2)
                        ins = nc.tensor.matmul(bank[7][:, p * S:(p + 1) * S], qt[:, b, hh].rearrange("p r s -> p (r s)"),
                                               ktn[:, hh, b * S:(b + 1) * S], start=True, stop=True)
                    ins.then_inc(pe_sn, 1)

                def scores(t, p):
                    b, hh = divmod(p, HK2)
                    if hh == 0:
                        pe.wait_ge(kg_rdy, (h * NB + t * TB + b + 1))
                    if p >= 2:
                        pe.wait_ge(ttr, (h * NT + t) * NP + p - 1)
                    nc.tensor.matmul(bank[p % 2][:], qt[:, b, hh].rearrange("p r s -> p (r s)"),
                                     kg[b % 2][:, hh].rearrange("p g s -> p (g s)"), start=True, stop=True).then_inc(s_mm, 1)

                def values(t, p):
                    g = h * NT + t
                    b, hh = divmod(p, HK2)
                    if p % 2:
                        pe.wait_ge(pt_a, g * (NP // 2) + p // 2 + 1)
                    else:
                        pe.wait_ge(pt_d, g * (NP // 2) + p // 2 + 1)
                    if hh == 0:
                        pe.wait_ge(v_ld[b % 2], (h * (NB // 2) + t * 2 + b // 2 + 1) * (16 * PG))
                        pe.wait_ge(on_rdy, g * TB + b + 1)
                    for c in range(KC):
                        nc.tensor.matmul(bank[4 + b % 2][:, hh * HD:(hh + 1) * HD], pts[p % 2][:, c, :],
                                         vg[b % 2][:, c, hh * HD:(hh + 1) * HD], start=(hh == 0 and c == 0), stop=False,
                                         skip_group_check=True)

                def values_new(t, b):
                    g = h * NT + t
                    pe.wait_ge(tn_ev, g * TB + b + 1)
                    if b == 0:
                        pe.wait_ge(v_ev, g + 1)
                    for hh in range(HK2):
                        ins = nc.tensor.matmul(bank[4 + b % 2][:, hh * HD:(hh + 1) * HD], pnt[:, hh, :],
                                               vn[:, hh * HD:(hh + 1) * HD], start=False, stop=(hh == HK2 - 1),
                                               skip_group_check=True)
                    ins.then_inc(pe_o, 1)

                def out_t_(t, b):
                    pe.wait_ge(on_rdy, (h * NT + t) * TB + b + 3)
                    block_t(bank[6], on[:].rearrange("p h d -> p (h d)"), pe_ot)

                for u in range(ROPE_UNITS):
                    unit(0, h * NT, u, first=True)
                tail(h * NT)
                tail_sn(h * NT)

                def tile(t, last):
                    g = h * NT + t
                    scores(t, 0)
                    for p in range(NP):
                        if p + 1 < NP:
                            scores(t, p + 1)
                        if p >= 1:
                            values(t, p - 1)
                        if p >= 4 and p % 4 == 0:
                            values_new(t, p // 4 - 1)
                        if p in FILL and not last:
                            unit(t + 1, g + 1, FILL[p])
                        if p % 4 == 2 and p >= 6:
                            out_t_(t, (p - 6) // 4)
                        pe.wait_ge(ex, g * NP + p + 1)
                        block_t(bank[2 + p % 2], sm[p % 2], pe_t)
                        if p % 4 == 3:
                            b = p // 4
                            pe.wait_ge(exn, g * NP + p + 1)
                            if b >= 1:
                                pe.wait_ge(ot_ev, g * TB + b)
                            block_t(bank[6], pz[:, b].rearrange("p h c -> p (h c)"), pe_tn)
                    values(t, NP - 1)
                    values_new(t, TB - 1)
                    if not last:
                        tail(g + 1)
                    out_t_(t, TB - 1)
                    if not last:
                        tail_sn(g + 1)
                    pe.wait_ge(ot_ev, g * TB + TB)
                    for k in range(HQ2):
                        ins = nc.tensor.matmul(bank[6][:], ots[:, k, :], wot[:, k, :], start=(k == 0), stop=(k == HQ2 - 1))
                    ins.then_inc(pe_op, 1)

                with pe.Fori(0, NT - 1) as t:
                    tile(t, False)
                tile(NT - 1, True)

            pe.drain().then_inc(phase, 1)
            pe.wait_ge(phase, 4 * NHALF + 4)
            for u in range(3 * NI):
                m, c = divmod(u, NI)
                n = P if c < NI - 1 else ILAST
                r, j = R_FFN + u // 4, u % 4
                pe.wait_ge(nat_full[j], (r + 1) * 16)
                pe.wait_ge(prep_ev[j], r)
                for k in range(4):
                    if m < 2:
                        ins = nc.tensor.transpose(bank[j][:, k * P:k * P + n], nat[j][0:n, k * P:(k + 1) * P], ident[0:n, 0:n])
                    else:
                        ins = nc.tensor.transpose(bank[j][0:n, k * P:(k + 1) * P], nat[j][:, k * P:k * P + n], ident[:])
                ins.then_inc(prep_tr[j], 1)

            def at_in(n):
                pe.wait_ge(an_ld, (n + 1) * 16)
                for k in range(KC):
                    if k >= 2:
                        pe.wait_ge(at_ev, n * KC + k - 1)
                    for i in range(GT):
                        ins = nc.tensor.transpose(bank[6 + k % 2][:, i * P:(i + 1) * P], an4[:, i, k * P:(k + 1) * P], ident[:])
                    ins.then_inc(pe_at, 1)

            at_in(0)
            for j in range(4):
                pe.wait_ge(prep_ev[j], R_FFN + (3 * NI - j + 3) // 4)

            def group(n, last):
                pe.wait_ge(at_ev, n * KC + KC)
                for c in range(NI):
                    m = P if c < NI - 1 else ILAST
                    if c >= 2:
                        pe.wait_ge(hm, n * NI + c - 1)
                    for w in range(2):
                        for k in range(KC):
                            ins = nc.tensor.matmul(bank[2 * w + c % 2][0:m, :], wgt_t[w][:, k, c * P:c * P + m], at4[:, k, :],
                                                   start=(k == 0), stop=(k == KC - 1))
                    ins.then_inc(pe_gu, 1)
                if not last:
                    at_in(n + 1)
                pe.wait_ge(hm, n * NI + NI)
                for i in range(GT):
                    pe.wait_ge(out_add, n * GT + i + 1)
                    for c in range(NI):
                        m = P if c < NI - 1 else ILAST
                        ins = nc.tensor.matmul(bank[4 + i % 2][:], ht[0:m, c, i * P:(i + 1) * P], wdt[0:m, c, :],
                                               start=(c == 0), stop=(c == NI - 1))
                    ins.then_inc(pe_dn, 1)

            with pe.Fori(0, NGRP - 1) as n:
                group(n, False)
            group(NGRP - 1, True)

        @block.vector
        def _(dve):
            V = nc.vector

            def prep(rnd, dst):
                for j in (1, 3):
                    dve.wait_ge(prep_tr[j], rnd + 1)
                    dve.sem_inc(gate["dve"], 1)
                    o, i = dst(j)
                    V.tensor_copy(o, i).then_inc(prep_ev[j], 1)

            class Steps:

                def __init__(self, sem_, start):
                    self.sem, self.start, self.n = sem_, start, 0

                def done(self, ins):
                    ins.then_inc(self.sem, 1)
                    self.n += 1

                def wait(self):
                    dve.wait_ge(self.sem, self.start + self.n)

            dve.sem_inc(on_rdy, 2)
            dve.sem_inc(out_add, 2)
            V.memset(zero[:], 0.0).then_inc(zeroed, 1)
            V.memset(xtz[:], 0.0).then_inc(zeroed, 1)

            dve.wait_ge(c2_ld, 64)
            st = Steps(rtab, 0)
            invf, ptok = con2[:, 0:HD // 2], con2[:, HD // 2:HD // 2 + 1]
            tri = con2[:, HD // 2 + 1:HD // 2 + 1 + NE * NE].rearrange("p (a b) -> p a b", a=NE)
            st.done(V.tensor_copy(seqf[:], seqi[:]))
            st.wait()
            for b in range(TB):
                rows = slice(b * S, (b + 1) * S)
                st.done(V.tensor_copy(pos[rows, :], seqf[rows, :].rearrange("p (t b) -> p b t", b=TB)[:, b, :]))
            st.wait()
            st.done(V.tensor_scalar(pos[:], pos[:], ptok, None, ALU.add))
            st.wait()
            st.done(V.tensor_tensor(ang[:], pos[:].unsqueeze(2).to_broadcast([P, NT, HD // 2]),
                                    invf.unsqueeze(1).to_broadcast([P, NT, HD // 2]), ALU.mult))
            st.wait()
            st.done(V.tensor_scalar(cos_[:], ang[:], 1.0 / TWO_PI, MAGIC, ALU.mult, ALU.add))
            st.wait()
            st.done(V.tensor_scalar(sin_[:], cos_[:], -MAGIC, None, ALU.add))
            src = ang
            for part in (PI1, PI2, PI3):
                st.wait()
                st.done(V.scalar_tensor_tensor(out=red[:], in0=sin_[:], scalar=-part, in1=src[:], op0=ALU.mult, op1=ALU.add))
                src = red
            st.wait()
            st.done(V.tensor_scalar(red[:], red[:], 3.1415925, -3.1415925, ALU.min, ALU.max))
            assert st.n == RED_OPS
            prep(0, lambda j: cond_dst(0, j))
            half = HD // 2
            dve.wait_ge(trig, 2)
            st.done(V.tensor_tensor(ang[:], cos_[:], cos_[:], ALU.mult))
            st.wait()
            st.done(V.tensor_scalar(ang[:], ang[:], -2.0, 1.0, ALU.mult, ALU.add))
            st.done(V.tensor_scalar(qkw[:, 0, :], qkw[:, 0, :], -SCALE, None, ALU.mult))
            st.wait()
            for n in range(2):
                w1 = qkw[:, n, 0:half].unsqueeze(1).to_broadcast([P, NT, half])
                w2 = qkw[:, n, half:HD].unsqueeze(1).to_broadcast([P, NT, half])
                st.done(V.tensor_tensor(tabs[:, :, 2 * n, 0:half], ang[:], w1, ALU.mult))
                st.done(V.tensor_tensor(tabs[:, :, 2 * n, half:HD], ang[:], w2, ALU.mult))
                st.done(V.scalar_tensor_tensor(out=tabs[:, :, 2 * n + 1, 0:half], in0=sin_[:], scalar=-1.0, in1=w2, op0=ALU.mult, op1=ALU.mult))
                st.done(V.tensor_tensor(tabs[:, :, 2 * n + 1, half:HD], sin_[:], w1, ALU.mult))
            assert st.n == TAB_OPS

            with dve.Fori(1, NID) as i:
                prep(i, lambda j: cond_dst(i, j))
            prep(R_BASE, base_dst)
            dve.wait_ge(pe_r, 1)
            V.tensor_copy(w_base[:, :, D:D + NE], bank[7][:, 0:KC * NE].rearrange("p (k e) -> p k e", k=KC)).then_inc(r_ev, 1)

            def l0(t):
                st = Steps(rt, (t - 1) * RT_OPS)
                dve.wait_ge(pe_mid, t)
                st.done(V.tensor_reduce(nmx[:], bank[4][:, 0:NE], AX.X, ALU.max, negate=True))
                dve.wait_ge(rexp, t)
                st.done(V.reciprocal(rsm[:, 1:2], rsm[:, 0:1]))
                st.wait()
                st.done(V.tensor_scalar(prb[:], rex[:], rsm[:, 1:2], None, ALU.mult))
                st.wait()
                by_j = prb[:].unsqueeze(1).to_broadcast([P, NE, NE])
                by_e = prb[:].unsqueeze(2).to_broadcast([P, NE, NE])
                st.done(V.tensor_tensor(cmp_[:], by_j, by_e, ALU.is_gt))
                st.done(V.tensor_tensor(eq[:], by_j, by_e, ALU.is_equal))
                st.wait()
                st.done(V.tensor_tensor(eq[:], eq[:], tri, ALU.mult))
                st.wait()
                st.done(V.tensor_tensor(cmp_[:], cmp_[:], eq[:], ALU.add))
                st.wait()
                st.done(V.tensor_reduce(rank[:], cmp_[:], AX.X, ALU.add))
                st.wait()
                st.done(V.scalar_tensor_tensor(out=sel[:], in0=rank[:], scalar=2.0, in1=prb[:], op0=ALU.is_lt, op1=ALU.mult))
                st.wait()
                st.done(V.tensor_reduce(rsm[:, 2:3], sel[:], AX.X, ALU.add))
                st.wait()
                st.done(V.reciprocal(rsm[:, 3:4], rsm[:, 2:3]))
                st.wait()
                st.done(V.tensor_scalar(wgt[:], sel[:], rsm[:, 3:4], 2.0, ALU.mult, ALU.mult))
                st.wait()
                st.done(V.tensor_tensor(mm[:], bank[4][:, NE:NE + P].rearrange("p (e r) -> p e r", e=NE),
                                        wgt[:].unsqueeze(2).to_broadcast([P, NE, RANK]), ALU.mult))
                assert st.n == RT_OPS
                dve.wait_ge(pe_y0, t)
                dve.wait_ge(xres_ld, t * 16)
                if not isinstance(t, int) or t > 1:
                    dve.wait_ge(x1_st, (t - 1) * 16)
                    dve.wait_ge(pe_x1t, t - 1)
                V.tensor_tensor(x1n[:], bank[3][:], xres[:], ALU.add).then_inc(x1_rdy, 1)

            l0(1)
            with dve.Fori(2, NT + 1) as t:
                l0(t)

            with dve.Fori(0, NHALF) as h:
                dve.drain().then_inc(phase, 1)
                dve.wait_ge(phase, 4 * h + 4)
                dve.sem_inc(gate["dve"], 1)
                V.memset(pz[:], 0.0).then_inc(pz_zero, 1)
                r0 = h * HALF_ROUNDS + R_HALF
                with dve.Fori(0, 4) as i:
                    prep(r0 + i, lambda j: wq_dst(i, j))
                prep(r0 + 4, lambda j: kv_dst(0, j))
                prep(r0 + 5, lambda j: kv_dst(1, j))
                with dve.Fori(0, 4) as i:
                    prep(r0 + 6 + i, lambda j: wo_dst(i, j))
                with dve.Fori(0, NPAGES // 16) as i:
                    prep(r0 + 10 + i, lambda j: kt_dst(i, j))
                for j in range(4):
                    dve.wait_ge(prep_ev[j], r0 + HALF_ROUNDS)
                dve.sem_inc(gate["dve"], 1)

                def rotate(t, j, u):
                    st = Steps(rope, j * ROPE_OPS + 4 * u)
                    n = 2 if u == 0 else 0
                    c = tab[:, n, :].unsqueeze(1).to_broadcast([P, REP, HD])
                    s1 = tab[:, n + 1, 0:half].unsqueeze(1).to_broadcast([P, REP, half])
                    s2 = tab[:, n + 1, half:HD].unsqueeze(1).to_broadcast([P, REP, half])
                    dve.wait_ge(unit_cp, j * ROPE_UNITS + u + 1)
                    if u == 0:
                        dve.wait_ge(tab_ld, (h * (NT + 1) + t + 1) * 16)
                    else:
                        st.wait()
                    st.done(V.tensor_tensor(qkf[:, u], qn[:], c, ALU.mult))
                    st.done(V.tensor_tensor(qb[:, :, 0:half], qn[:, :, half:HD], s1, ALU.mult))
                    st.done(V.tensor_tensor(qb[:, :, half:HD], qn[:, :, 0:half], s2, ALU.mult))
                    st.wait()
                    st.done(V.tensor_tensor(qkf[:, u], qkf[:, u], qb[:], ALU.add))

                def rsqrt(j):
                    st = Steps(rope, j * ROPE_OPS + 4 * ROPE_UNITS)
                    dve.wait_ge(unit_ev, j * ROPE_UNITS + ROPE_UNITS)
                    st.wait()
                    st.done(V.tensor_scalar(xs[:], ssq[:], EPS, None, ALU.add))
                    st.wait()
                    st.done(V.tensor_scalar(yi[:], xs[:].bitcast(I32), 1, None, ALU.logical_shift_right))
                    st.done(V.tensor_scalar(xh[:], xs[:], -0.5, None, ALU.mult))
                    st.wait()
                    st.done(V.tensor_scalar(yy[:].bitcast(I32), yi[:], -1.0, RSQRT_BITS, ALU.mult, ALU.add))
                    for _ in range(3):
                        st.wait()
                        st.done(V.tensor_tensor(y2[:], yy[:], yy[:], ALU.mult))
                        st.wait()
                        st.done(V.tensor_tensor(y3[:], y2[:], xh[:], ALU.mult))
                        st.wait()
                        st.done(V.scalar_tensor_tensor(out=yy[:], in0=y3[:], scalar=1.5, in1=yy[:], op0=ALU.add, op1=ALU.mult))

                def norm(j, part):
                    st = Steps(rope, j * ROPE_OPS + 4 * ROPE_UNITS + 13 + part)
                    if part == 0:
                        st.wait()
                    u0, u1 = (0, 2) if part == 0 else (2, ROPE_UNITS)
                    v = qkf[:, u0:u1].rearrange("p u r d -> p (u r) d")
                    st.done(V.tensor_tensor(v, v, yy[:, 4 * u0:4 * u1].unsqueeze(2).to_broadcast([P, 4 * (u1 - u0), HD]), ALU.mult))

                def gather(n, par, part, pg=None):
                    pg = regs(DVE_, pages[0:1, bass.ds(n * PG + part * 8, 8)])
                    for i in range(8):
                        ins = V.tensor_copy(kg[par][:, :, part * 8 + i, :],
                                            ktall[:, bass.ds(pg[i], 1)].rearrange("p a h s -> p (a h) s"))
                    if part:
                        ins.then_inc(kg_rdy, 1)

                def key_mask(t, b):
                    g = h * NT + t
                    if b:
                        dve.wait_ge(ttr, g * NP + b * HK2)
                        dve.sem_inc(gate["dve"], 1)
                    V.tensor_scalar(mask[:], keyidx[:], seqf[:, bass.ds(t * TB + b, 1)], BIG, ALU.is_ge, ALU.mult).then_inc(mk, 1)

                def least(t, p):
                    g = h * NT + t
                    b = p // HK2
                    if p % HK2 == 0:
                        key_mask(t, b)
                        dve.wait_ge(mk, g * TB + b + 1)
                        dve.sem_inc(gate["dve"], 1)
                    dve.wait_ge(s_mm, g * NP + p + 1)
                    dve.sem_inc(gate["dve"], 1)
                    V.tensor_tensor_reduce(out=sm[p % 2][:], in0=bank[p % 2][:], in1=mask[:], scale=1.0, scalar=mnew[:, p:p + 1],
                                           op0=ALU.add, op1=ALU.min, accum_out=mp[:, p:p + 1]).then_inc(ttr, 1)

                def out_norm(t, b):
                    g = h * NT + t
                    c = slice(b * HK2, (b + 1) * HK2)
                    dve.wait_ge(pe_o, g * TB + b + 1)
                    V.tensor_tensor(rsum[:, c], sumc[:, c], sumn[:, c], ALU.add).then_inc(osum, 1)
                    dve.wait_ge(osum, (g * TB + b) * 2 + 1)
                    V.reciprocal(rinv[:, c], rsum[:, c]).then_inc(osum, 1)
                    dve.wait_ge(osum, (g * TB + b) * 2 + 2)
                    V.tensor_tensor(on[:], bank[4 + b % 2][:].rearrange("p (h d) -> p h d", h=HK2),
                                    rinv[:, c].unsqueeze(2).to_broadcast([P, HK2, HD]), ALU.mult).then_inc(on_rdy, 1)

                def tail(j):
                    for k in range(2, 4):
                        dve.wait_ge(pe_qt, j * 4 + k + 1)
                        V.tensor_copy(qt[:, :, k], bank[k][:].rearrange("p (r b s) -> p b r s", r=REP, b=TB)).then_inc(qt_d, 1)
                    dve.wait_ge(sn_ev, j + 1)
                    V.tensor_reduce(mnew[:], sn[:], AX.X, ALU.min).then_inc(mn, 1)

                gather(0, 0, 0)
                gather(0, 0, 1)
                for u in range(ROPE_UNITS):
                    rotate(0, h * NT, u)
                rsqrt(h * NT)
                norm(h * NT, 0)
                norm(h * NT, 1)
                tail(h * NT)

                def tile(t, last):
                    g = h * NT + t
                    j = g + 1
                    dve.wait_ge(mn, g + 1)
                    dve.sem_inc(gate["dve"], 1)
                    least(t, 0)
                    for p in range(NP):
                        b = p // HK2
                        if p + 1 < NP:
                            least(t, p + 1)
                        if p % 4 in (1, 2) and not (last and b == TB - 1):
                            gather(t * TB + b + 1, (b + 1) % 2, p % 4 - 1)
                        if not last:
                            if p - 1 in FILL:
                                rotate(t + 1, j, FILL[p - 1])
                            if p == 11:
                                rsqrt(j)
                            if p in (12, 13):
                                norm(j, p - 12)
                        if p >= 4 and p % 4 == 0:
                            out_norm(t, p // 4 - 1)
                        if p % 2 == 0:
                            dve.wait_ge(pe_t, g * NP + p + 1)
                            V.tensor_copy(pts[0][:].rearrange("p k c -> p (k c)"), bank[2][:]).then_inc(pt_d, 1)
                    out_norm(t, TB - 1)
                    if not last:
                        tail(j)
                    dve.wait_ge(pe_op, g + 1)
                    dve.wait_ge(a_ld, g * 16 + 16)
                    V.tensor_tensor(an[:], bank[6][:], an[:], ALU.add).then_inc(op_ev, 1)

                with dve.Fori(0, NT - 1) as t:
                    tile(t, False)
                tile(NT - 1, True)

            dve.drain().then_inc(phase, 1)
            dve.wait_ge(phase, 4 * NHALF + 4)
            for u in range(3 * NI):
                if u % 2:
                    dve.wait_ge(prep_tr[u % 4], R_FFN + u // 4 + 1)
                    o, i = ffn_dst(u)
                    V.tensor_copy(o, i).then_inc(prep_ev[u % 4], 1)

            def group(n):
                for c in range(NI):
                    m = P if c < NI - 1 else ILAST
                    dve.wait_ge(silu, n * NI + c + 1)
                    V.tensor_tensor(ht[0:m, c, :], bank[2 + c % 2][0:m, :], sg[c % 2][0:m, :], ALU.mult).then_inc(hm, 1)
                for i in range(GT):
                    dve.wait_ge(pe_dn, n * GT + i + 1)
                    dve.wait_ge(x1b_ld[i % 2], (n * 2 + i // 2 + 1) * 16)
                    if not isinstance(n, int) or i >= 2:
                        dve.wait_ge(o_st[i % 2], (n * 2 + i // 2) * 16)
                    V.tensor_tensor(ob[i % 2][:], bank[4 + i % 2][:], x1b[i % 2][:], ALU.add).then_inc(out_add, 1)

            group(0)
            with dve.Fori(1, NGRP) as n:
                group(n)


_NAMES = ["x", "itok_B_3_7", "itok_Bx16_0_63", "itok_B_207_1644", "L0_cond_weight", "L0_ffn_base_W", "L0_ffn_router_W",
          "L0_ffn_lora_A", "L0_ffn_lora_B", "L1_cond_Wq", "L1_cond_Wk", "L1_cond_Wv", "L1_cond_Wo", "L1_cond_q_norm_w",
          "L1_cond_k_norm_w", "L1_cond_k_cache", "L1_cond_v_cache", "L1_ffn_codebook"]


def kernel(**inputs):
    import numpy as np
    import concourse.bacc as bacc
    from concourse.bass_utils import run_bass_kernel_spmd

    nc = bacc.Bacc("TRN2", target_bir_lowering=False, num_devices=1, dynamic_dma_scratch_size=4096)
    arrays = {f"in_{n}": np.ascontiguousarray(inputs[n]) for n in _NAMES}
    arrays["idx_all"] = np.concatenate([np.asarray(inputs[f"L1_ffn_idx_{n}"]).reshape(-1) for n in ("gate", "up", "down")]).reshape(P, -1)
    half = HD // 2
    arrays["con_a"] = np.concatenate([np.eye(P), np.tile(np.arange(L), (P, 1))], 1).astype(np.float32)
    invf = (np.float32(1.0) / np.float32(10000.0) ** (np.arange(0, HD, 2, dtype=np.float32) / np.float32(HD))).astype(np.float32)
    tri = (np.arange(NE)[:, None] > np.arange(NE)[None, :]).astype(np.float32).reshape(-1)
    arrays["con_b"] = np.concatenate([np.tile(invf, (P, 1)), (np.arange(P) % S)[:, None], np.tile(tri, (P, 1))], 1).astype(np.float32)
    args = [nc.dram_tensor(n, a.shape, mybir.dt.from_np(a.dtype), kind="ExternalInput").ap() for n, a in arrays.items()]
    out = nc.dram_tensor("out", (64, S, D), F32, kind="ExternalOutput").ap()
    adaln_ffn_kernel(nc, *args, out)
    r = run_bass_kernel_spmd(nc, [arrays], core_ids=[0])
    return r.results[0]["out"]
```

```python
from contextlib import ExitStack

import concourse.bass as bass
from concourse import mybir

F32 = mybir.dt.float32
F32R = mybir.dt.float32r
I32 = mybir.dt.int32
ALU = mybir.AluOpType
ACT = mybir.ActivationFunctionType
AX = mybir.AxisListType
PE_, DVE_, SP_ = mybir.EngineType.PE, mybir.EngineType.DVE, mybir.EngineType.SP

P = 128
S = 32
TB = P // S
D = 512
KC = D // P
NE, RANK = 8, 16
NHALF = 2
PG = 16
PSZ = 32
L = PG * PSZ
HD = 128
REP = 4
HK2 = 4
HQ2 = REP * HK2
QKV = (HQ2 + 2 * HK2) * P
NP = TB * HK2
BIG = 1e30
SCALE = HD ** -0.5
EPS = 1e-6
MAGIC = 12582912.0
TWO_PI = 6.283185307179586
PI1 = 6.28125
PI2 = 0.0019350051879882812
PI3 = TWO_PI - PI1 - PI2
RSQRT_BITS = 1597463007.0
ROPE_UNITS = 5
ROPE_OPS = 4 * ROPE_UNITS + 13 + 2
CHUNK = 43
RED_OPS = 1 + TB + 1 + 1 + 2 + 3 + 1
TAB_OPS = RED_OPS + 3 + 8
RT_OPS = 13
SN_AT = 12


def adaln_ffn_kernel(nc, x, ids, table, seqlens, w_cond, base_w, router_w, lora_a, lora_b,
                     wq, wk, wv, wo, qnw, knw, k_cache, v_cache, codebook, idx_all,
                     con_a, con_b, out):
    NB = x.shape[0]
    NT = NB * S // P
    NPAGES = k_cache.shape[0]
    NID = w_cond.shape[0]
    NG = idx_all.shape[1]
    CW = codebook.shape[1]
    I = NG * P * CW // (3 * D)
    NI = -(-I // P)
    ILAST = I - (NI - 1) * P
    ROUNDS = NG // CHUNK // 2
    assert NB * S == NT * P and NG % (2 * CHUNK) == 0
    GT = 4
    NGRP = NT // GT

    x_t = x.rearrange("(t b) s d -> t (b s) d", b=TB)
    out_t = out.rearrange("(t b) s d -> t (b s) d", b=TB)
    x1_d = nc.dram_tensor("x1_d", (NT, P, D), F32).ap()
    x1t_d = nc.dram_tensor("x1t_d", (NT + 1, P, D), F32).ap()
    tab_d = nc.dram_tensor("tab_d", (NT + 1, P, 4 * HD), F32).ap()
    qkv_d = nc.dram_tensor("qkv_d", (NT + 1, P, QKV), F32).ap()
    a_d = nc.dram_tensor("a_d", (NT, P, D), F32).ap()
    w_d = nc.dram_tensor("w_d", (P, NG * CW), F32).ap()

    with ExitStack() as ctx:
        def sem(name):
            return ctx.enter_context(nc.semaphore(name))

        bank = [ctx.enter_context(nc.psum_tensor(f"bank{i}", [P, 512], F32)) for i in range(8)]

        base = (nc.sbuf_base + 63) // 64 * 64
        at = [base]

        def sb(name, shape, dt=F32):
            t = nc.alloc_sbuf_tensor_at(name, shape, dt, offset=at[0])
            n = 4
            for s in shape[1:]:
                n *= s
            at[0] += (n + 31) // 32 * 32
            return t

        ident = sb("ident", [P, P])
        keyidx = sb("keyidx", [P, L])
        pages = sb("pages", [1, NB * PG], I32)
        seqf = sb("seqf", [P, NB])
        gidx = [sb(f"gidx{u}", [P, CHUNK], I32) for u in range(2)]
        stage = [sb(f"stage{u}", [P, CHUNK, CW]) for u in range(2)]
        nat = [sb(f"nat{j}", [P, 512]) for j in range(4)]
        nat_at = at[0] - 4 * 2048
        phase_at = at[0]

        wt_all = sb("wt_all", [P, NID, KC, D])
        w_base = sb("w_base", [P, KC, D + NE + NE * RANK])
        lorab = sb("lorab", [P, D])
        routn = sb("routn", [NE, D])
        idb = sb("idb", [1, NB], I32)
        con2 = sb("con2", [P, con_b.shape[1]])
        seqi = sb("seqi", [P, NB], I32)
        qkw = sb("qkw", [P, 2, HD])
        pos = sb("pos", [P, NT])
        ang = sb("ang", [P, NT, HD // 2])
        red = sb("red", [P, NT, HD // 2])
        sin_ = sb("sin_", [P, NT, HD // 2])
        cos_ = sb("cos_", [P, NT, HD // 2])
        tabs = sb("tabs", [P, NT, 4, HD])
        zero = sb("zero", [P, D])
        xn = sb("xn", [P, D])
        xtz = sb("xtz", [P, KC, 5 * P])
        cn = sb("cn", [P, D])
        ct = sb("ct", [P, D])
        mm = sb("mm", [P, NE, RANK])
        mt = sb("mt", [P, P])
        xres = sb("xres", [P, D])
        x1n = sb("x1n", [P, D])
        x1t = sb("x1t", [P, D])
        nmx = sb("nmx", [P, 1])
        rex = sb("rex", [P, NE])
        rsm = sb("rsm", [P, 4])
        prb = sb("prb", [P, NE])
        cmp_ = sb("cmp_", [P, NE, NE])
        eq = sb("eq", [P, NE, NE])
        rank = sb("rank", [P, NE])
        sel = sb("sel", [P, NE])
        wgt = sb("wgt", [P, NE])
        end0 = at[0]

        at[0] = phase_at
        qkv = [sb(f"qkv{i}", [P, QKV]) for i in range(2)]
        heads_at = at[0]
        wqs = sb("wqs", [P, 2, KC, HQ2 * HD], F32R)
        wkvs = sb("wkvs", [P, 2, KC, 2 * HK2 * HD], F32R)
        xt = [sb(f"xt{i}", [P, KC, P]) for i in range(2)]
        xs2 = [sb(f"xs2_{i}", [P, 2, KC, P], F32R) for i in range(2)]
        tab = [sb(f"tab{i}", [P, 4, HD]) for i in range(2)]
        qn = sb("qn", [P, ROPE_UNITS, REP, HD])
        qb = sb("qb", [P, REP, HD])
        qkf = [sb(f"qkf{i}", [P, ROPE_UNITS, REP, HD]) for i in range(2)]
        ssq = [sb(f"ssq{i}", [P, 20]) for i in range(2)]
        xs = sb("xs", [P, 20])
        xh = sb("xh", [P, 20])
        yy = sb("yy", [P, 20])
        y2 = sb("y2", [P, 20])
        y3 = sb("y3", [P, 20])
        yi = sb("yi", [P, 20], I32)
        end1 = at[0]

        at[0] = heads_at
        ots = sb("ots", [P, 2, HQ2, P], F32R)
        wots = sb("wots", [P, 2, HQ2, D], F32R)
        ktall = sb("ktall", [P, NPAGES, HK2, PSZ])
        vg = [sb(f"vg{i}", [P, KC, HK2 * HD]) for i in range(2)]
        kg = [sb(f"kg{i}", [P, HK2, PG, PSZ]) for i in range(2)]
        sm = [sb(f"sm{i}", [P, L]) for i in range(2)]
        pts = [sb(f"pts{i}", [P, KC, P]) for i in range(2)]
        pz = sb("pz", [P, TB, HK2, P])
        pnt = sb("pnt", [P, HK2, P])
        sn = [sb(f"sn{i}", [P, NP, S]) for i in range(2)]
        on = sb("on", [P, HK2, HD])
        an = sb("an", [P, D])
        mask = sb("mask", [P, L])
        mp = sb("mp", [P, NP])
        mnew = sb("mnew", [P, NP])
        sumc = sb("sumc", [P, NP])
        sumn = sb("sumn", [P, NP])
        rsum = sb("rsum", [P, NP])
        rinv = sb("rinv", [P, NP])
        end1 = max(end1, at[0])

        at[0] = phase_at
        wgus = [sb(f"w{n}s", [P, 2, KC, I], F32R) for n in "gu"]
        wds = sb("wds", [P, 2, NI, D], F32R)
        an4 = sb("an4", [P, GT, D])
        at4 = sb("at4", [P, 2, KC, GT * P], F32R)
        ht = sb("ht", [P, 2, NI, GT * P], F32R)
        sg = [sb(f"sg{i}", [P, GT * P]) for i in range(2)]
        end2 = at[0]
        at[0] = nat_at
        x1b = [sb(f"x1b{i}", [P, D]) for i in range(2)]
        ob = [sb(f"ob{i}", [P, D]) for i in range(2)]
        assert at[0] == phase_at
        assert max(end0, end1, end2) <= 229344, (end0, end1, end2)

        c_ld = sem("c_ld")
        c2_ld = sem("c2_ld")
        nat_full = [sem(f"nat_full{j}") for j in range(4)]
        prep_tr = [sem(f"prep_tr{j}") for j in range(4)]
        prep_ev = [sem(f"prep_ev{j}") for j in range(4)]
        phase = sem("phase")
        gate = {e: sem(f"gate_{e}") for e in ("pool", "act", "dve", "sp", "pe")}
        rtab = sem("rtab")
        trig = sem("trig")
        tab_st = sem("tab_st")
        zeroed = sem("zeroed")
        x_ld = sem("x_ld")
        xres_ld = sem("xres_ld")
        pe_xt, xtz_ev = sem("pe_xt"), sem("xtz_ev")
        pe_cond, c_ev = sem("pe_cond"), sem("c_ev")
        pe_ct, ct_ev = sem("pe_ct"), sem("ct_ev")
        pe_mid, rt = sem("pe_mid"), sem("rt")
        rexp = sem("rexp")
        pe_mt, mt_ev = sem("pe_mt"), sem("mt_ev")
        pe_y0, x1_rdy = sem("pe_y0"), sem("x1_rdy")
        pe_x1t, x1t_ev = sem("pe_x1t"), sem("x1t_ev")
        x1_st, x1t_st = sem("x1_st"), sem("x1t_st")
        pe_r, r_ev = sem("pe_r"), sem("r_ev")
        pz_zero = sem("pz_zero")
        xt_ld = [sem(f"xt_ld{i}") for i in range(2)]
        tab_ld = [sem(f"tab_ld{i}") for i in range(2)]
        xs_hi, xs_lo = sem("xs_hi"), sem("xs_lo")
        prep_hi = sem("prep_hi")
        unit_mm, unit_cp, unit_ev = sem("unit_mm"), sem("unit_cp"), sem("unit_ev")
        rope = sem("rope")
        pe_v, v_ev = sem("pe_v"), sem("v_ev")
        pe_tb, tb_ev = sem("pe_tb"), sem("tb_ev")
        proj_st = [sem(f"proj_st{i}") for i in range(2)]
        pad_st = sem("pad_st")
        qkv_ld = [sem(f"qkv_ld{i}") for i in range(2)]
        v_ld = [sem(f"v_ld{i}") for i in range(2)]
        a_ld, a_st = sem("a_ld"), sem("a_st")
        pe_sn, sn_ev, mn = sem("pe_sn"), sem("sn_ev"), sem("mn")
        kg_rdy, mk = sem("kg_rdy"), sem("mk")
        s_mm, ttr = sem("s_mm"), sem("ttr")
        ex, exn = sem("ex"), sem("exn")
        pe_t, pt_a = sem("pe_t"), sem("pt_a")
        pe_tn, tn_ev = sem("pe_tn"), sem("tn_ev")
        pe_o, osum, on_rdy = sem("pe_o"), sem("osum"), sem("on_rdy")
        pe_ot, ot_hi, ot_ev = sem("pe_ot"), sem("ot_hi"), sem("ot_ev")
        pe_op, op_ev = sem("pe_op"), sem("op_ev")
        gi_ld = [sem(f"gi_ld{u}") for u in range(2)]
        gat = [sem(f"gat{u}") for u in range(2)]
        g_st = [sem(f"g_st{u}") for u in range(2)]
        an_ld, pe_at, at_hi, at_ev = sem("an_ld"), sem("pe_at"), sem("at_hi"), sem("at_ev")
        pe_gu, silu, hmul, ht_hi, hm = sem("pe_gu"), sem("silu"), sem("hmul"), sem("ht_hi"), sem("hm")
        pe_dn, out_add = sem("pe_dn"), sem("out_add")
        x1b_ld = [sem(f"x1b_ld{i}") for i in range(2)]
        o_st = [sem(f"o_st{i}") for i in range(2)]

        R_BASE = NID
        R_HALF = NID + 1
        HALF_ROUNDS = 4 + 1 + 1 + 4 + NPAGES // 16
        R_FFN = R_HALF + NHALF * HALF_ROUNDS

        def regs(engine, ap):
            return nc.values_load_multi_w_load_instructions(
                ap, engines=[engine], min_val=0, max_val=63,
                skip_runtime_bounds_check_because="they index a table of 64 pages or fewer")[1]

        def cols(j):
            return bank[j][:].rearrange("p (k c) -> p k c", k=4)

        def cond_dst(i, j):
            return wt_all[:, bass.ds(i, 1), :, j * P:(j + 1) * P].rearrange("p a k c -> p (a k) c"), cols(j)

        def base_dst(j):
            return w_base[:, :, j * P:(j + 1) * P], cols(j)

        def wq_dst(i, j, part):
            return wqs[:, part, :, bass.ds(i * 512 + j * P, P)], cols(j)

        def kv_dst(v, j, part):
            return wkvs[:, part, :, v * 512 + j * P:v * 512 + (j + 1) * P], cols(j)

        def wo_dst(i, j, part):
            return wots[:, part, bass.ds(i * 4 + j, 1), :].rearrange("p a d -> p (a d)"), bank[j][:]

        def qt_of(buf):
            return buf[:, 0:HQ2 * P].rearrange("p (b h r s) -> p b h r s", b=TB, h=HK2, r=REP)

        def kt_of(buf):
            return buf[:, HQ2 * P:(HQ2 + HK2) * P]

        def v_of(buf):
            return buf[:, (HQ2 + HK2) * P:QKV]

        def each_tile(engine, tile):
            tile(0, 0, 0, True, False)
            with engine.Fori(0, NT // 2 - 1) as i:
                tile(i * 2 + 1, i, 1, False, False)
                tile(i * 2 + 2, i + 1, 0, False, False)
            tile(NT - 1, NT // 2 - 1, 1, False, True)

        def each_tile_2(engine, tile):
            tile(0, 0, 0, True, False)
            tile(1, 0, 1, False, False)
            with engine.Fori(1, NT // 2 - 1) as i:
                tile(i * 2, i, 0, False, False)
                tile(i * 2 + 1, i, 1, False, False)
            tile(NT - 2, NT // 2 - 1, 0, False, False)
            tile(NT - 1, NT // 2 - 1, 1, False, True)

        SPLITS = 10
        LOADS = (NT // 2 + 1, NT // 2)

        def kt_dst(i, j):
            return (ktall[:, bass.ds(i * 16 + j * 4, 4)].rearrange("p g h s -> p h g s"),
                    bank[j][:].rearrange("p (h g s) -> p h g s", h=HK2, g=4))

        def ffn_dst(u, part):
            m, c = divmod(u, NI)
            n = P if c < NI - 1 else ILAST
            if m < 2:
                return wgus[m][:, part, :, c * P:c * P + n], cols(u % 4)[:, :, 0:n]
            return wds[0:n, part, c, :], bank[u % 4][0:n, :]

        def xtz_diag(b):
            return xtz[:, :, b * (P + S):b * (P + S) + S]

        block = ctx.enter_context(nc.Block())

        @block.sync
        def _(sp):
            def nat_round(rnd, srcs, whole=False):
                for j, (dst, src) in enumerate(srcs):
                    if not (isinstance(rnd, int) and rnd == 0):
                        sp.wait_ge(prep_tr[3 if whole else j], rnd)
                    sp.dma_start(dst, src).then_inc(nat_full[j], 16)

            sp.dma_start(ident[:], con_a[:, 0:P]).then_inc(c_ld, 16)
            nat_round(0, [(nat[j][:], w_cond[0, j * P:(j + 1) * P, :]) for j in range(4)])
            sp.dma_start(keyidx[:], con_a[:, P:]).then_inc(c_ld, 16)
            sp.dma_start(con2[:], con_b).then_inc(c2_ld, 16)
            sp.dma_start(seqi[:], seqlens.partition_broadcast(P)).then_inc(c2_ld, 16)
            sp.dma_start(qkw[:, 0, :], qnw.partition_broadcast(P)).then_inc(c2_ld, 16)
            sp.dma_start(qkw[:, 1, :], knw.partition_broadcast(P)).then_inc(c2_ld, 16)
            sp.dma_start(pages[:], table.rearrange("(a b) c -> a (b c)", a=1)).then_inc(c_ld, 16)
            sp.dma_start(idb[:], ids.rearrange("(a b) -> a b", a=1)).then_inc(c_ld, 16)
            sp.dma_start(routn[:], router_w).then_inc(c_ld, 16)
            sp.dma_start(lorab[:], lora_b.rearrange("e r d -> (e r) d")).then_inc(c_ld, 16)
            for kc in range(KC):
                sp.dma_start(w_base[:, kc, D + NE:].rearrange("p (e r) -> p e r", e=NE),
                             lora_a[:, kc * P:(kc + 1) * P, :].rearrange("e p r -> p e r")).then_inc(c_ld, 16)
            sp.dma_start(xn[:], x_t[0]).then_inc(x_ld, 16)
            with sp.Fori(1, NID) as i:
                nat_round(i, [(nat[j][:], w_cond[bass.ds(i, 1), j * P:(j + 1) * P, :]
                               .rearrange("a p d -> (a p) d")) for j in range(4)])
            nat_round(R_BASE, [(nat[j][:], base_w[j * P:(j + 1) * P, :]) for j in range(4)])
            sp.wait_ge(zeroed, 1)
            sp.dma_start(a_d.rearrange("t p d -> p t d"),
                         zero[:].unsqueeze(1).to_broadcast([P, NT, D])).then_inc(a_st, 16)
            sp.wait_ge(rtab, TAB_OPS)
            sp.dma_start(tab_d[0:NT].rearrange("t p c -> p t c"),
                         tabs[:].rearrange("p t a c -> p t (a c)")).then_inc(tab_st, 16)
            sp.dma_start(tab_d[NT], tabs[:, NT - 1].rearrange("p a c -> p (a c)")).then_inc(tab_st, 16)

            def l0(t, load, res, pad=False):
                if load:
                    sp.wait_ge(pe_xt, t + 1)
                    sp.dma_start(xn[:], x_t[bass.ds(t + 1, 1)].rearrange("a p d -> (a p) d")).then_inc(x_ld, 16)
                if res:
                    if not isinstance(t, int) or t > 1:
                        sp.wait_ge(x1_rdy, t - 1)
                    sp.dma_start(xres[:], x_t[bass.ds(t - 1, 1)].rearrange("a p d -> (a p) d")).then_inc(xres_ld, 16)
                    sp.wait_ge(x1_rdy, t)
                    sp.dma_start(x1_d[bass.ds(t - 1, 1)].rearrange("a p d -> (a p) d"), x1n[:]).then_inc(x1_st, 16)
                    sp.wait_ge(x1t_ev, t)
                    sp.dma_start(x1t_d[bass.ds(t - 1, 1)].rearrange("a p d -> (a p) d"), x1t[:]).then_inc(x1t_st, 16)
                    if pad:
                        sp.dma_start(x1t_d[NT], x1t[:]).then_inc(x1t_st, 16)

            l0(0, True, False)
            l0(1, True, True)
            with sp.Fori(2, NT - 1) as t:
                l0(t, True, True)
            l0(NT - 1, False, True)
            l0(NT, False, True, pad=True)
            sp.wait_ge(x1_st, 16 * NT)
            sp.wait_ge(x1t_st, 16 * (NT + 1))
            sp.wait_ge(tab_st, 32)

            with sp.Fori(0, NHALF) as h:
                sp.drain().then_inc(phase, 1)
                sp.wait_ge(phase, 8 * h + 4)
                sp.sem_inc(gate["sp"], 1)
                r0 = h * HALF_ROUNDS + R_HALF
                with sp.Fori(0, 4) as i:
                    nat_round(r0 + i, [(nat[j][:], wq[bass.ds(h * (HQ2 * HD) + i * 512 + j * P, P), :]) for j in range(4)])
                nat_round(r0 + 4, [(nat[j][:], wk[bass.ds(h * (HK2 * HD) + j * P, P), :]) for j in range(4)])
                nat_round(r0 + 5, [(nat[j][:], wv[bass.ds(h * (HK2 * HD) + j * P, P), :]) for j in range(4)])

                def xt_load(t, par):
                    sp.dma_start(xt[par][:].rearrange("p k c -> p (k c)"),
                                 x1t_d[bass.ds(t, 1)].rearrange("a p d -> (a p) d")).then_inc(xt_ld[par], 16)

                def tab_load(t, par):
                    sp.dma_start(tab[par][:].rearrange("p k c -> p (k c)"),
                                 tab_d[bass.ds(t, 1)].rearrange("a p d -> (a p) d")).then_inc(tab_ld[par], 16)

                def proj_store(t, par):
                    sp.dma_start(qkv_d[bass.ds(t, 1)].rearrange("a p d -> (a p) d"), qkv[par][:]).then_inc(proj_st[par], 16)

                for t in range(2):
                    xt_load(t, t)
                    tab_load(t, t)

                def project(t, n, par, first, last):
                    g = h * NT + t
                    if not last:
                        sp.wait_ge(xs_lo, g + 1)
                        sp.sem_inc(gate["sp"], 1)
                        xt_load(t + 2, par)
                        sp.wait_ge(rope, g * ROPE_OPS + 4 * ROPE_UNITS)
                        sp.sem_inc(gate["sp"], 1)
                        tab_load(t + 2, par)
                    if not first:
                        sp.wait_ge(tb_ev, g * ROPE_UNITS + 2)
                        sp.sem_inc(gate["sp"], 1)
                        proj_store(t - 1, 1 - par)
                    if isinstance(t, int) and t == 1:
                        sp.dma_start(qkv_d[NT], qkv[0][:]).then_inc(pad_st, 16)

                each_tile_2(sp, project)
                sp.wait_ge(tb_ev, (h + 1) * (NT * ROPE_UNITS) + 2)
                sp.sem_inc(gate["sp"], 1)
                proj_store(NT - 1, 1)
                sp.wait_ge(xt_ld[0], (h + 1) * (16 * LOADS[0]))
                sp.sem_inc(gate["sp"], 1)
                sp.wait_ge(tab_ld[0], (h + 1) * (16 * LOADS[0]))
                sp.sem_inc(gate["sp"], 1)
                sp.drain().then_inc(phase, 1)
                sp.wait_ge(phase, 8 * h + 8)
                sp.sem_inc(gate["sp"], 1)

                with sp.Fori(0, 4) as i:
                    nat_round(r0 + 6 + i, [(nat[j][:], wo[j * P:(j + 1) * P, bass.ds(h * (HQ2 * HD) + i * 512, 512)])
                                           for j in range(4)], whole=True)
                with sp.Fori(0, NPAGES // 16) as i:
                    nat_round(r0 + 10 + i, [(nat[j][:].rearrange("p (h d) -> p h d", h=HK2),
                                             k_cache[bass.ds(i * 16 + j * 4, 4), :, bass.ds(h * HK2, HK2), :]
                                             .rearrange("a s h d -> (a s) h d")) for j in range(4)], whole=True)

                def v_load(n, par):
                    pg = regs(SP_, pages[0:1, bass.ds(n * PG, PG)])
                    for j in range(PG):
                        q = j % 4
                        sp.dma_start(vg[par][PSZ * q:PSZ * (q + 1), j // 4, :],
                                     v_cache[bass.ds(pg[j], 1), :, bass.ds(h * HK2, HK2), :]
                                     .rearrange("a s h d -> (a s) (h d)")).then_inc(v_ld[par], 16)

                def qkv_load(t, par):
                    sp.dma_start(qkv[par][:], qkv_d[bass.ds(t, 1)].rearrange("a p d -> (a p) d")).then_inc(qkv_ld[par], 16)

                for par in range(2):
                    sp.wait_ge(proj_st[par], (h + 1) * (16 * (NT // 2)))
                    sp.sem_inc(gate["sp"], 1)
                sp.wait_ge(pad_st, (h + 1) * 16)
                sp.sem_inc(gate["sp"], 1)
                qkv_load(0, 0)
                qkv_load(1, 1)
                v_load(0, 0)
                v_load(1, 1)

                def sum_load(t):
                    sp.wait_ge(a_st, (h * NT + t + 1) * 16)
                    sp.sem_inc(gate["sp"], 1)
                    sp.dma_start(an[:], a_d[bass.ds(t, 1)].rearrange("a p d -> (a p) d")).then_inc(a_ld, 16)

                def sum_store(t):
                    sp.wait_ge(op_ev, h * NT + t + 1)
                    sp.sem_inc(gate["sp"], 1)
                    sp.dma_start(a_d[bass.ds(t, 1)].rearrange("a p d -> (a p) d"), an[:]).then_inc(a_st, 16)

                def attend(t, n, par, first, last):
                    g = h * NT + t
                    if not first:
                        sum_load(t - 1)
                    for b in range(TB):
                        if not (last and b >= 2):
                            sp.wait_ge(pe_o, g * TB + b + 1)
                            sp.sem_inc(gate["sp"], 1)
                            v_load(t * TB + b + 2, b % 2)
                        if b == 0 and not first:
                            sum_store(t - 1)
                        if b == TB - 1 and not last:
                            qkv_load(t + 2, par)

                each_tile(sp, attend)
                sum_load(NT - 1)
                sum_store(NT - 1)
                sp.wait_ge(qkv_ld[0], (h + 1) * (16 * LOADS[0]))
                sp.sem_inc(gate["sp"], 1)

            sp.drain().then_inc(phase, 1)
            sp.wait_ge(phase, 8 * NHALF + 4)
            sp.wait_ge(a_st, 16 * (NHALF * NT + 1))
            for u in range(2):
                sp.wait_ge(g_st[u], 16 * ROUNDS)
            flat = w_d.rearrange("p c -> (p c)")
            wrow = [flat[m * I * D:(m + 1) * I * D].rearrange("(i j) -> i j", j=D) for m in range(2)]
            wdrow = flat[2 * I * D:].rearrange("(i j) -> i j", j=I)
            for u in range(3 * NI):
                m, c = divmod(u, NI)
                n = P if c < NI - 1 else ILAST
                r, j = R_FFN + u // 4, u % 4
                sp.wait_ge(prep_tr[j], r)
                if m < 2:
                    sp.dma_start(nat[j][0:n, :], wrow[m][c * P:c * P + n, :]).then_inc(nat_full[j], 16)
                else:
                    sp.dma_start(nat[j][:].rearrange("p (o c) -> p o c", o=4)[:, :, 0:n],
                                 wdrow[:, c * P:c * P + n].rearrange("(o p) c -> p o c", p=P)).then_inc(nat_full[j], 16)

            def an_load(n):
                sp.dma_start(an4[:], a_d[bass.ds(n * GT, GT)].rearrange("t p d -> p t d")).then_inc(an_ld, 16)

            an_load(0)
            for j in range(4):
                sp.wait_ge(prep_tr[j], R_FFN + (3 * NI - j + 3) // 4)

            def group(n, last):
                if not last:
                    sp.wait_ge(pe_at, (n + 1) * 4)
                    an_load(n + 1)
                for i in range(GT):
                    sp.wait_ge(out_add, n * GT + i + 1)
                    sp.dma_start(x1b[i % 2][:], x1_d[bass.ds(n * GT + i, 1)].rearrange("a p d -> (a p) d")).then_inc(x1b_ld[i % 2], 16)
                    if i >= 1:
                        sp.wait_ge(out_add, n * GT + i + 2)
                        sp.dma_start(out_t[bass.ds(n * GT + i - 1, 1)].rearrange("a p d -> (a p) d"), ob[(i - 1) % 2][:]).then_inc(o_st[(i - 1) % 2], 16)
                sp.wait_ge(out_add, n * GT + GT + 2)
                sp.dma_start(out_t[bass.ds(n * GT + GT - 1, 1)].rearrange("a p d -> (a p) d"), ob[(GT - 1) % 2][:]).then_inc(o_st[(GT - 1) % 2], 16)

            with sp.Fori(0, NGRP - 1) as n:
                group(n, False)
            group(NGRP - 1, True)
            for i in range(2):
                sp.wait_ge(o_st[i], 16 * (NT // 2))

        @block.gpsimd
        def _(pool):
            def load_numbers(r, u):
                pool.dma_start(gidx[u][:], idx_all[:, bass.ds((r * 2 + u) * CHUNK, CHUNK)]).then_inc(gi_ld[u], 16)

            def store(r, u, more):
                pool.wait_ge(gat[u], (r + 1) * (16 * CHUNK))
                pool.sem_inc(gate["pool"], 1)
                pool.dma_start(w_d[:, bass.ds((r * 2 + u) * (CHUNK * CW), CHUNK * CW)],
                               stage[u][:].rearrange("p n c -> p (n c)")).then_inc(g_st[u], 16)
                if more:
                    load_numbers(r + 1, u)

            def round_(r, first, last):
                for u in range(2):
                    pool.wait_ge(gi_ld[u], (r + 1) * 16)
                    pool.sem_inc(gate["pool"], 1)
                    if not first:
                        pool.wait_ge(g_st[u], r * 16)
                        pool.sem_inc(gate["pool"], 1)
                    for n in range(CHUNK):
                        if n == 8:
                            if u:
                                store(r, 0, not last)
                            elif not first:
                                store(r - 1, 1, True)
                        pool.indirect_dma_start(
                            out=stage[u][:, n, :], out_offset=None, in_=codebook,
                            in_offset=bass.IndirectOffsetOnAxis(ap=gidx[u][:, n:n + 1], axis=0)).then_inc(gat[u], 16)

            load_numbers(0, 0)
            load_numbers(0, 1)
            round_(0, True, False)
            with pool.Fori(1, ROUNDS - 1) as r:
                round_(r, False, False)
            round_(ROUNDS - 1, False, True)
            store(ROUNDS - 1, 1, False)

        @block.scalar
        def _(act):
            def copy(dst, src):
                return nc.scalar.activation(dst, src, ACT.Copy)

            def prep(rnd, dst):
                for j in (0, 2):
                    act.wait_ge(prep_tr[j], rnd + 1)
                    act.sem_inc(gate["act"], 1)
                    o, i = dst(j)
                    copy(o, i).then_inc(prep_ev[j], 1)

            def prep_high(rnd, dst):
                for j in range(4):
                    act.wait_ge(prep_tr[j], rnd + 1)
                    act.sem_inc(gate["act"], 1)
                    o, i = dst(j)
                    copy(o, i).then_inc(prep_hi, 1)

            act.sem_inc(tb_ev, 2)
            prep(0, lambda j: cond_dst(0, j))
            act.wait_ge(rtab, RED_OPS)
            nc.scalar.activation(sin_[:].rearrange("p a b -> p (a b)"), red[:].rearrange("p a b -> p (a b)"), ACT.Sin).then_inc(trig, 1)
            nc.scalar.activation(cos_[:].rearrange("p a b -> p (a b)"), red[:].rearrange("p a b -> p (a b)"), ACT.Sin, scale=0.5).then_inc(trig, 1)
            with act.Fori(1, NID) as i:
                prep(i, lambda j: cond_dst(i, j))
            prep(R_BASE, base_dst)
            act.wait_ge(zeroed, 2)
            act.wait_ge(pe_xt, 1)
            for b in range(TB):
                ins = copy(xtz_diag(b), bank[0][:].rearrange("p (k c) -> p k c", k=KC)[:, :, b * S:(b + 1) * S])
            ins.then_inc(xtz_ev, 1)

            def l0(t, cond, nxt, prev):
                if prev:
                    act.wait_ge(rt, (t - 1) * RT_OPS + 1)
                    nc.scalar.activation(rex[:], bank[4][:, 0:NE], ACT.Exp, bias=nmx[:], accum_out=rsm[:, 0:1]).then_inc(rexp, 1)
                if cond:
                    act.wait_ge(pe_cond, t + 1)
                    copy(cn[:], bank[1][:]).then_inc(c_ev, 1)
                if nxt:
                    act.wait_ge(pe_xt, t + 2)
                    for b in range(TB):
                        ins = copy(xtz_diag(b), bank[0][:].rearrange("p (k c) -> p k c", k=KC)[:, :, b * S:(b + 1) * S])
                    ins.then_inc(xtz_ev, 1)
                if prev:
                    act.wait_ge(pe_mt, t)
                    copy(mt[:], bank[5][:, 0:P]).then_inc(mt_ev, 1)
                if cond:
                    act.wait_ge(pe_ct, t + 1)
                    copy(ct[:], bank[2][:]).then_inc(ct_ev, 1)
                if prev:
                    act.wait_ge(pe_x1t, t)
                    if not isinstance(t, int) or t > 1:
                        act.wait_ge(x1t_st, (t - 1) * 16)
                    copy(x1t[:], bank[6][:]).then_inc(x1t_ev, 1)

            l0(0, True, True, False)
            l0(1, True, True, True)
            with act.Fori(2, NT - 1) as t:
                l0(t, True, True, True)
            l0(NT - 1, True, False, True)
            l0(NT, False, False, True)

            with act.Fori(0, NHALF) as h:
                act.drain().then_inc(phase, 1)
                act.wait_ge(phase, 8 * h + 4)
                act.sem_inc(gate["act"], 1)
                r0 = h * HALF_ROUNDS + R_HALF
                with act.Fori(0, 4) as i:
                    prep_high(r0 + i, lambda j: wq_dst(i, j, 0))
                prep_high(r0 + 4, lambda j: kv_dst(0, j, 0))
                prep_high(r0 + 5, lambda j: kv_dst(1, j, 0))

                def x_high(t, n, par):
                    act.wait_ge(xt_ld[par], (h * LOADS[par] + n + 1) * 16)
                    copy(xs2[par][:, 0], xt[par][:]).then_inc(xs_hi, 1)

                def unit(g, par, u, first):
                    act.wait_ge(unit_mm, g * ROPE_UNITS + u + 1)
                    if not first:
                        act.wait_ge(rope, g * ROPE_OPS + (4 * u + 3 - ROPE_OPS))
                    act.sem_inc(gate["act"], 1)
                    copy(qn[:, u].rearrange("p r d -> p (r d)"), bank[u][:]).then_inc(unit_cp, 1)
                    act.wait_ge(unit_cp, g * ROPE_UNITS + u + 1)
                    for i in range(REP):
                        ins = nc.scalar.activation(bank[u][:, i * HD:(i + 1) * HD], bank[u][:, i * HD:(i + 1) * HD], ACT.Square,
                                                   scale=HD ** -0.5, accum_out=ssq[par][:, 4 * u + i:4 * u + i + 1])
                    ins.then_inc(unit_ev, 1)

                def transposed(g, par, q):
                    act.wait_ge(pe_tb, g * ROPE_UNITS + q + 1)
                    src = bank[6 + (par + q) % 2]
                    if q < 4:
                        copy(qt_of(qkv[par])[:, :, q], src[:].rearrange("p (r b s) -> p b r s", r=REP, b=TB)).then_inc(tb_ev, 1)
                    else:
                        copy(kt_of(qkv[par]), src[:]).then_inc(tb_ev, 1)

                x_high(0, 0, 0)

                def project(t, n, par, first, last):
                    g = h * NT + t
                    for u in range(ROPE_UNITS):
                        unit(g, par, u, first)
                        if u == 1 and not last:
                            if not first:
                                act.wait_ge(pe_v, g)
                            x_high(t + 1, n + par, 1 - par)
                        if u >= 1 and not first:
                            transposed(g - 1, 1 - par, u - 1)
                    act.wait_ge(pe_v, g + 1)
                    if not (isinstance(t, int) and t < 2):
                        act.wait_ge(proj_st[par], (h * (NT // 2) + n) * 16)
                        if par == 0:
                            act.wait_ge(pad_st, (h + 1) * 16)
                    act.sem_inc(gate["act"], 1)
                    copy(v_of(qkv[par]), bank[5][:]).then_inc(v_ev, 1)
                    if not first:
                        transposed(g - 1, 1 - par, 4)

                each_tile_2(act, project)
                for q in range(ROPE_UNITS):
                    transposed(h * NT + NT - 1, 1, q)
                act.drain().then_inc(phase, 1)
                act.wait_ge(phase, 8 * h + 8)
                act.sem_inc(gate["act"], 1)

                with act.Fori(0, 4) as i:
                    prep_high(r0 + 6 + i, lambda j: wo_dst(i, j, 0))
                with act.Fori(0, NPAGES // 16) as i:
                    prep(r0 + 10 + i, lambda j: kt_dst(i, j))

                def softmax(g, par, p):
                    b, hh = divmod(p, HK2)
                    act.wait_ge(ttr, g * NP + p + 1)
                    nc.scalar.activation(sm[p % 2][:], sm[p % 2][:], ACT.Exp, bias=mp[:, p:p + 1], scale=-1.0,
                                         accum_out=sumc[:, p:p + 1]).then_inc(ex, 1)
                    nc.scalar.activation(pz[:, b, hh, b * S:(b + 1) * S], sn[par][:, p, :], ACT.Exp, bias=mp[:, p:p + 1], scale=-1.0,
                                         accum_out=sumn[:, p:p + 1]).then_inc(exn, 1)

                def pt_out(g, p):
                    act.wait_ge(pe_t, g * NP + p + 1)
                    copy(pts[p % 2][:].rearrange("p k c -> p (k c)"), bank[2 + p % 2][:]).then_inc(pt_a, 1)

                def ot_high(g, b):
                    act.wait_ge(pe_ot, g * TB + b + 1)
                    copy(ots[:, 0, :, b * S:(b + 1) * S], bank[6][:].rearrange("p (h s) -> p h s", s=S)).then_inc(ot_hi, 1)

                def new_scores(g, par):
                    act.wait_ge(pe_sn, g + 1)
                    copy(sn[par][:].rearrange("p n s -> p (n s)"), bank[7][:]).then_inc(sn_ev, 1)

                new_scores(h * NT, 0)
                act.wait_ge(pz_zero, h + 1)
                act.wait_ge(sn_ev, h * NT + 1)
                softmax(h * NT, 0, 0)

                def attend(t, n, par, first, last):
                    g = h * NT + t
                    for p in range(NP):
                        pt_out(g, p)
                        if p < NP - 1:
                            softmax(g, par, p + 1)
                        elif not last:
                            act.wait_ge(sn_ev, g + 2)
                            softmax(g + 1, 1 - par, 0)
                        if p % 4 == 3:
                            act.wait_ge(pe_tn, g * TB + p // 4 + 1)
                            copy(pnt[:].rearrange("p h c -> p (h c)"), bank[6][:]).then_inc(tn_ev, 1)
                        if p % 4 == 2 and p >= 6:
                            ot_high(g, (p - 6) // 4)
                        if p == 2 and not first:
                            ot_high(g - 1, TB - 1)
                        if p == SN_AT + 1 and not last:
                            new_scores(g + 1, 1 - par)

                each_tile(act, attend)
                ot_high(h * NT + NT - 1, TB - 1)

            act.drain().then_inc(phase, 1)
            act.wait_ge(phase, 8 * NHALF + 4)
            for u in range(3 * NI):
                act.wait_ge(prep_tr[u % 4], R_FFN + u // 4 + 1)
                o, i = ffn_dst(u, 0)
                copy(o, i).then_inc(prep_hi, 1)

            def at_out(n):
                for k in range(KC):
                    act.wait_ge(pe_at, n * KC + k + 1)
                    copy(at4[:, 0, k, :], bank[6 + k % 2][:]).then_inc(at_hi, 1)

            def ht_high(n, c):
                m = P if c < NI - 1 else ILAST
                act.wait_ge(hmul, n * NI + c + 1)
                copy(ht[0:m, 0, c, :], sg[c % 2][0:m, :]).then_inc(ht_hi, 1)

            at_out(0)

            def group(n, last):
                for c in range(NI):
                    m = P if c < NI - 1 else ILAST
                    act.wait_ge(pe_gu, n * NI + c + 1)
                    if c >= 2:
                        act.wait_ge(hm, n * NI + c - 1)
                    nc.scalar.activation(sg[c % 2][0:m, :], bank[c % 2][0:m, :], ACT.Silu).then_inc(silu, 1)
                    if c:
                        ht_high(n, c - 1)
                ht_high(n, NI - 1)
                if not last:
                    at_out(n + 1)

            with act.Fori(0, NGRP - 1) as n:
                group(n, False)
            group(NGRP - 1, True)

        @block.tensor
        def _(pe):
            def prep(rnd, cols=4):
                for j in range(4):
                    pe.wait_ge(nat_full[j], (rnd + 1) * 16)
                    if not (isinstance(rnd, int) and rnd == 0):
                        pe.wait_ge(prep_ev[j], rnd)
                    for k in range(4):
                        ins = nc.tensor.transpose(bank[j][:, k * P:(k + 1) * P], nat[j][:, k * P:(k + 1) * P], ident[:])
                    ins.then_inc(prep_tr[j], 1)

            def prep_wo(rnd):
                for j in range(4):
                    pe.wait_ge(nat_full[j], (rnd + 1) * 16)
                    pe.wait_ge(prep_ev[j], rnd)
                for j in range(4):
                    for k in range(4):
                        ins = nc.tensor.transpose(bank[j][:, k * P:(k + 1) * P], nat[k][:, j * P:(j + 1) * P], ident[:])
                    ins.then_inc(prep_tr[j], 1)

            def product(out_, x2, w2, first, last):
                for n, (a, b) in enumerate(((0, 0), (0, 1), (1, 0))):
                    ins = nc.tensor.matmul(out_, x2[:, a], w2[:, b], start=first and n == 0, stop=last and n == 2)
                return ins

            def block_t(dst, src, done):
                for k in range(4):
                    ins = nc.tensor.transpose(dst[:, k * P:(k + 1) * P], src[:, k * P:(k + 1) * P], ident[:])
                ins.then_inc(done, 1)

            pe.wait_ge(c_ld, 16 * 10)
            prep(0)
            with pe.Fori(1, NID) as i:
                prep(i)
            prep(R_BASE)
            for k in range(KC):
                ins = nc.tensor.transpose(bank[7][:, k * NE:(k + 1) * NE], routn[:, k * P:(k + 1) * P], ident[0:NE, 0:NE])
            ins.then_inc(pe_r, 1)
            for j in range(4):
                pe.wait_ge(prep_ev[j], R_BASE + 1)
            pe.wait_ge(r_ev, 1)
            pe.wait_ge(x_ld, 16)
            block_t(bank[0], xn, pe_xt)

            def l0(t, cond, nxt, prev):
                if cond:
                    wid = nc.values_load_multi_w_load_instructions(
                        idb[0:1, bass.ds(t * TB, TB)], engines=[PE_], min_val=0, max_val=NID - 1,
                        skip_runtime_bounds_check_because="adapter numbers are below the adapters' count")[1]
                    pe.wait_ge(xtz_ev, t + 1)
                    for b in range(TB):
                        for k in range(KC):
                            ins = nc.tensor.matmul(bank[1][:], xtz[:, k, b * P:(b + 1) * P],
                                                   wt_all[:, bass.ds(wid[b], 1), k, :].rearrange("p a d -> p (a d)"),
                                                   start=(b == 0 and k == 0), stop=(b == TB - 1 and k == KC - 1))
                    ins.then_inc(pe_cond, 1)
                if nxt:
                    pe.wait_ge(x_ld, (t + 2) * 16)
                    block_t(bank[0], xn, pe_xt)
                if prev:
                    pe.wait_ge(rt, t * RT_OPS)
                    nc.tensor.transpose(bank[5][:, 0:P], mm[:].rearrange("p e r -> p (e r)"), ident[:]).then_inc(pe_mt, 1)
                    pe.wait_ge(mt_ev, t)
                    nc.tensor.matmul(bank[3][:], mt[:], lorab[:], start=False, stop=True).then_inc(pe_y0, 1)
                if cond:
                    pe.wait_ge(c_ev, t + 1)
                    block_t(bank[2], cn, pe_ct)
                if prev:
                    pe.wait_ge(x1_rdy, t)
                    if not isinstance(t, int) or t > 1:
                        pe.wait_ge(x1t_ev, t - 1)
                    block_t(bank[6], x1n, pe_x1t)
                if cond:
                    pe.wait_ge(ct_ev, t + 1)
                    for k in range(KC):
                        nc.tensor.matmul(bank[3][:], ct[:, k * P:(k + 1) * P], w_base[:, k, 0:D], start=(k == 0), stop=False)
                    for k in range(KC):
                        ins = nc.tensor.matmul(bank[4][:, 0:NE + P], ct[:, k * P:(k + 1) * P], w_base[:, k, D:],
                                               start=(k == 0), stop=(k == KC - 1))
                    ins.then_inc(pe_mid, 1)

            l0(0, True, True, False)
            l0(1, True, True, True)
            with pe.Fori(2, NT - 1) as t:
                l0(t, True, True, True)
            l0(NT - 1, True, False, True)
            l0(NT, False, False, True)

            with pe.Fori(0, NHALF) as h:
                pe.drain().then_inc(phase, 1)
                pe.wait_ge(phase, 8 * h + 4)
                pe.sem_inc(gate["pe"], 1)
                r0 = h * HALF_ROUNDS + R_HALF
                with pe.Fori(0, 4) as i:
                    prep(r0 + i)
                prep(r0 + 4)
                prep(r0 + 5)
                for k in range(4):
                    pe.wait_ge(prep_ev[k], r0 + 6)

                def unit(g, par, u, first):
                    if u == 0:
                        pe.wait_ge(xs_lo, g + 1)
                    if not first:
                        if u < ROPE_UNITS:
                            pe.wait_ge(unit_ev, g * ROPE_UNITS + (u + 1 - ROPE_UNITS))
                        else:
                            pe.wait_ge(v_ev, g)
                    if u == 0:
                        w = wkvs[:, :, :, 0:512]
                    elif u < ROPE_UNITS:
                        w = wqs[:, :, :, (u - 1) * 512:u * 512]
                    else:
                        w = wkvs[:, :, :, 512:1024]
                    for k in range(KC):
                        ins = product(bank[u][:], xs2[par][:, :, k, :], w[:, :, k, :], k == 0, k == KC - 1)
                    ins.then_inc(unit_mm if u < ROPE_UNITS else pe_v, 1)

                def transposed(g, par, q):
                    if q == 0:
                        pe.wait_ge(rope, (g + 1) * ROPE_OPS)
                    pe.wait_ge(tb_ev, g * ROPE_UNITS + (q + 1))
                    block_t(bank[6 + (par + q) % 2], qkf[par][:, (q + 1) % ROPE_UNITS].rearrange("p r d -> p (r d)"), pe_tb)

                def project(t, n, par, first, last):
                    g = h * NT + t
                    for u in range(ROPE_UNITS + 1):
                        unit(g, par, u, first)
                        if u and not first:
                            transposed(g - 1, 1 - par, u - 1)

                each_tile_2(pe, project)
                for q in range(ROPE_UNITS):
                    transposed(h * NT + NT - 1, 1, q)
                pe.drain().then_inc(phase, 1)
                pe.wait_ge(phase, 8 * h + 8)
                pe.sem_inc(gate["pe"], 1)

                with pe.Fori(0, 4) as i:
                    prep_wo(r0 + 6 + i)
                with pe.Fori(0, NPAGES // 16) as i:
                    prep(r0 + 10 + i)
                for k in range(4):
                    pe.wait_ge(prep_ev[k], r0 + HALF_ROUNDS)

                def new_scores(g, n, par, free, pairs):
                    if pairs[0] == 0:
                        pe.wait_ge(qkv_ld[par], (h * LOADS[par] + n + 1) * 16)
                    if pairs[0] == 0 and free:
                        pe.wait_ge(sn_ev, g)
                    for p in pairs:
                        b, hh = divmod(p, HK2)
                        ins = nc.tensor.matmul(bank[7][:, p * S:(p + 1) * S], qt_of(qkv[par])[:, b, hh].rearrange("p r s -> p (r s)"),
                                               kt_of(qkv[par])[:, hh * P + b * S:hh * P + (b + 1) * S], start=True, stop=True)
                    if pairs[-1] == NP - 1:
                        ins.then_inc(pe_sn, 1)

                def scores(t, par, p, free=True):
                    b, hh = divmod(p, HK2)
                    if hh == 0:
                        pe.wait_ge(kg_rdy, (h * NB + t * TB + b + 1))
                    if free:
                        pe.wait_ge(ttr, (h * NT + t) * NP + (p - 1))
                    nc.tensor.matmul(bank[p % 2][:], qt_of(qkv[par])[:, b, hh].rearrange("p r s -> p (r s)"),
                                     kg[b % 2][:, hh].rearrange("p g s -> p (g s)"), start=True, stop=True).then_inc(s_mm, 1)

                def values(t, p):
                    g = h * NT + t
                    b, hh = divmod(p, HK2)
                    pe.wait_ge(pt_a, g * NP + p + 1)
                    if hh == 0:
                        pe.wait_ge(v_ld[b % 2], (h * (NB // 2) + t * 2 + b // 2 + 1) * (16 * PG))
                        pe.wait_ge(on_rdy, g * TB + b + 1)
                    for c in range(KC):
                        nc.tensor.matmul(bank[4 + b % 2][:, hh * HD:(hh + 1) * HD], pts[p % 2][:, c, :],
                                         vg[b % 2][:, c, hh * HD:(hh + 1) * HD], start=(hh == 0 and c == 0), stop=False,
                                         skip_group_check=True)

                def values_new(t, par, b):
                    g = h * NT + t
                    pe.wait_ge(tn_ev, g * TB + b + 1)
                    for hh in range(HK2):
                        ins = nc.tensor.matmul(bank[4 + b % 2][:, hh * HD:(hh + 1) * HD], pnt[:, hh, :],
                                               v_of(qkv[par])[:, hh * HD:(hh + 1) * HD], start=False, stop=(hh == HK2 - 1),
                                               skip_group_check=True)
                    ins.then_inc(pe_o, 1)

                def out_t_(t, b):
                    pe.wait_ge(on_rdy, (h * NT + t) * TB + b + 3)
                    block_t(bank[6], on[:].rearrange("p h d -> p (h d)"), pe_ot)

                def out_product(g, part):
                    if part == 0:
                        pe.wait_ge(ot_ev, (g + 1) * TB)
                    for k in range(part * HQ2 // 3, (part + 1) * HQ2 // 3):
                        ins = product(bank[7][:], ots[:, :, k, :], wots[:, :, k, :], k == 0, k == HQ2 - 1)
                    if part == 2:
                        ins.then_inc(pe_op, 1)

                new_scores(h * NT, 0, 0, False, range(NP))
                scores(0, 0, 0, False)

                def attend(t, n, par, first, last):
                    g = h * NT + t
                    for p in range(NP):
                        if p < NP - 1:
                            scores(t, par, p + 1, not (first and p == 0))
                        elif not last:
                            scores(t + 1, 1 - par, 0)
                        pe.wait_ge(ex, g * NP + p + 1)
                        block_t(bank[2 + p % 2], sm[p % 2], pe_t)
                        if p % 4 == 3:
                            b = p // 4
                            pe.wait_ge(exn, g * NP + p + 1)
                            if not (first and b == 0):
                                pe.wait_ge(ot_ev, g * TB + b)
                            block_t(bank[6], pz[:, b].rearrange("p h c -> p (h c)"), pe_tn)
                        if p >= 1:
                            values(t, p - 1)
                        elif not first:
                            values(t - 1, NP - 1)
                        if p >= 4 and p % 4 == 0:
                            values_new(t, par, p // 4 - 1)
                        if p == 0 and not first:
                            values_new(t - 1, 1 - par, TB - 1)
                        if p % 4 == 2 and p >= 6:
                            out_t_(t, (p - 6) // 4)
                        if p == 2 and not first:
                            out_t_(t - 1, TB - 1)
                        if p in (3, 4, 5) and not first:
                            if p == 3:
                                pe.wait_ge(sn_ev, g + 1)
                            out_product(g - 1, p - 3)
                        if SN_AT - 4 <= p <= SN_AT and not last:
                            if p == SN_AT - 4 and not first:
                                pe.wait_ge(op_ev, g)
                            k = p - SN_AT + 4
                            new_scores(g + 1, n + par, 1 - par, True, range(NP)[k * NP // 5:(k + 1) * NP // 5])

                each_tile(pe, attend)
                values(NT - 1, NP - 1)
                values_new(NT - 1, 1, TB - 1)
                out_t_(NT - 1, TB - 1)
                for part in range(3):
                    out_product(h * NT + NT - 1, part)

            pe.drain().then_inc(phase, 1)
            pe.wait_ge(phase, 8 * NHALF + 4)
            for u in range(3 * NI):
                m, c = divmod(u, NI)
                n = P if c < NI - 1 else ILAST
                r, j = R_FFN + u // 4, u % 4
                pe.wait_ge(nat_full[j], (r + 1) * 16)
                pe.wait_ge(prep_ev[j], r)
                for k in range(4):
                    if m < 2:
                        ins = nc.tensor.transpose(bank[j][:, k * P:k * P + n], nat[j][0:n, k * P:(k + 1) * P], ident[0:n, 0:n])
                    else:
                        ins = nc.tensor.transpose(bank[j][0:n, k * P:(k + 1) * P], nat[j][:, k * P:k * P + n], ident[:])
                ins.then_inc(prep_tr[j], 1)

            def at_in(n):
                pe.wait_ge(an_ld, (n + 1) * 16)
                for k in range(KC):
                    if k >= 2:
                        pe.wait_ge(at_ev, n * KC + k - 1)
                    for i in range(GT):
                        ins = nc.tensor.transpose(bank[6 + k % 2][:, i * P:(i + 1) * P], an4[:, i, k * P:(k + 1) * P], ident[:])
                    ins.then_inc(pe_at, 1)

            at_in(0)
            for j in range(4):
                pe.wait_ge(prep_ev[j], R_FFN + (3 * NI - j + 3) // 4)

            def group(n, last):
                pe.wait_ge(at_ev, n * KC + KC)
                for c in range(NI):
                    m = P if c < NI - 1 else ILAST
                    if c >= 2:
                        pe.wait_ge(hmul, n * NI + c - 1)
                    for w in range(2):
                        for k in range(KC):
                            ins = product(bank[2 * w + c % 2][0:m, :], wgus[w][:, :, k, c * P:c * P + m], at4[:, :, k, :],
                                          k == 0, k == KC - 1)
                    ins.then_inc(pe_gu, 1)
                if not last:
                    at_in(n + 1)
                pe.wait_ge(hm, n * NI + NI)
                for i in range(GT):
                    pe.wait_ge(out_add, n * GT + i + 1)
                    for c in range(NI):
                        m = P if c < NI - 1 else ILAST
                        ins = product(bank[4 + i % 2][:], ht[0:m, :, c, i * P:(i + 1) * P], wds[0:m, :, c, :],
                                      c == 0, c == NI - 1)
                    ins.then_inc(pe_dn, 1)

            with pe.Fori(0, NGRP - 1) as n:
                group(n, False)
            group(NGRP - 1, True)

        @block.vector
        def _(dve):
            V = nc.vector

            def prep(rnd, dst):
                for j in (1, 3):
                    dve.wait_ge(prep_tr[j], rnd + 1)
                    dve.sem_inc(gate["dve"], 1)
                    o, i = dst(j)
                    V.tensor_copy(o, i).then_inc(prep_ev[j], 1)

            def prep_low(rnd, n, dst):
                for j in range(4):
                    dve.wait_ge(prep_hi, n * 4 + (j + 1))
                    dve.sem_inc(gate["dve"], 1)
                    (low, src), high = dst(j, 1), dst(j, 0)[0]
                    V.tensor_tensor(low, src, high.bitcast(F32), ALU.subtract).then_inc(prep_ev[j], 1)

            class Steps:

                def __init__(self, sem_, start):
                    self.sem, self.start, self.n = sem_, start, 0

                def done(self, ins):
                    ins.then_inc(self.sem, 1)
                    self.n += 1

                def wait(self):
                    dve.wait_ge(self.sem, self.start + self.n)

            dve.sem_inc(on_rdy, 2)
            dve.sem_inc(out_add, 2)
            V.memset(zero[:], 0.0).then_inc(zeroed, 1)
            V.memset(xtz[:], 0.0).then_inc(zeroed, 1)

            dve.wait_ge(c2_ld, 64)
            st = Steps(rtab, 0)
            invf, ptok = con2[:, 0:HD // 2], con2[:, HD // 2:HD // 2 + 1]
            tri = con2[:, HD // 2 + 1:HD // 2 + 1 + NE * NE].rearrange("p (a b) -> p a b", a=NE)
            st.done(V.tensor_copy(seqf[:], seqi[:]))
            st.wait()
            for b in range(TB):
                rows = slice(b * S, (b + 1) * S)
                st.done(V.tensor_copy(pos[rows, :], seqf[rows, :].rearrange("p (t b) -> p b t", b=TB)[:, b, :]))
            st.wait()
            st.done(V.tensor_scalar(pos[:], pos[:], ptok, None, ALU.add))
            st.wait()
            st.done(V.tensor_tensor(ang[:], pos[:].unsqueeze(2).to_broadcast([P, NT, HD // 2]),
                                    invf.unsqueeze(1).to_broadcast([P, NT, HD // 2]), ALU.mult))
            st.wait()
            st.done(V.tensor_scalar(cos_[:], ang[:], 1.0 / TWO_PI, MAGIC, ALU.mult, ALU.add))
            st.wait()
            st.done(V.tensor_scalar(sin_[:], cos_[:], -MAGIC, None, ALU.add))
            src = ang
            for part in (PI1, PI2, PI3):
                st.wait()
                st.done(V.scalar_tensor_tensor(out=red[:], in0=sin_[:], scalar=-part, in1=src[:], op0=ALU.mult, op1=ALU.add))
                src = red
            st.wait()
            st.done(V.tensor_scalar(red[:], red[:], 3.1415925, -3.1415925, ALU.min, ALU.max))
            assert st.n == RED_OPS
            prep(0, lambda j: cond_dst(0, j))
            half = HD // 2
            dve.wait_ge(trig, 2)
            st.done(V.tensor_tensor(ang[:], cos_[:], cos_[:], ALU.mult))
            st.wait()
            st.done(V.tensor_scalar(ang[:], ang[:], -2.0, 1.0, ALU.mult, ALU.add))
            st.done(V.tensor_scalar(qkw[:, 0, :], qkw[:, 0, :], -SCALE, None, ALU.mult))
            st.wait()
            for n in range(2):
                w1 = qkw[:, n, 0:half].unsqueeze(1).to_broadcast([P, NT, half])
                w2 = qkw[:, n, half:HD].unsqueeze(1).to_broadcast([P, NT, half])
                st.done(V.tensor_tensor(tabs[:, :, 2 * n, 0:half], ang[:], w1, ALU.mult))
                st.done(V.tensor_tensor(tabs[:, :, 2 * n, half:HD], ang[:], w2, ALU.mult))
                st.done(V.scalar_tensor_tensor(out=tabs[:, :, 2 * n + 1, 0:half], in0=sin_[:], scalar=-1.0, in1=w2, op0=ALU.mult, op1=ALU.mult))
                st.done(V.tensor_tensor(tabs[:, :, 2 * n + 1, half:HD], sin_[:], w1, ALU.mult))
            assert st.n == TAB_OPS

            with dve.Fori(1, NID) as i:
                prep(i, lambda j: cond_dst(i, j))
            prep(R_BASE, base_dst)
            dve.wait_ge(pe_r, 1)
            V.tensor_copy(w_base[:, :, D:D + NE], bank[7][:, 0:KC * NE].rearrange("p (k e) -> p k e", k=KC)).then_inc(r_ev, 1)

            def l0(t):
                st = Steps(rt, (t - 1) * RT_OPS)
                dve.wait_ge(pe_mid, t)
                st.done(V.tensor_reduce(nmx[:], bank[4][:, 0:NE], AX.X, ALU.max, negate=True))
                dve.wait_ge(rexp, t)
                st.done(V.reciprocal(rsm[:, 1:2], rsm[:, 0:1]))
                st.wait()
                st.done(V.tensor_scalar(prb[:], rex[:], rsm[:, 1:2], None, ALU.mult))
                st.wait()
                by_j = prb[:].unsqueeze(1).to_broadcast([P, NE, NE])
                by_e = prb[:].unsqueeze(2).to_broadcast([P, NE, NE])
                st.done(V.tensor_tensor(cmp_[:], by_j, by_e, ALU.is_gt))
                st.done(V.tensor_tensor(eq[:], by_j, by_e, ALU.is_equal))
                st.wait()
                st.done(V.tensor_tensor(eq[:], eq[:], tri, ALU.mult))
                st.wait()
                st.done(V.tensor_tensor(cmp_[:], cmp_[:], eq[:], ALU.add))
                st.wait()
                st.done(V.tensor_reduce(rank[:], cmp_[:], AX.X, ALU.add))
                st.wait()
                st.done(V.scalar_tensor_tensor(out=sel[:], in0=rank[:], scalar=2.0, in1=prb[:], op0=ALU.is_lt, op1=ALU.mult))
                st.wait()
                st.done(V.tensor_reduce(rsm[:, 2:3], sel[:], AX.X, ALU.add))
                st.wait()
                st.done(V.reciprocal(rsm[:, 3:4], rsm[:, 2:3]))
                st.wait()
                st.done(V.tensor_scalar(wgt[:], sel[:], rsm[:, 3:4], 2.0, ALU.mult, ALU.mult))
                st.wait()
                st.done(V.tensor_tensor(mm[:], bank[4][:, NE:NE + P].rearrange("p (e r) -> p e r", e=NE),
                                        wgt[:].unsqueeze(2).to_broadcast([P, NE, RANK]), ALU.mult))
                assert st.n == RT_OPS
                dve.wait_ge(pe_y0, t)
                dve.wait_ge(xres_ld, t * 16)
                if not isinstance(t, int) or t > 1:
                    dve.wait_ge(x1_st, (t - 1) * 16)
                    dve.wait_ge(pe_x1t, t - 1)
                V.tensor_tensor(x1n[:], bank[3][:], xres[:], ALU.add).then_inc(x1_rdy, 1)

            l0(1)
            with dve.Fori(2, NT + 1) as t:
                l0(t)

            with dve.Fori(0, NHALF) as h:
                dve.drain().then_inc(phase, 1)
                dve.wait_ge(phase, 8 * h + 4)
                dve.sem_inc(gate["dve"], 1)
                r0 = h * HALF_ROUNDS + R_HALF
                with dve.Fori(0, 4) as i:
                    prep_low(r0 + i, h * SPLITS + i, lambda j, part: wq_dst(i, j, part))
                prep_low(r0 + 4, h * SPLITS + 4, lambda j, part: kv_dst(0, j, part))
                prep_low(r0 + 5, h * SPLITS + 5, lambda j, part: kv_dst(1, j, part))

                def rotate(g, n, par, u):
                    st = Steps(rope, g * ROPE_OPS + 4 * u)
                    v = 2 if u == 0 else 0
                    c = tab[par][:, v, :].unsqueeze(1).to_broadcast([P, REP, HD])
                    s1 = tab[par][:, v + 1, 0:half].unsqueeze(1).to_broadcast([P, REP, half])
                    s2 = tab[par][:, v + 1, half:HD].unsqueeze(1).to_broadcast([P, REP, half])
                    dve.wait_ge(unit_cp, g * ROPE_UNITS + u + 1)
                    if u == 0:
                        dve.wait_ge(tab_ld[par], (h * LOADS[par] + n + 1) * 16)
                    else:
                        st.wait()
                    st.done(V.tensor_tensor(qkf[par][:, u], qn[:, u], c, ALU.mult))
                    st.done(V.tensor_tensor(qb[:, :, 0:half], qn[:, u, :, half:HD], s1, ALU.mult))
                    st.done(V.tensor_tensor(qb[:, :, half:HD], qn[:, u, :, 0:half], s2, ALU.mult))
                    st.wait()
                    st.done(V.tensor_tensor(qkf[par][:, u], qkf[par][:, u], qb[:], ALU.add))

                def rsqrt(g, par):
                    st = Steps(rope, g * ROPE_OPS + 4 * ROPE_UNITS)
                    dve.wait_ge(unit_ev, g * ROPE_UNITS + ROPE_UNITS)
                    st.wait()
                    st.done(V.tensor_scalar(xs[:], ssq[par][:], EPS, None, ALU.add))
                    st.wait()
                    st.done(V.tensor_scalar(yi[:], xs[:].bitcast(I32), 1, None, ALU.logical_shift_right))
                    st.done(V.tensor_scalar(xh[:], xs[:], -0.5, None, ALU.mult))
                    st.wait()
                    st.done(V.tensor_scalar(yy[:].bitcast(I32), yi[:], -1.0, RSQRT_BITS, ALU.mult, ALU.add))
                    for _ in range(3):
                        st.wait()
                        st.done(V.tensor_tensor(y2[:], yy[:], yy[:], ALU.mult))
                        st.wait()
                        st.done(V.tensor_tensor(y3[:], y2[:], xh[:], ALU.mult))
                        st.wait()
                        st.done(V.scalar_tensor_tensor(out=yy[:], in0=y3[:], scalar=1.5, in1=yy[:], op0=ALU.add, op1=ALU.mult))

                def norm(g, par, part):
                    st = Steps(rope, g * ROPE_OPS + 4 * ROPE_UNITS + 13 + part)
                    if part == 0:
                        st.wait()
                    u0, u1 = (0, 2) if part == 0 else (2, ROPE_UNITS)
                    v = qkf[par][:, u0:u1].rearrange("p u r d -> p (u r) d")
                    st.done(V.tensor_tensor(v, v, yy[:, 4 * u0:4 * u1].unsqueeze(2).to_broadcast([P, 4 * (u1 - u0), HD]), ALU.mult))

                def x_low(g, par):
                    dve.wait_ge(xs_hi, g + 1)
                    V.tensor_tensor(xs2[par][:, 1], xt[par][:], xs2[par][:, 0].bitcast(F32), ALU.subtract).then_inc(xs_lo, 1)

                x_low(h * NT, 0)

                def project(t, n, par, first, last):
                    g = h * NT + t
                    for u in range(ROPE_UNITS):
                        rotate(g, n, par, u)
                        if u == 1 and not last:
                            x_low(g + 1, 1 - par)
                    rsqrt(g, par)
                    norm(g, par, 0)
                    norm(g, par, 1)

                each_tile_2(dve, project)
                dve.drain().then_inc(phase, 1)
                dve.wait_ge(phase, 8 * h + 8)
                dve.sem_inc(gate["dve"], 1)

                V.memset(pz[:], 0.0).then_inc(pz_zero, 1)
                with dve.Fori(0, 4) as i:
                    prep_low(r0 + 6 + i, h * SPLITS + 6 + i, lambda j, part: wo_dst(i, j, part))
                with dve.Fori(0, NPAGES // 16) as i:
                    prep(r0 + 10 + i, lambda j: kt_dst(i, j))
                for j in range(4):
                    dve.wait_ge(prep_ev[j], r0 + HALF_ROUNDS)
                dve.sem_inc(gate["dve"], 1)

                def gather(n, par, part):
                    pg = regs(DVE_, pages[0:1, bass.ds(n * PG + part * 8, 8)])
                    for i in range(8):
                        ins = V.tensor_copy(kg[par][:, :, part * 8 + i, :],
                                            ktall[:, bass.ds(pg[i], 1)].rearrange("p a h s -> p (a h) s"))
                    if part:
                        ins.then_inc(kg_rdy, 1)

                def key_mask(t, b, free):
                    g = h * NT + t
                    if free:
                        dve.wait_ge(ttr, g * NP + b * HK2)
                        dve.sem_inc(gate["dve"], 1)
                    V.tensor_scalar(mask[:], keyidx[:], seqf[:, bass.ds(t * TB + b, 1)], BIG, ALU.is_ge, ALU.mult).then_inc(mk, 1)

                def least(t, p, free=True):
                    g = h * NT + t
                    b = p // HK2
                    if p % HK2 == 0:
                        key_mask(t, b, free)
                        dve.wait_ge(mk, g * TB + b + 1)
                        dve.sem_inc(gate["dve"], 1)
                    dve.wait_ge(s_mm, g * NP + p + 1)
                    dve.sem_inc(gate["dve"], 1)
                    V.tensor_tensor_reduce(out=sm[p % 2][:], in0=bank[p % 2][:], in1=mask[:], scale=1.0, scalar=mnew[:, p:p + 1],
                                           op0=ALU.add, op1=ALU.min, accum_out=mp[:, p:p + 1]).then_inc(ttr, 1)

                def out_norm(g, b):
                    c = slice(b * HK2, (b + 1) * HK2)
                    dve.wait_ge(pe_o, g * TB + b + 1)
                    V.tensor_tensor(rsum[:, c], sumc[:, c], sumn[:, c], ALU.add).then_inc(osum, 1)
                    dve.wait_ge(osum, (g * TB + b) * 2 + 1)
                    V.reciprocal(rinv[:, c], rsum[:, c]).then_inc(osum, 1)
                    dve.wait_ge(osum, (g * TB + b) * 2 + 2)
                    V.tensor_tensor(on[:], bank[4 + b % 2][:].rearrange("p (h d) -> p h d", h=HK2),
                                    rinv[:, c].unsqueeze(2).to_broadcast([P, HK2, HD]), ALU.mult).then_inc(on_rdy, 1)

                def ot_low(g, b):
                    dve.wait_ge(ot_hi, g * TB + b + 1)
                    V.tensor_tensor(ots[:, 1, :, b * S:(b + 1) * S], bank[6][:].rearrange("p (h s) -> p h s", s=S),
                                    ots[:, 0, :, b * S:(b + 1) * S].bitcast(F32), ALU.subtract).then_inc(ot_ev, 1)

                def new_least(g, par, free):
                    if free:
                        dve.wait_ge(ttr, g * NP)
                    dve.wait_ge(sn_ev, g + 1)
                    V.tensor_reduce(mnew[:], sn[par][:], AX.X, ALU.min).then_inc(mn, 1)

                def sum_add(g):
                    dve.wait_ge(pe_op, g + 1)
                    dve.wait_ge(a_ld, (g + 1) * 16)
                    V.tensor_tensor(an[:], bank[7][:], an[:], ALU.add).then_inc(op_ev, 1)

                gather(0, 0, 0)
                gather(0, 0, 1)
                gather(1, 1, 0)
                new_least(h * NT, 0, False)
                dve.wait_ge(mn, h * NT + 1)
                dve.sem_inc(gate["dve"], 1)
                least(0, 0, False)

                def attend(t, n, par, first, last):
                    g = h * NT + t
                    for p in range(NP):
                        b = p // HK2
                        if p < NP - 1:
                            least(t, p + 1)
                        elif not last:
                            dve.wait_ge(mn, g + 2)
                            dve.sem_inc(gate["dve"], 1)
                            least(t + 1, 0)
                        if p % 4 == 3 and not (last and b >= TB - 2):
                            gather(t * TB + b + 2, b % 2, 0)
                        if p % 4 == 0 and not (last and b == TB - 1):
                            gather(t * TB + b + 1, (b + 1) % 2, 1)
                        if p % 4 == 1 and p > 1:
                            out_norm(g, p // 4 - 1)
                        if p == 1 and not first:
                            out_norm(g - 1, TB - 1)
                        if p % 4 == 2 and p >= 6:
                            ot_low(g, (p - 6) // 4)
                        if p == 2 and not first:
                            ot_low(g - 1, TB - 1)
                        if p == 7 and not first:
                            sum_add(g - 1)
                        if p == NP - 2 and not last:
                            new_least(g + 1, 1 - par, True)

                each_tile(dve, attend)
                out_norm(h * NT + NT - 1, TB - 1)
                ot_low(h * NT + NT - 1, TB - 1)
                sum_add(h * NT + NT - 1)

            dve.drain().then_inc(phase, 1)
            dve.wait_ge(phase, 8 * NHALF + 4)
            for u in range(3 * NI):
                dve.wait_ge(prep_hi, NHALF * SPLITS * 4 + u + 1)
                (low, src), high = ffn_dst(u, 1), ffn_dst(u, 0)[0]
                V.tensor_tensor(low, src, high.bitcast(F32), ALU.subtract).then_inc(prep_ev[u % 4], 1)

            def at_low(n):
                for k in range(KC):
                    dve.wait_ge(at_hi, n * KC + k + 1)
                    V.tensor_tensor(at4[:, 1, k, :], bank[6 + k % 2][:], at4[:, 0, k, :].bitcast(F32), ALU.subtract).then_inc(at_ev, 1)

            def ht_low(n, c):
                m = P if c < NI - 1 else ILAST
                dve.wait_ge(ht_hi, n * NI + c + 1)
                V.tensor_tensor(ht[0:m, 1, c, :], sg[c % 2][0:m, :], ht[0:m, 0, c, :].bitcast(F32), ALU.subtract).then_inc(hm, 1)

            at_low(0)

            def group(n, last):
                for c in range(NI):
                    m = P if c < NI - 1 else ILAST
                    dve.wait_ge(silu, n * NI + c + 1)
                    V.tensor_tensor(sg[c % 2][0:m, :], bank[2 + c % 2][0:m, :], sg[c % 2][0:m, :], ALU.mult).then_inc(hmul, 1)
                    if c:
                        ht_low(n, c - 1)
                ht_low(n, NI - 1)
                if not last:
                    at_low(n + 1)
                for i in range(GT):
                    dve.wait_ge(pe_dn, n * GT + i + 1)
                    dve.wait_ge(x1b_ld[i % 2], (n * 2 + i // 2 + 1) * 16)
                    if not isinstance(n, int) or i >= 2:
                        dve.wait_ge(o_st[i % 2], (n * 2 + i // 2) * 16)
                    V.tensor_tensor(ob[i % 2][:], bank[4 + i % 2][:], x1b[i % 2][:], ALU.add).then_inc(out_add, 1)

            group(0, False)
            with dve.Fori(1, NGRP - 1) as n:
                group(n, False)
            group(NGRP - 1, True)


_NAMES = ["x", "itok_B_3_7", "itok_Bx16_0_63", "itok_B_207_1644", "L0_cond_weight", "L0_ffn_base_W", "L0_ffn_router_W",
          "L0_ffn_lora_A", "L0_ffn_lora_B", "L1_cond_Wq", "L1_cond_Wk", "L1_cond_Wv", "L1_cond_Wo", "L1_cond_q_norm_w",
          "L1_cond_k_norm_w", "L1_cond_k_cache", "L1_cond_v_cache", "L1_ffn_codebook"]


def kernel(**inputs):
    import numpy as np
    import concourse.bacc as bacc
    from concourse.bass_utils import run_bass_kernel_spmd

    nc = bacc.Bacc("TRN2", target_bir_lowering=False, num_devices=1, dynamic_dma_scratch_size=4096)
    arrays = {f"in_{n}": np.ascontiguousarray(inputs[n]) for n in _NAMES}
    arrays["idx_all"] = np.concatenate([np.asarray(inputs[f"L1_ffn_idx_{n}"]).reshape(-1) for n in ("gate", "up", "down")]).reshape(P, -1)
    half = HD // 2
    arrays["con_a"] = np.concatenate([np.eye(P), np.tile(np.arange(L), (P, 1))], 1).astype(np.float32)
    invf = (np.float32(1.0) / np.float32(10000.0) ** (np.arange(0, HD, 2, dtype=np.float32) / np.float32(HD))).astype(np.float32)
    tri = (np.arange(NE)[:, None] > np.arange(NE)[None, :]).astype(np.float32).reshape(-1)
    arrays["con_b"] = np.concatenate([np.tile(invf, (P, 1)), (np.arange(P) % S)[:, None], np.tile(tri, (P, 1))], 1).astype(np.float32)
    args = [nc.dram_tensor(n, a.shape, mybir.dt.from_np(a.dtype), kind="ExternalInput").ap() for n, a in arrays.items()]
    out = nc.dram_tensor("out", (64, S, D), F32, kind="ExternalOutput").ap()
    adaln_ffn_kernel(nc, *args, out)
    r = run_bass_kernel_spmd(nc, [arrays], core_ids=[0])
    return r.results[0]["out"]
```

```python
from contextlib import ExitStack

import concourse.bass as bass
from concourse import mybir

F32 = mybir.dt.float32
F32R = mybir.dt.float32r
I32 = mybir.dt.int32
ALU = mybir.AluOpType
ACT = mybir.ActivationFunctionType
AX = mybir.AxisListType
PE_, DVE_, SP_ = mybir.EngineType.PE, mybir.EngineType.DVE, mybir.EngineType.SP

P = 128
S = 32
TB = P // S
D = 512
KC = D // P
NE, RANK = 8, 16
NHALF = 2
PG = 16
PSZ = 32
L = PG * PSZ
HD = 128
REP = 4
HK2 = 4
HQ2 = REP * HK2
QKV = (HQ2 + 2 * HK2) * P
NP = TB * HK2
BIG = 1e30
SCALE = HD ** -0.5
EPS = 1e-6
MAGIC = 12582912.0
TWO_PI = 6.283185307179586
PI1 = 6.28125
PI2 = 0.0019350051879882812
PI3 = TWO_PI - PI1 - PI2
RSQRT_BITS = 1597463007.0
ROPE_UNITS = 5
ROPE_OPS = 4 * ROPE_UNITS + 13 + 2
CHUNK = 43
RED_OPS = 1 + TB + 1 + 1 + 2 + 3 + 1
TAB_OPS = RED_OPS + 3
RT_OPS = 13
SN_AT = 12


def adaln_ffn_kernel(nc, x, ids, table, seqlens, w_cond, base_w, router_w, lora_a, lora_b,
                     wq, wk, wv, wo, qnw, knw, k_cache, v_cache, codebook, idx_all,
                     con_a, con_b, out):
    NB = x.shape[0]
    NT = NB * S // P
    NPAGES = k_cache.shape[0]
    NID = w_cond.shape[0]
    NG = idx_all.shape[1]
    CW = codebook.shape[1]
    I = NG * P * CW // (3 * D)
    NI = -(-I // P)
    ILAST = I - (NI - 1) * P
    ROUNDS = NG // CHUNK // 2
    assert NB * S == NT * P and NG % (2 * CHUNK) == 0
    GT = 4
    NGRP = NT // GT

    x_t = x.rearrange("(t b) s d -> t (b s) d", b=TB)
    out_t = out.rearrange("(t b) s d -> t (b s) d", b=TB)
    x1_d = nc.dram_tensor("x1_d", (NT, P, D), F32).ap()
    x1t_d = nc.dram_tensor("x1t_d", (NT + 1, P, D), F32).ap()
    tab_d = nc.dram_tensor("tab_d", (NT + 1, P, 4 * HD), F32).ap()
    qkv_d = nc.dram_tensor("qkv_d", (NT + 1, P, QKV), F32).ap()
    a_d = nc.dram_tensor("a_d", (NT, P, D), F32).ap()
    w_d = nc.dram_tensor("w_d", (P, NG * CW), F32).ap()

    with ExitStack() as ctx:
        def sem(name):
            return ctx.enter_context(nc.semaphore(name))

        bank = [ctx.enter_context(nc.psum_tensor(f"bank{i}", [P, 512], F32)) for i in range(8)]

        base = (nc.sbuf_base + 63) // 64 * 64
        at = [base]

        def sb(name, shape, dt=F32):
            t = nc.alloc_sbuf_tensor_at(name, shape, dt, offset=at[0])
            n = 4
            for s in shape[1:]:
                n *= s
            at[0] += (n + 31) // 32 * 32
            return t

        ident = sb("ident", [P, P])
        keyidx = sb("keyidx", [P, L])
        pages = sb("pages", [1, NB * PG], I32)
        seqf = sb("seqf", [P, NB])
        gidx = [sb(f"gidx{u}", [P, CHUNK], I32) for u in range(2)]
        stage = [sb(f"stage{u}", [P, CHUNK, CW]) for u in range(2)]
        nat = [sb(f"nat{j}", [P, 512]) for j in range(4)]
        nat_at = at[0] - 4 * 2048
        phase_at = at[0]

        wt_all = sb("wt_all", [P, 2, NID, KC, D], F32R)
        w_base = sb("w_base", [P, 2, KC, D + NE + NE * RANK], F32R)
        lorab = sb("lorab", [P, D])
        routn = sb("routn", [NE, D])
        idb = sb("idb", [1, NB], I32)
        con2 = sb("con2", [P, con_b.shape[1]])
        seqi = sb("seqi", [P, NB], I32)
        qkw = sb("qkw", [P, 2, HD])
        pos = sb("pos", [P, NT])
        sin_ = sb("sin_", [P, NT, HD // 2])
        cos_ = sb("cos_", [P, NT, HD // 2])
        tab1 = sb("tab1", [P, 4, HD])
        xn = sb("xn", [P, D])
        xtz = sb("xtz", [P, 2, KC, 5 * P], F32R)
        low_at = at[0] - KC * 5 * P * 4
        assert 2 * NT * (HD // 2) <= KC * 5 * P
        ang = nc.alloc_sbuf_tensor_at("ang", [P, NT, HD // 2], F32, offset=low_at)
        red = nc.alloc_sbuf_tensor_at("red", [P, NT, HD // 2], F32, offset=low_at + NT * (HD // 2) * 4)
        cn = sb("cn", [P, D])
        lora_n = cn
        ct = sb("ct", [P, 2, D], F32R)
        mm = sb("mm", [P, NE, RANK])
        mt = sb("mt", [P, P])
        xres = sb("xres", [P, D])
        x1n = sb("x1n", [P, D])
        x1t = sb("x1t", [P, D])
        zero = x1t
        nmx = sb("nmx", [P, 1])
        rex = sb("rex", [P, NE])
        rsm = sb("rsm", [P, 4])
        prb = sb("prb", [P, NE])
        cmp_ = sb("cmp_", [P, NE, NE])
        eq = sb("eq", [P, NE, NE])
        rank = sb("rank", [P, NE])
        sel = sb("sel", [P, NE])
        wgt = sb("wgt", [P, NE])
        end0 = at[0]

        at[0] = phase_at
        qkv = [sb(f"qkv{i}", [P, QKV]) for i in range(2)]
        heads_at = at[0]
        wqs = sb("wqs", [P, 2, KC, HQ2 * HD], F32R)
        wkvs = sb("wkvs", [P, 2, KC, 2 * HK2 * HD], F32R)
        xt = [sb(f"xt{i}", [P, KC, P]) for i in range(2)]
        xs2 = [sb(f"xs2_{i}", [P, 2, KC, P], F32R) for i in range(2)]
        tab = [sb(f"tab{i}", [P, 4, HD]) for i in range(2)]
        qn = sb("qn", [P, ROPE_UNITS, REP, HD])
        qb = sb("qb", [P, REP, HD])
        qkf = [sb(f"qkf{i}", [P, ROPE_UNITS, REP, HD]) for i in range(2)]
        ssq = [sb(f"ssq{i}", [P, 20]) for i in range(2)]
        xs = sb("xs", [P, 20])
        xh = sb("xh", [P, 20])
        yy = sb("yy", [P, 20])
        y2 = sb("y2", [P, 20])
        y3 = sb("y3", [P, 20])
        yi = sb("yi", [P, 20], I32)
        raw = sb("raw", [P, 4, 4, 512])
        raw_at = at[0] - 4 * 4 * 2048
        end1 = at[0]

        at[0] = heads_at
        ots = sb("ots", [P, 2, HQ2, P], F32R)
        wots = sb("wots", [P, 2, HQ2, D], F32R)
        ktall = sb("ktall", [P, NPAGES, HK2, PSZ])
        assert at[0] <= raw_at
        vg = [sb(f"vg{i}", [P, KC, HK2 * HD]) for i in range(2)]
        kg = [sb(f"kg{i}", [P, HK2, PG, PSZ]) for i in range(2)]
        sm = [sb(f"sm{i}", [P, L]) for i in range(2)]
        pts = [sb(f"pts{i}", [P, KC, P]) for i in range(2)]
        pz = sb("pz", [P, TB, HK2, P])
        pnt = sb("pnt", [P, HK2, P])
        sn = [sb(f"sn{i}", [P, NP, S]) for i in range(2)]
        on = sb("on", [P, HK2, HD])
        an = sb("an", [P, D])
        mask = [sb(f"mask{i}", [P, L]) for i in range(2)]
        mp = sb("mp", [P, NP])
        mnew = sb("mnew", [P, NP])
        sumc = sb("sumc", [P, NP])
        sumn = sb("sumn", [P, NP])
        rsum = sb("rsum", [P, NP])
        rinv = sb("rinv", [P, NP])
        end1 = max(end1, at[0])

        at[0] = phase_at
        wgus = [sb(f"w{n}s", [P, 2, KC, I], F32R) for n in "gu"]
        wds = sb("wds", [P, 2, NI, D], F32R)
        an4 = sb("an4", [P, GT, D])
        at4 = sb("at4", [P, 2, KC, GT * P], F32R)
        ht = sb("ht", [P, 2, NI, GT * P], F32R)
        sg = [sb(f"sg{i}", [P, GT * P]) for i in range(2)]
        end2 = at[0]
        at[0] = nat_at
        x1b = [sb(f"x1b{i}", [P, D]) for i in range(2)]
        ob = [sb(f"ob{i}", [P, D]) for i in range(2)]
        assert at[0] == phase_at
        assert max(end0, end1, end2) <= 229344, (end0, end1, end2)

        c_ld = sem("c_ld")
        c2_ld = sem("c2_ld")
        nat_full = [sem(f"nat_full{j}") for j in range(4)]
        raw_full = sem("raw_full")
        prep_tr = [sem(f"prep_tr{j}") for j in range(4)]
        prep_ev = [sem(f"prep_ev{j}") for j in range(4)]
        phase = sem("phase")
        gate = {e: sem(f"gate_{e}") for e in ("pool", "act", "dve", "sp", "pe")}
        rtab = sem("rtab")
        trig = sem("trig")
        tab_st = sem("tab_st")
        zeroed = sem("zeroed")
        x_ld = sem("x_ld")
        xres_ld = sem("xres_ld")
        pe_xt, xtz_ev, xtz_lo = sem("pe_xt"), sem("xtz_ev"), sem("xtz_lo")
        pe_cond, c_ev = sem("pe_cond"), sem("c_ev")
        pe_ct, ct_ev, ct_lo = sem("pe_ct"), sem("ct_ev"), sem("ct_lo")
        pe_mid, rt = sem("pe_mid"), sem("rt")
        rexp = sem("rexp")
        pe_mt, mt_ev = sem("pe_mt"), sem("mt_ev")
        pe_y0, x1_rdy = sem("pe_y0"), sem("x1_rdy")
        pe_x1t, x1t_ev = sem("pe_x1t"), sem("x1t_ev")
        x1_st, x1t_st = sem("x1_st"), sem("x1t_st")
        pe_r, r_ev = sem("pe_r"), sem("r_ev")
        pz_zero = sem("pz_zero")
        xt_ld = [sem(f"xt_ld{i}") for i in range(2)]
        tab_ld = [sem(f"tab_ld{i}") for i in range(2)]
        xs_hi, xs_lo = sem("xs_hi"), sem("xs_lo")
        prep_hi = sem("prep_hi")
        unit_mm, unit_cp, unit_ev = sem("unit_mm"), sem("unit_cp"), sem("unit_ev")
        rope = sem("rope")
        pe_v, v_ev = sem("pe_v"), sem("v_ev")
        pe_tb, tb_ev = sem("pe_tb"), sem("tb_ev")
        proj_st = [sem(f"proj_st{i}") for i in range(2)]
        pad_st = sem("pad_st")
        qkv_ld = [sem(f"qkv_ld{i}") for i in range(2)]
        v_ld = [sem(f"v_ld{i}") for i in range(2)]
        a_ld, a_st = sem("a_ld"), sem("a_st")
        pe_sn, sn_ev, mn = sem("pe_sn"), sem("sn_ev"), sem("mn")
        kg_rdy, mk = sem("kg_rdy"), sem("mk")
        s_mm, ttr = sem("s_mm"), sem("ttr")
        ex, exn = sem("ex"), sem("exn")
        pe_t, pt_a = sem("pe_t"), sem("pt_a")
        pe_tn, tn_ev = sem("pe_tn"), sem("tn_ev")
        pe_o, osum, on_rdy = sem("pe_o"), sem("osum"), sem("on_rdy")
        pe_ot, ot_hi, ot_ev = sem("pe_ot"), sem("ot_hi"), sem("ot_ev")
        pe_op, op_ev = sem("pe_op"), sem("op_ev")
        gi_ld = [sem(f"gi_ld{u}") for u in range(2)]
        gat = [sem(f"gat{u}") for u in range(2)]
        g_st = [sem(f"g_st{u}") for u in range(2)]
        an_ld, pe_at, at_hi, at_ev = sem("an_ld"), sem("pe_at"), sem("at_hi"), sem("at_ev")
        pe_gu, silu, hmul, ht_hi, hm = sem("pe_gu"), sem("silu"), sem("hmul"), sem("ht_hi"), sem("hm")
        pe_dn, out_add = sem("pe_dn"), sem("out_add")
        x1b_ld = [sem(f"x1b_ld{i}") for i in range(2)]
        o_st = [sem(f"o_st{i}") for i in range(2)]

        R_BASE = NID
        R_HALF = NID + 1
        HALF_ROUNDS = 4 + 1 + 1 + 4 + NPAGES // 16
        HALF_LOADS = 4 + 1 + 1 + NPAGES // 16
        R_FFN = R_HALF + NHALF * HALF_ROUNDS

        def regs(engine, ap):
            return nc.values_load_multi_w_load_instructions(
                ap, engines=[engine], min_val=0, max_val=63,
                skip_runtime_bounds_check_because="they index a table of 64 pages or fewer")[1]

        def cols(j):
            return bank[j][:].rearrange("p (k c) -> p k c", k=4)

        def cond_dst(i, j, part):
            return wt_all[:, part, bass.ds(i, 1), :, j * P:(j + 1) * P].rearrange("p a k c -> p (a k) c"), cols(j)

        def base_dst(j, part):
            return w_base[:, part, :, j * P:(j + 1) * P], cols(j)

        def wq_dst(i, j, part):
            return wqs[:, part, :, bass.ds(i * 512 + j * P, P)], cols(j)

        def kv_dst(v, j, part):
            return wkvs[:, part, :, v * 512 + j * P:v * 512 + (j + 1) * P], cols(j)

        def wo_dst(i, j, part):
            return wots[:, part, bass.ds(i * 4 + j, 1), :].rearrange("p a d -> p (a d)"), bank[j][:]

        def qt_of(buf):
            return buf[:, 0:HQ2 * P].rearrange("p (b h r s) -> p b h r s", b=TB, h=HK2, r=REP)

        def kt_of(buf):
            return buf[:, HQ2 * P:(HQ2 + HK2) * P]

        def v_of(buf):
            return buf[:, (HQ2 + HK2) * P:QKV]

        def each_tile(engine, tile):
            tile(0, 0, 0, True, False)
            with engine.Fori(0, NT // 2 - 1) as i:
                tile(i * 2 + 1, i, 1, False, False)
                tile(i * 2 + 2, i + 1, 0, False, False)
            tile(NT - 1, NT // 2 - 1, 1, False, True)

        def each_tile_2(engine, tile):
            tile(0, 0, 0, True, False)
            tile(1, 0, 1, False, False)
            with engine.Fori(1, NT // 2 - 1) as i:
                tile(i * 2, i, 0, False, False)
                tile(i * 2 + 1, i, 1, False, False)
            tile(NT - 2, NT // 2 - 1, 0, False, False)
            tile(NT - 1, NT // 2 - 1, 1, False, True)

        SPLITS = 10
        LOADS = (NT // 2 + 1, NT // 2)

        def kt_dst(i, j):
            return (ktall[:, bass.ds(i * 16 + j * 4, 4)].rearrange("p g h s -> p h g s"),
                    bank[j][:].rearrange("p (h g s) -> p h g s", h=HK2, g=4))

        def ffn_dst(u, part):
            m, c = divmod(u, NI)
            n = P if c < NI - 1 else ILAST
            if m < 2:
                return wgus[m][:, part, :, c * P:c * P + n], cols(u % 4)[:, :, 0:n]
            return wds[0:n, part, c, :], bank[u % 4][0:n, :]

        def xtz_diag(b, part):
            return xtz[:, part, :, b * (P + S):b * (P + S) + S]

        block = ctx.enter_context(nc.Block())

        @block.sync
        def _(sp):
            def nat_round(rnd, srcs):
                for j, (dst, src) in enumerate(srcs):
                    if not (isinstance(rnd, int) and rnd == 0):
                        sp.wait_ge(prep_tr[j], rnd)
                    sp.dma_start(dst, src).then_inc(nat_full[j], 16)

            sp.dma_start(ident[:], con_a[:, 0:P]).then_inc(c_ld, 16)
            nat_round(0, [(nat[j][:], w_cond[0, j * P:(j + 1) * P, :]) for j in range(4)])
            sp.dma_start(keyidx[:], con_a[:, P:]).then_inc(c_ld, 16)
            sp.dma_start(con2[:], con_b).then_inc(c2_ld, 16)
            sp.dma_start(seqi[:], seqlens.partition_broadcast(P)).then_inc(c2_ld, 16)
            sp.dma_start(qkw[:, 0, :], qnw.partition_broadcast(P)).then_inc(c2_ld, 16)
            sp.dma_start(qkw[:, 1, :], knw.partition_broadcast(P)).then_inc(c2_ld, 16)
            sp.dma_start(pages[:], table.rearrange("(a b) c -> a (b c)", a=1)).then_inc(c_ld, 16)
            sp.dma_start(idb[:], ids.rearrange("(a b) -> a b", a=1)).then_inc(c_ld, 16)
            sp.dma_start(routn[:], router_w).then_inc(c_ld, 16)
            sp.dma_start(lorab[:], lora_b.rearrange("e r d -> (e r) d")).then_inc(c_ld, 16)
            for kc in range(KC):
                sp.dma_start(lora_n[:, kc * P:(kc + 1) * P].rearrange("p (e r) -> p e r", e=NE),
                             lora_a[:, kc * P:(kc + 1) * P, :].rearrange("e p r -> p e r")).then_inc(c_ld, 16)
            sp.dma_start(xn[:], x_t[0]).then_inc(x_ld, 16)
            with sp.Fori(1, NID) as i:
                nat_round(i, [(nat[j][:], w_cond[bass.ds(i, 1), j * P:(j + 1) * P, :]
                               .rearrange("a p d -> (a p) d")) for j in range(4)])
            nat_round(R_BASE, [(nat[j][:], base_w[j * P:(j + 1) * P, :]) for j in range(4)])
            sp.wait_ge(zeroed, 1)
            sp.dma_start(a_d.rearrange("t p d -> p t d"),
                         zero[:].unsqueeze(1).to_broadcast([P, NT, D])).then_inc(a_st, 16)
            def l0(t, load, res, pad=False):
                if load:
                    sp.wait_ge(pe_xt, t + 1)
                    sp.dma_start(xn[:], x_t[bass.ds(t + 1, 1)].rearrange("a p d -> (a p) d")).then_inc(x_ld, 16)
                if res:
                    if not isinstance(t, int) or t > 1:
                        sp.wait_ge(x1_rdy, t - 1)
                    sp.dma_start(xres[:], x_t[bass.ds(t - 1, 1)].rearrange("a p d -> (a p) d")).then_inc(xres_ld, 16)
                    sp.wait_ge(x1_rdy, t)
                    sp.dma_start(x1_d[bass.ds(t - 1, 1)].rearrange("a p d -> (a p) d"), x1n[:]).then_inc(x1_st, 16)
                    sp.wait_ge(x1t_ev, t)
                    sp.dma_start(x1t_d[bass.ds(t - 1, 1)].rearrange("a p d -> (a p) d"), x1t[:]).then_inc(x1t_st, 16)
                    sp.wait_ge(rtab, t * 8 + TAB_OPS)
                    sp.sem_inc(gate["sp"], 1)
                    sp.dma_start(tab_d[bass.ds(t - 1, 1)].rearrange("a p d -> (a p) d"), tab1[:].rearrange("p a c -> p (a c)")).then_inc(tab_st, 16)
                    if pad:
                        sp.dma_start(x1t_d[NT], x1t[:]).then_inc(x1t_st, 16)
                        sp.dma_start(tab_d[NT], tab1[:].rearrange("p a c -> p (a c)")).then_inc(tab_st, 16)

            l0(0, True, False)
            l0(1, True, True)
            with sp.Fori(2, NT - 1) as t:
                l0(t, True, True)
            l0(NT - 1, False, True)
            l0(NT, False, True, pad=True)
            sp.wait_ge(x1_st, 16 * NT)
            sp.wait_ge(x1t_st, 16 * (NT + 1))
            sp.wait_ge(tab_st, 16 * (NT + 1))

            with sp.Fori(0, NHALF) as h:
                sp.drain().then_inc(phase, 1)
                sp.wait_ge(phase, 8 * h + 4)
                sp.sem_inc(gate["sp"], 1)
                r0 = h * HALF_ROUNDS + R_HALF
                with sp.Fori(0, 4) as i:
                    nat_round(r0 + i, [(nat[j][:], wq[bass.ds(h * (HQ2 * HD) + i * 512 + j * P, P), :]) for j in range(4)])
                nat_round(r0 + 4, [(nat[j][:], wk[bass.ds(h * (HK2 * HD) + j * P, P), :]) for j in range(4)])
                nat_round(r0 + 5, [(nat[j][:], wv[bass.ds(h * (HK2 * HD) + j * P, P), :]) for j in range(4)])

                def xt_load(t, par):
                    sp.dma_start(xt[par][:].rearrange("p k c -> p (k c)"),
                                 x1t_d[bass.ds(t, 1)].rearrange("a p d -> (a p) d")).then_inc(xt_ld[par], 16)

                def tab_load(t, par):
                    sp.dma_start(tab[par][:].rearrange("p k c -> p (k c)"),
                                 tab_d[bass.ds(t, 1)].rearrange("a p d -> (a p) d")).then_inc(tab_ld[par], 16)

                def proj_store(t, par):
                    sp.dma_start(qkv_d[bass.ds(t, 1)].rearrange("a p d -> (a p) d"), qkv[par][:]).then_inc(proj_st[par], 16)

                for t in range(2):
                    xt_load(t, t)
                    tab_load(t, t)

                def project(t, n, par, first, last):
                    g = h * NT + t
                    if not last:
                        sp.wait_ge(xs_lo, g + 1)
                        sp.sem_inc(gate["sp"], 1)
                        xt_load(t + 2, par)
                        sp.wait_ge(rope, g * ROPE_OPS + 4 * ROPE_UNITS)
                        sp.sem_inc(gate["sp"], 1)
                        tab_load(t + 2, par)
                    if not first:
                        sp.wait_ge(tb_ev, g * ROPE_UNITS + 2)
                        sp.sem_inc(gate["sp"], 1)
                        proj_store(t - 1, 1 - par)
                    if isinstance(t, int) and t == 1:
                        sp.dma_start(qkv_d[NT], qkv[0][:]).then_inc(pad_st, 16)

                def turn(i):
                    project(i * 2, i, 0, False, False)
                    project(i * 2 + 1, i, 1, False, False)

                project(0, 0, 0, True, False)
                project(1, 0, 1, False, False)
                with sp.Fori(1, 5) as i:
                    turn(i)
                    for j in range(4):
                        sp.dma_start(raw[:, bass.ds(i - 1, 1), j, :].rearrange("p a d -> p (a d)"),
                                     wo[j * P:(j + 1) * P, bass.ds(h * (HQ2 * HD) + (i - 1) * 512, 512)]).then_inc(raw_full, 16)
                with sp.Fori(5, NT // 2 - 1) as i:
                    turn(i)
                project(NT - 2, NT // 2 - 1, 0, False, False)
                project(NT - 1, NT // 2 - 1, 1, False, True)

                def key_round(i, rnd):
                    nat_round(rnd, [(nat[j][:].rearrange("p (h d) -> p h d", h=HK2),
                                     k_cache[bass.ds(i * 16 + j * 4, 4), :, bass.ds(h * HK2, HK2), :]
                                     .rearrange("a s h d -> (a s) h d")) for j in range(4)])

                key_round(0, r0 + 6)
                sp.wait_ge(tb_ev, (h + 1) * (NT * ROPE_UNITS) + 2)
                sp.sem_inc(gate["sp"], 1)
                proj_store(NT - 1, 1)
                sp.wait_ge(xt_ld[0], (h + 1) * (16 * LOADS[0]))
                sp.sem_inc(gate["sp"], 1)
                sp.wait_ge(tab_ld[0], (h + 1) * (16 * LOADS[0]))
                sp.sem_inc(gate["sp"], 1)
                sp.drain().then_inc(phase, 1)
                sp.wait_ge(phase, 8 * h + 8)
                sp.sem_inc(gate["sp"], 1)

                with sp.Fori(1, NPAGES // 16) as i:
                    key_round(i, r0 + 5 + i * 2)

                def v_load(n, par):
                    pg = regs(SP_, pages[0:1, bass.ds(n * PG, PG)])
                    for j in range(PG):
                        q = j % 4
                        sp.dma_start(vg[par][PSZ * q:PSZ * (q + 1), j // 4, :],
                                     v_cache[bass.ds(pg[j], 1), :, bass.ds(h * HK2, HK2), :]
                                     .rearrange("a s h d -> (a s) (h d)")).then_inc(v_ld[par], 16)

                def qkv_load(t, par):
                    sp.dma_start(qkv[par][:], qkv_d[bass.ds(t, 1)].rearrange("a p d -> (a p) d")).then_inc(qkv_ld[par], 16)

                for par in range(2):
                    sp.wait_ge(proj_st[par], (h + 1) * (16 * (NT // 2)))
                    sp.sem_inc(gate["sp"], 1)
                sp.wait_ge(pad_st, (h + 1) * 16)
                sp.sem_inc(gate["sp"], 1)
                qkv_load(0, 0)
                qkv_load(1, 1)
                v_load(0, 0)
                v_load(1, 1)

                def sum_load(t):
                    sp.wait_ge(a_st, (h * NT + t + 1) * 16)
                    sp.sem_inc(gate["sp"], 1)
                    sp.dma_start(an[:], a_d[bass.ds(t, 1)].rearrange("a p d -> (a p) d")).then_inc(a_ld, 16)

                def sum_store(t):
                    sp.wait_ge(op_ev, h * NT + t + 1)
                    sp.sem_inc(gate["sp"], 1)
                    sp.dma_start(a_d[bass.ds(t, 1)].rearrange("a p d -> (a p) d"), an[:]).then_inc(a_st, 16)

                def attend(t, n, par, first, last):
                    g = h * NT + t
                    if not first:
                        sum_load(t - 1)
                    for b in range(TB):
                        if not (last and b >= 2):
                            sp.wait_ge(pe_o, g * TB + b + 1)
                            sp.sem_inc(gate["sp"], 1)
                            v_load(t * TB + b + 2, b % 2)
                        if b == 0 and not first:
                            sum_store(t - 1)
                        if b == TB - 1 and not last:
                            qkv_load(t + 2, par)

                each_tile(sp, attend)
                sum_load(NT - 1)
                sum_store(NT - 1)
                sp.wait_ge(qkv_ld[0], (h + 1) * (16 * LOADS[0]))
                sp.sem_inc(gate["sp"], 1)

            sp.drain().then_inc(phase, 1)
            sp.wait_ge(phase, 8 * NHALF + 4)
            sp.wait_ge(a_st, 16 * (NHALF * NT + 1))
            for u in range(2):
                sp.wait_ge(g_st[u], 16 * ROUNDS)
            flat = w_d.rearrange("p c -> (p c)")
            wrow = [flat[m * I * D:(m + 1) * I * D].rearrange("(i j) -> i j", j=D) for m in range(2)]
            wdrow = flat[2 * I * D:].rearrange("(i j) -> i j", j=I)
            for u in range(3 * NI):
                m, c = divmod(u, NI)
                n = P if c < NI - 1 else ILAST
                r, j = R_FFN + u // 4, u % 4
                sp.wait_ge(prep_tr[j], r)
                if m < 2:
                    sp.dma_start(nat[j][0:n, :], wrow[m][c * P:c * P + n, :]).then_inc(nat_full[j], 16)
                else:
                    sp.dma_start(nat[j][:].rearrange("p (o c) -> p o c", o=4)[:, :, 0:n],
                                 wdrow[:, c * P:c * P + n].rearrange("(o p) c -> p o c", p=P)).then_inc(nat_full[j], 16)

            def an_load(n):
                sp.dma_start(an4[:], a_d[bass.ds(n * GT, GT)].rearrange("t p d -> p t d")).then_inc(an_ld, 16)

            an_load(0)
            for j in range(4):
                sp.wait_ge(prep_tr[j], R_FFN + (3 * NI - j + 3) // 4)

            def group(n, last):
                if not last:
                    sp.wait_ge(pe_at, (n + 1) * 4)
                    an_load(n + 1)
                for i in range(GT):
                    sp.wait_ge(out_add, n * GT + i + 1)
                    sp.dma_start(x1b[i % 2][:], x1_d[bass.ds(n * GT + i, 1)].rearrange("a p d -> (a p) d")).then_inc(x1b_ld[i % 2], 16)
                    if i >= 1:
                        sp.wait_ge(out_add, n * GT + i + 2)
                        sp.dma_start(out_t[bass.ds(n * GT + i - 1, 1)].rearrange("a p d -> (a p) d"), ob[(i - 1) % 2][:]).then_inc(o_st[(i - 1) % 2], 16)
                sp.wait_ge(out_add, n * GT + GT + 2)
                sp.dma_start(out_t[bass.ds(n * GT + GT - 1, 1)].rearrange("a p d -> (a p) d"), ob[(GT - 1) % 2][:]).then_inc(o_st[(GT - 1) % 2], 16)

            with sp.Fori(0, NGRP - 1) as n:
                group(n, False)
            group(NGRP - 1, True)
            for i in range(2):
                sp.wait_ge(o_st[i], 16 * (NT // 2))

        @block.gpsimd
        def _(pool):
            def load_numbers(r, u):
                pool.dma_start(gidx[u][:], idx_all[:, bass.ds((r * 2 + u) * CHUNK, CHUNK)]).then_inc(gi_ld[u], 16)

            def store(r, u, more):
                pool.wait_ge(gat[u], (r + 1) * (16 * CHUNK))
                pool.sem_inc(gate["pool"], 1)
                pool.dma_start(w_d[:, bass.ds((r * 2 + u) * (CHUNK * CW), CHUNK * CW)],
                               stage[u][:].rearrange("p n c -> p (n c)")).then_inc(g_st[u], 16)
                if more:
                    load_numbers(r + 1, u)

            def round_(r, first, last):
                for u in range(2):
                    pool.wait_ge(gi_ld[u], (r + 1) * 16)
                    pool.sem_inc(gate["pool"], 1)
                    if not first:
                        pool.wait_ge(g_st[u], r * 16)
                        pool.sem_inc(gate["pool"], 1)
                    for n in range(CHUNK):
                        if n == 8:
                            if u:
                                store(r, 0, not last)
                            elif not first:
                                store(r - 1, 1, True)
                        pool.indirect_dma_start(
                            out=stage[u][:, n, :], out_offset=None, in_=codebook,
                            in_offset=bass.IndirectOffsetOnAxis(ap=gidx[u][:, n:n + 1], axis=0)).then_inc(gat[u], 16)

            load_numbers(0, 0)
            load_numbers(0, 1)
            round_(0, True, False)
            with pool.Fori(1, ROUNDS - 1) as r:
                round_(r, False, False)
            round_(ROUNDS - 1, False, True)
            store(ROUNDS - 1, 1, False)

        @block.scalar
        def _(act):
            def copy(dst, src):
                return nc.scalar.activation(dst, src, ACT.Copy)

            def prep(rnd, dst):
                for j in (0, 2):
                    act.wait_ge(prep_tr[j], rnd + 1)
                    act.sem_inc(gate["act"], 1)
                    o, i = dst(j)
                    copy(o, i).then_inc(prep_ev[j], 1)

            def prep_high(rnd, dst):
                for j in range(4):
                    act.wait_ge(prep_tr[j], rnd + 1)
                    act.sem_inc(gate["act"], 1)
                    o, i = dst(j)
                    copy(o, i).then_inc(prep_hi, 1)

            act.sem_inc(tb_ev, 2)
            prep_high(0, lambda j: cond_dst(0, j, 0))
            act.wait_ge(rtab, RED_OPS)
            nc.scalar.activation(sin_[:].rearrange("p a b -> p (a b)"), red[:].rearrange("p a b -> p (a b)"), ACT.Sin).then_inc(trig, 1)
            nc.scalar.activation(cos_[:].rearrange("p a b -> p (a b)"), red[:].rearrange("p a b -> p (a b)"), ACT.Sin, scale=0.5).then_inc(trig, 1)
            with act.Fori(1, NID) as i:
                prep_high(i, lambda j: cond_dst(i, j, 0))
            prep_high(R_BASE, lambda j: base_dst(j, 0))
            act.wait_ge(zeroed, 2)
            act.wait_ge(pe_xt, 1)
            for b in range(TB):
                ins = copy(xtz_diag(b, 0), bank[0][:].rearrange("p (k c) -> p k c", k=KC)[:, :, b * S:(b + 1) * S])
            ins.then_inc(xtz_ev, 1)

            def l0(t, cond, nxt, prev):
                if prev:
                    act.wait_ge(rt, (t - 1) * RT_OPS + 1)
                    nc.scalar.activation(rex[:], bank[4][:, 0:NE], ACT.Exp, bias=nmx[:], accum_out=rsm[:, 0:1]).then_inc(rexp, 1)
                if cond:
                    act.wait_ge(pe_cond, t + 1)
                    copy(cn[:], bank[1][:]).then_inc(c_ev, 1)
                if prev:
                    act.wait_ge(pe_mt, t)
                    copy(mt[:], bank[5][:, 0:P]).then_inc(mt_ev, 1)
                if nxt:
                    act.wait_ge(pe_xt, t + 2)
                    for b in range(TB):
                        ins = copy(xtz_diag(b, 0), bank[0][:].rearrange("p (k c) -> p k c", k=KC)[:, :, b * S:(b + 1) * S])
                    ins.then_inc(xtz_ev, 1)
                if cond:
                    act.wait_ge(pe_ct, t + 1)
                    copy(ct[:, 0], bank[2][:]).then_inc(ct_ev, 1)
                if prev:
                    act.wait_ge(pe_x1t, t)
                    if not isinstance(t, int) or t > 1:
                        act.wait_ge(x1t_st, (t - 1) * 16)
                    else:
                        act.wait_ge(a_st, 16)
                    copy(x1t[:], bank[6][:]).then_inc(x1t_ev, 1)

            l0(0, True, True, False)
            l0(1, True, True, True)
            with act.Fori(2, NT - 1) as t:
                l0(t, True, True, True)
            l0(NT - 1, True, False, True)
            l0(NT, False, False, True)

            with act.Fori(0, NHALF) as h:
                act.drain().then_inc(phase, 1)
                act.wait_ge(phase, 8 * h + 4)
                act.sem_inc(gate["act"], 1)
                r0 = h * HALF_ROUNDS + R_HALF
                with act.Fori(0, 4) as i:
                    prep_high(r0 + i, lambda j: wq_dst(i, j, 0))
                prep_high(r0 + 4, lambda j: kv_dst(0, j, 0))
                prep_high(r0 + 5, lambda j: kv_dst(1, j, 0))

                def x_high(t, n, par):
                    act.wait_ge(xt_ld[par], (h * LOADS[par] + n + 1) * 16)
                    copy(xs2[par][:, 0], xt[par][:]).then_inc(xs_hi, 1)

                def unit(g, par, u, first):
                    act.wait_ge(unit_mm, g * ROPE_UNITS + u + 1)
                    if not first:
                        act.wait_ge(rope, g * ROPE_OPS + (4 * u + 3 - ROPE_OPS))
                    act.sem_inc(gate["act"], 1)
                    copy(qn[:, u].rearrange("p r d -> p (r d)"), bank[u][:]).then_inc(unit_cp, 1)
                    act.wait_ge(unit_cp, g * ROPE_UNITS + u + 1)
                    for i in range(REP):
                        ins = nc.scalar.activation(bank[u][:, i * HD:(i + 1) * HD], bank[u][:, i * HD:(i + 1) * HD], ACT.Square,
                                                   scale=HD ** -0.5, accum_out=ssq[par][:, 4 * u + i:4 * u + i + 1])
                    ins.then_inc(unit_ev, 1)

                def transposed(g, par, q):
                    act.wait_ge(pe_tb, g * ROPE_UNITS + q + 1)
                    src = bank[6 + (par + q) % 2]
                    if q < 4:
                        copy(qt_of(qkv[par])[:, :, q], src[:].rearrange("p (r b s) -> p b r s", r=REP, b=TB)).then_inc(tb_ev, 1)
                    else:
                        copy(kt_of(qkv[par]), src[:]).then_inc(tb_ev, 1)

                x_high(0, 0, 0)

                def project(t, n, par, first, last):
                    g = h * NT + t
                    for u in range(ROPE_UNITS):
                        unit(g, par, u, first)
                        if u == 1 and not last:
                            if not first:
                                act.wait_ge(pe_v, g)
                            x_high(t + 1, n + par, 1 - par)
                        if u >= 1 and not first:
                            transposed(g - 1, 1 - par, u - 1)
                    act.wait_ge(pe_v, g + 1)
                    if not (isinstance(t, int) and t < 2):
                        act.wait_ge(proj_st[par], (h * (NT // 2) + n) * 16)
                        if par == 0:
                            act.wait_ge(pad_st, (h + 1) * 16)
                    act.sem_inc(gate["act"], 1)
                    copy(v_of(qkv[par]), bank[5][:]).then_inc(v_ev, 1)
                    if not first:
                        transposed(g - 1, 1 - par, 4)

                each_tile_2(act, project)
                for q in range(ROPE_UNITS):
                    transposed(h * NT + NT - 1, 1, q)
                act.drain().then_inc(phase, 1)
                act.wait_ge(phase, 8 * h + 8)
                act.sem_inc(gate["act"], 1)

                with act.Fori(0, NPAGES // 16) as i:
                    prep(r0 + 6 + i * 2, lambda j: kt_dst(i, j))
                    prep_high(r0 + 7 + i * 2, lambda j: wo_dst(i, j, 0))

                def softmax(g, par, p):
                    b, hh = divmod(p, HK2)
                    act.wait_ge(ttr, g * NP + p + 1)
                    nc.scalar.activation(sm[p % 2][:], sm[p % 2][:], ACT.Exp, bias=mp[:, p:p + 1], scale=-1.0,
                                         accum_out=sumc[:, p:p + 1]).then_inc(ex, 1)
                    nc.scalar.activation(pz[:, b, hh, b * S:(b + 1) * S], sn[par][:, p, :], ACT.Exp, bias=mp[:, p:p + 1], scale=-1.0,
                                         accum_out=sumn[:, p:p + 1]).then_inc(exn, 1)

                def pt_out(g, p):
                    act.wait_ge(pe_t, g * NP + p + 1)
                    copy(pts[p % 2][:].rearrange("p k c -> p (k c)"), bank[2 + p % 2][:]).then_inc(pt_a, 1)

                def new_probs(g, b):
                    act.wait_ge(pe_tn, g * TB + b + 1)
                    copy(pnt[:].rearrange("p h c -> p (h c)"), bank[6][:]).then_inc(tn_ev, 1)

                def ot_high(g, b):
                    act.wait_ge(pe_ot, g * TB + b + 1)
                    copy(ots[:, 0, :, b * S:(b + 1) * S], bank[6][:].rearrange("p (h s) -> p h s", s=S)).then_inc(ot_hi, 1)

                def new_scores(g, par):
                    act.wait_ge(pe_sn, g + 1)
                    copy(sn[par][:].rearrange("p n s -> p (n s)"), bank[7][:]).then_inc(sn_ev, 1)

                new_scores(h * NT, 0)
                act.wait_ge(pz_zero, h + 1)
                act.wait_ge(sn_ev, h * NT + 1)
                softmax(h * NT, 0, 0)

                def attend(t, n, par, first, last):
                    g = h * NT + t
                    for p in range(NP):
                        if p % 4 == 0 and p:
                            new_probs(g, p // 4 - 1)
                        elif p == 0 and not first:
                            new_probs(g - 1, TB - 1)
                        pt_out(g, p)
                        if p < NP - 1:
                            softmax(g, par, p + 1)
                        elif not last:
                            act.wait_ge(sn_ev, g + 2)
                            softmax(g + 1, 1 - par, 0)
                        if p % 4 == 2 and p >= 6:
                            ot_high(g, (p - 6) // 4)
                        if p == 2 and not first:
                            ot_high(g - 1, TB - 1)
                        if p == SN_AT + 1 and not last:
                            new_scores(g + 1, 1 - par)

                each_tile(act, attend)
                new_probs(h * NT + NT - 1, TB - 1)
                ot_high(h * NT + NT - 1, TB - 1)

            act.drain().then_inc(phase, 1)
            act.wait_ge(phase, 8 * NHALF + 4)
            for u in range(3 * NI):
                act.wait_ge(prep_tr[u % 4], R_FFN + u // 4 + 1)
                o, i = ffn_dst(u, 0)
                copy(o, i).then_inc(prep_hi, 1)

            def at_out(n):
                for k in range(KC):
                    act.wait_ge(pe_at, n * KC + k + 1)
                    copy(at4[:, 0, k, :], bank[6 + k % 2][:]).then_inc(at_hi, 1)

            def ht_high(n, c):
                m = P if c < NI - 1 else ILAST
                act.wait_ge(hmul, n * NI + c + 1)
                copy(ht[0:m, 0, c, :], sg[c % 2][0:m, :]).then_inc(ht_hi, 1)

            at_out(0)

            def group(n, last):
                for c in range(NI):
                    m = P if c < NI - 1 else ILAST
                    act.wait_ge(pe_gu, n * NI + c + 1)
                    if c >= 2:
                        act.wait_ge(hm, n * NI + c - 1)
                    nc.scalar.activation(sg[c % 2][0:m, :], bank[c % 2][0:m, :], ACT.Silu).then_inc(silu, 1)
                    if c:
                        ht_high(n, c - 1)
                ht_high(n, NI - 1)
                if not last:
                    at_out(n + 1)

            with act.Fori(0, NGRP - 1) as n:
                group(n, False)
            group(NGRP - 1, True)

        @block.tensor
        def _(pe):
            def prep(rnd, load):
                for j in range(4):
                    pe.wait_ge(nat_full[j], (load + 1) * 16)
                    if not (isinstance(rnd, int) and rnd == 0):
                        pe.wait_ge(prep_ev[j], rnd)
                    for k in range(4):
                        ins = nc.tensor.transpose(bank[j][:, k * P:(k + 1) * P], nat[j][:, k * P:(k + 1) * P], ident[:])
                    ins.then_inc(prep_tr[j], 1)

            def prep_wo(rnd, i):
                for j in range(4):
                    pe.wait_ge(prep_ev[j], rnd)
                for j in range(4):
                    for k in range(4):
                        ins = nc.tensor.transpose(bank[j][:, k * P:(k + 1) * P], raw[:, i, k, j * P:(j + 1) * P], ident[:])
                    ins.then_inc(prep_tr[j], 1)

            def product(out_, x2, w2, first, last):
                for n, (a, b) in enumerate(((0, 0), (0, 1), (1, 0))):
                    ins = nc.tensor.matmul(out_, x2[:, a], w2[:, b], start=first and n == 0, stop=last and n == 2)
                return ins

            def block_t(dst, src, done):
                for k in range(4):
                    ins = nc.tensor.transpose(dst[:, k * P:(k + 1) * P], src[:, k * P:(k + 1) * P], ident[:])
                ins.then_inc(done, 1)

            pe.wait_ge(c_ld, 16 * 10)
            prep(0, 0)
            with pe.Fori(1, NID) as i:
                prep(i, i)
            prep(R_BASE, R_BASE)
            for k in range(KC):
                ins = nc.tensor.transpose(bank[7][:, k * NE:(k + 1) * NE], routn[:, k * P:(k + 1) * P], ident[0:NE, 0:NE])
            ins.then_inc(pe_r, 1)
            for j in range(4):
                pe.wait_ge(prep_ev[j], R_BASE + 1)
            pe.wait_ge(r_ev, 4)
            pe.wait_ge(x_ld, 16)
            block_t(bank[0], xn, pe_xt)

            def l0(t, cond, nxt, prev):
                if cond:
                    wid = nc.values_load_multi_w_load_instructions(
                        idb[0:1, bass.ds(t * TB, TB)], engines=[PE_], min_val=0, max_val=NID - 1,
                        skip_runtime_bounds_check_because="adapter numbers are below the adapters' count")[1]
                    pe.wait_ge(xtz_lo, t + 1)
                    for b in range(TB):
                        for k in range(KC):
                            ins = product(bank[1][:], xtz[:, :, k, b * P:(b + 1) * P],
                                          wt_all[:, :, bass.ds(wid[b], 1), k, :].rearrange("p w a d -> p w (a d)"),
                                          b == 0 and k == 0, b == TB - 1 and k == KC - 1)
                    ins.then_inc(pe_cond, 1)
                if prev:
                    pe.wait_ge(rt, t * RT_OPS)
                    nc.tensor.transpose(bank[5][:, 0:P], mm[:].rearrange("p e r -> p (e r)"), ident[:]).then_inc(pe_mt, 1)
                if nxt:
                    pe.wait_ge(x_ld, (t + 2) * 16)
                    block_t(bank[0], xn, pe_xt)
                if prev:
                    pe.wait_ge(mt_ev, t)
                    nc.tensor.matmul(bank[3][:], mt[:], lorab[:], start=False, stop=True).then_inc(pe_y0, 1)
                if cond:
                    pe.wait_ge(c_ev, t + 1)
                    block_t(bank[2], cn, pe_ct)
                if prev:
                    pe.wait_ge(x1_rdy, t)
                    if not isinstance(t, int) or t > 1:
                        pe.wait_ge(x1t_ev, t - 1)
                    block_t(bank[6], x1n, pe_x1t)
                if cond:
                    pe.wait_ge(ct_lo, t + 1)
                    for k in range(KC):
                        product(bank[3][:], ct[:, :, k * P:(k + 1) * P], w_base[:, :, k, 0:D], k == 0, False)
                    for k in range(KC):
                        ins = product(bank[4][:, 0:NE + P], ct[:, :, k * P:(k + 1) * P], w_base[:, :, k, D:],
                                      k == 0, k == KC - 1)
                    ins.then_inc(pe_mid, 1)

            l0(0, True, True, False)
            l0(1, True, True, True)
            with pe.Fori(2, NT - 1) as t:
                l0(t, True, True, True)
            l0(NT - 1, True, False, True)
            l0(NT, False, False, True)

            with pe.Fori(0, NHALF) as h:
                pe.drain().then_inc(phase, 1)
                pe.wait_ge(phase, 8 * h + 4)
                pe.sem_inc(gate["pe"], 1)
                r0 = h * HALF_ROUNDS + R_HALF
                l0_ = h * HALF_LOADS + R_HALF
                with pe.Fori(0, 4) as i:
                    prep(r0 + i, l0_ + i)
                prep(r0 + 4, l0_ + 4)
                prep(r0 + 5, l0_ + 5)
                for k in range(4):
                    pe.wait_ge(prep_ev[k], r0 + 6)

                def unit(g, par, u, first):
                    if u == 0:
                        pe.wait_ge(xs_lo, g + 1)
                    if not first:
                        if u < ROPE_UNITS:
                            pe.wait_ge(unit_ev, g * ROPE_UNITS + (u + 1 - ROPE_UNITS))
                        else:
                            pe.wait_ge(v_ev, g)
                    if u == 0:
                        w = wkvs[:, :, :, 0:512]
                    elif u < ROPE_UNITS:
                        w = wqs[:, :, :, (u - 1) * 512:u * 512]
                    else:
                        w = wkvs[:, :, :, 512:1024]
                    for k in range(KC):
                        ins = product(bank[u][:], xs2[par][:, :, k, :], w[:, :, k, :], k == 0, k == KC - 1)
                    ins.then_inc(unit_mm if u < ROPE_UNITS else pe_v, 1)

                def transposed(g, par, q):
                    if q == 0:
                        pe.wait_ge(rope, (g + 1) * ROPE_OPS)
                    pe.wait_ge(tb_ev, g * ROPE_UNITS + (q + 1))
                    block_t(bank[6 + (par + q) % 2], qkf[par][:, (q + 1) % ROPE_UNITS].rearrange("p r d -> p (r d)"), pe_tb)

                def project(t, n, par, first, last):
                    g = h * NT + t
                    for u in range(ROPE_UNITS + 1):
                        unit(g, par, u, first)
                        if u and not first:
                            transposed(g - 1, 1 - par, u - 1)

                each_tile_2(pe, project)
                for q in range(ROPE_UNITS):
                    transposed(h * NT + NT - 1, 1, q)
                pe.drain().then_inc(phase, 1)
                pe.wait_ge(phase, 8 * h + 8)
                pe.sem_inc(gate["pe"], 1)

                for i in range(NPAGES // 16):
                    prep(r0 + 6 + i * 2, l0_ + 6 + i)
                    if i == 0:
                        pe.wait_ge(raw_full, (h + 1) * (16 * 16))
                    prep_wo(r0 + 7 + i * 2, i)
                for k in range(4):
                    pe.wait_ge(prep_ev[k], r0 + HALF_ROUNDS)

                def new_scores(g, n, par, free, pairs):
                    if pairs[0] == 0:
                        pe.wait_ge(qkv_ld[par], (h * LOADS[par] + n + 1) * 16)
                    if pairs[0] == 0 and free:
                        pe.wait_ge(sn_ev, g)
                    for p in pairs:
                        b, hh = divmod(p, HK2)
                        ins = nc.tensor.matmul(bank[7][:, p * S:(p + 1) * S], qt_of(qkv[par])[:, b, hh].rearrange("p r s -> p (r s)"),
                                               kt_of(qkv[par])[:, hh * P + b * S:hh * P + (b + 1) * S], start=True, stop=True)
                    if pairs[-1] == NP - 1:
                        ins.then_inc(pe_sn, 1)

                def scores(t, par, p, free=True):
                    b, hh = divmod(p, HK2)
                    if hh == 0:
                        pe.wait_ge(kg_rdy, (h * NB + t * TB + b + 1))
                    if free:
                        pe.wait_ge(ttr, (h * NT + t) * NP + (p - 1))
                    nc.tensor.matmul(bank[p % 2][:], qt_of(qkv[par])[:, b, hh].rearrange("p r s -> p (r s)"),
                                     kg[b % 2][:, hh].rearrange("p g s -> p (g s)"), start=True, stop=True).then_inc(s_mm, 1)

                def values(t, p):
                    g = h * NT + t
                    b, hh = divmod(p, HK2)
                    pe.wait_ge(pt_a, g * NP + p + 1)
                    if hh == 0:
                        pe.wait_ge(v_ld[b % 2], (h * (NB // 2) + t * 2 + b // 2 + 1) * (16 * PG))
                        pe.wait_ge(on_rdy, g * TB + b + 1)
                    for c in range(KC):
                        nc.tensor.matmul(bank[4 + b % 2][:, hh * HD:(hh + 1) * HD], pts[p % 2][:, c, :],
                                         vg[b % 2][:, c, hh * HD:(hh + 1) * HD], start=(hh == 0 and c == 0), stop=False,
                                         skip_group_check=True)

                def values_new(t, par, b):
                    g = h * NT + t
                    pe.wait_ge(tn_ev, g * TB + b + 1)
                    for hh in range(HK2):
                        ins = nc.tensor.matmul(bank[4 + b % 2][:, hh * HD:(hh + 1) * HD], pnt[:, hh, :],
                                               v_of(qkv[par])[:, hh * HD:(hh + 1) * HD], start=False, stop=(hh == HK2 - 1),
                                               skip_group_check=True)
                    ins.then_inc(pe_o, 1)

                def new_probs(g, b, free):
                    pe.wait_ge(exn, g * NP + (b + 1) * HK2)
                    if free:
                        pe.wait_ge(ot_ev, g * TB + b)
                    block_t(bank[6], pz[:, b].rearrange("p h c -> p (h c)"), pe_tn)

                def out_t_(t, b):
                    pe.wait_ge(on_rdy, (h * NT + t) * TB + b + 3)
                    block_t(bank[6], on[:].rearrange("p h d -> p (h d)"), pe_ot)

                def out_product(g, part):
                    if part == 0:
                        pe.wait_ge(ot_ev, (g + 1) * TB)
                    for k in range(part * HQ2 // 3, (part + 1) * HQ2 // 3):
                        ins = product(bank[7][:], ots[:, :, k, :], wots[:, :, k, :], k == 0, k == HQ2 - 1)
                    if part == 2:
                        ins.then_inc(pe_op, 1)

                new_scores(h * NT, 0, 0, False, range(NP))
                scores(0, 0, 0, False)

                def attend(t, n, par, first, last):
                    g = h * NT + t
                    for p in range(NP):
                        if p < NP - 1:
                            scores(t, par, p + 1, not (first and p == 0))
                        elif not last:
                            scores(t + 1, 1 - par, 0)
                        if p % 4 == 0 and p:
                            new_probs(g, p // 4 - 1, not (first and p == 4))
                        elif p == 0 and not first:
                            new_probs(g - 1, TB - 1, True)
                        pe.wait_ge(ex, g * NP + p + 1)
                        block_t(bank[2 + p % 2], sm[p % 2], pe_t)
                        if p >= 1:
                            values(t, p - 1)
                        elif not first:
                            values(t - 1, NP - 1)
                        if p >= 4 and p % 4 == 0:
                            values_new(t, par, p // 4 - 1)
                        if p == 0 and not first:
                            values_new(t - 1, 1 - par, TB - 1)
                        if p in (4, 5, 6) and not first:
                            if p == 4:
                                pe.wait_ge(sn_ev, g + 1)
                            out_product(g - 1, p - 4)
                        if p % 4 == 2 and p >= 6:
                            out_t_(t, (p - 6) // 4)
                        if p == 2 and not first:
                            out_t_(t - 1, TB - 1)
                        if SN_AT - 4 <= p <= SN_AT and not last:
                            if p == SN_AT - 4 and not first:
                                pe.wait_ge(op_ev, g)
                            k = p - SN_AT + 4
                            new_scores(g + 1, n + par, 1 - par, True, range(NP)[k * NP // 5:(k + 1) * NP // 5])

                each_tile(pe, attend)
                new_probs(h * NT + NT - 1, TB - 1, True)
                values(NT - 1, NP - 1)
                values_new(NT - 1, 1, TB - 1)
                out_t_(NT - 1, TB - 1)
                for part in range(3):
                    out_product(h * NT + NT - 1, part)

            pe.drain().then_inc(phase, 1)
            pe.wait_ge(phase, 8 * NHALF + 4)
            for u in range(3 * NI):
                m, c = divmod(u, NI)
                n = P if c < NI - 1 else ILAST
                r, j = R_FFN + u // 4, u % 4
                pe.wait_ge(nat_full[j], (r + 1 - NHALF * (HALF_ROUNDS - HALF_LOADS)) * 16)
                pe.wait_ge(prep_ev[j], r)
                for k in range(4):
                    if m < 2:
                        ins = nc.tensor.transpose(bank[j][:, k * P:k * P + n], nat[j][0:n, k * P:(k + 1) * P], ident[0:n, 0:n])
                    else:
                        ins = nc.tensor.transpose(bank[j][0:n, k * P:(k + 1) * P], nat[j][:, k * P:k * P + n], ident[:])
                ins.then_inc(prep_tr[j], 1)

            def at_in(n):
                pe.wait_ge(an_ld, (n + 1) * 16)
                for k in range(KC):
                    if k >= 2:
                        pe.wait_ge(at_ev, n * KC + k - 1)
                    for i in range(GT):
                        ins = nc.tensor.transpose(bank[6 + k % 2][:, i * P:(i + 1) * P], an4[:, i, k * P:(k + 1) * P], ident[:])
                    ins.then_inc(pe_at, 1)

            at_in(0)
            for j in range(4):
                pe.wait_ge(prep_ev[j], R_FFN + (3 * NI - j + 3) // 4)

            def group(n, last):
                pe.wait_ge(at_ev, n * KC + KC)
                for c in range(NI):
                    m = P if c < NI - 1 else ILAST
                    if c >= 2:
                        pe.wait_ge(hmul, n * NI + c - 1)
                    for w in range(2):
                        for k in range(KC):
                            ins = product(bank[2 * w + c % 2][0:m, :], wgus[w][:, :, k, c * P:c * P + m], at4[:, :, k, :],
                                          k == 0, k == KC - 1)
                    ins.then_inc(pe_gu, 1)
                if not last:
                    at_in(n + 1)
                pe.wait_ge(hm, n * NI + NI)
                for i in range(GT):
                    pe.wait_ge(out_add, n * GT + i + 1)
                    for c in range(NI):
                        m = P if c < NI - 1 else ILAST
                        ins = product(bank[4 + i % 2][:], ht[0:m, :, c, i * P:(i + 1) * P], wds[0:m, :, c, :],
                                      c == 0, c == NI - 1)
                    ins.then_inc(pe_dn, 1)

            with pe.Fori(0, NGRP - 1) as n:
                group(n, False)
            group(NGRP - 1, True)

        @block.vector
        def _(dve):
            V = nc.vector

            def prep(rnd, dst):
                for j in (1, 3):
                    dve.wait_ge(prep_tr[j], rnd + 1)
                    dve.sem_inc(gate["dve"], 1)
                    o, i = dst(j)
                    V.tensor_copy(o, i).then_inc(prep_ev[j], 1)

            def prep_low(rnd, n, dst):
                for j in range(4):
                    dve.wait_ge(prep_hi, n * 4 + (j + 1))
                    dve.sem_inc(gate["dve"], 1)
                    (low, src), high = dst(j, 1), dst(j, 0)[0]
                    V.tensor_tensor(low, src, high.bitcast(F32), ALU.subtract).then_inc(prep_ev[j], 1)

            class Steps:

                def __init__(self, sem_, start):
                    self.sem, self.start, self.n = sem_, start, 0

                def done(self, ins):
                    ins.then_inc(self.sem, 1)
                    self.n += 1

                def wait(self):
                    dve.wait_ge(self.sem, self.start + self.n)

            dve.sem_inc(on_rdy, 2)
            dve.sem_inc(out_add, 2)
            V.memset(zero[:], 0.0).then_inc(zeroed, 1)
            V.memset(xtz[:, 0].bitcast(F32), 0.0).then_inc(zeroed, 1)

            dve.wait_ge(c2_ld, 64)
            st = Steps(rtab, 0)
            invf, ptok = con2[:, 0:HD // 2], con2[:, HD // 2:HD // 2 + 1]
            tri = con2[:, HD // 2 + 1:HD // 2 + 1 + NE * NE].rearrange("p (a b) -> p a b", a=NE)
            st.done(V.tensor_copy(seqf[:], seqi[:]))
            st.wait()
            for b in range(TB):
                rows = slice(b * S, (b + 1) * S)
                st.done(V.tensor_copy(pos[rows, :], seqf[rows, :].rearrange("p (t b) -> p b t", b=TB)[:, b, :]))
            st.wait()
            st.done(V.tensor_scalar(pos[:], pos[:], ptok, None, ALU.add))
            st.wait()
            st.done(V.tensor_tensor(ang[:], pos[:].unsqueeze(2).to_broadcast([P, NT, HD // 2]),
                                    invf.unsqueeze(1).to_broadcast([P, NT, HD // 2]), ALU.mult))
            st.wait()
            st.done(V.tensor_scalar(cos_[:], ang[:], 1.0 / TWO_PI, MAGIC, ALU.mult, ALU.add))
            st.wait()
            st.done(V.tensor_scalar(sin_[:], cos_[:], -MAGIC, None, ALU.add))
            src = ang
            for part in (PI1, PI2, PI3):
                st.wait()
                st.done(V.scalar_tensor_tensor(out=red[:], in0=sin_[:], scalar=-part, in1=src[:], op0=ALU.mult, op1=ALU.add))
                src = red
            st.wait()
            st.done(V.tensor_scalar(red[:], red[:], 3.1415925, -3.1415925, ALU.min, ALU.max))
            assert st.n == RED_OPS
            prep_low(0, 0, lambda j, part: cond_dst(0, j, part))
            half = HD // 2
            dve.wait_ge(trig, 2)
            st.done(V.tensor_tensor(cos_[:], cos_[:], cos_[:], ALU.mult))
            st.wait()
            st.done(V.tensor_scalar(cos_[:], cos_[:], -2.0, 1.0, ALU.mult, ALU.add))
            st.done(V.tensor_scalar(qkw[:, 0, :], qkw[:, 0, :], -SCALE, None, ALU.mult))
            st.wait()
            assert st.n == TAB_OPS
            V.memset(xtz[:, 1].bitcast(F32), 0.0).then_inc(zeroed, 1)

            def table(t):
                if not isinstance(t, int) or t > 1:
                    dve.wait_ge(tab_st, (t - 1) * 16)
                    dve.sem_inc(gate["dve"], 1)
                c = cos_[:, bass.ds(t - 1, 1)].rearrange("p a c -> p (a c)")
                sn_t = sin_[:, bass.ds(t - 1, 1)].rearrange("p a c -> p (a c)")
                for n in range(2):
                    w1, w2 = qkw[:, n, 0:half], qkw[:, n, half:HD]
                    V.tensor_tensor(tab1[:, 2 * n, 0:half], c, w1, ALU.mult).then_inc(rtab, 1)
                    V.tensor_tensor(tab1[:, 2 * n, half:HD], c, w2, ALU.mult).then_inc(rtab, 1)
                    V.scalar_tensor_tensor(out=tab1[:, 2 * n + 1, 0:half], in0=sn_t, scalar=-1.0, in1=w2, op0=ALU.mult, op1=ALU.mult).then_inc(rtab, 1)
                    V.tensor_tensor(tab1[:, 2 * n + 1, half:HD], sn_t, w1, ALU.mult).then_inc(rtab, 1)

            with dve.Fori(1, NID) as i:
                prep_low(i, i, lambda j, part: cond_dst(i, j, part))
            prep_low(R_BASE, R_BASE, lambda j, part: base_dst(j, part))

            def side(part):
                return (w_base[:, part, :, D:D + NE], w_base[:, part, :, D + NE:])

            router = bank[7][:, 0:KC * NE].rearrange("p (k e) -> p k e", k=KC)
            lora = lora_n[:].rearrange("p (k c) -> p k c", k=KC)
            dve.wait_ge(pe_r, 1)
            V.tensor_copy(side(0)[0], router).then_inc(r_ev, 1)
            dve.wait_ge(c_ld, 16 * 10)
            V.tensor_copy(side(0)[1], lora).then_inc(r_ev, 1)
            dve.wait_ge(r_ev, 2)
            V.tensor_tensor(side(1)[0], router, side(0)[0].bitcast(F32), ALU.subtract).then_inc(r_ev, 1)
            V.tensor_tensor(side(1)[1], lora, side(0)[1].bitcast(F32), ALU.subtract).then_inc(r_ev, 1)

            def x_low(t):
                dve.wait_ge(xtz_ev, t + 1)
                dve.sem_inc(gate["dve"], 1)
                for b in range(TB):
                    ins = V.tensor_tensor(xtz_diag(b, 1), bank[0][:].rearrange("p (k c) -> p k c", k=KC)[:, :, b * S:(b + 1) * S],
                                          xtz_diag(b, 0).bitcast(F32), ALU.subtract)
                ins.then_inc(xtz_lo, 1)

            def c_low(t):
                dve.wait_ge(ct_ev, t + 1)
                V.tensor_tensor(ct[:, 1], bank[2][:], ct[:, 0].bitcast(F32), ALU.subtract).then_inc(ct_lo, 1)

            dve.wait_ge(zeroed, 3)
            x_low(0)
            x_low(1)
            c_low(0)

            def l0(t):
                st = Steps(rt, (t - 1) * RT_OPS)
                dve.wait_ge(pe_mid, t)
                st.done(V.tensor_reduce(nmx[:], bank[4][:, 0:NE], AX.X, ALU.max, negate=True))
                dve.wait_ge(rexp, t)
                st.done(V.reciprocal(rsm[:, 1:2], rsm[:, 0:1]))
                st.wait()
                st.done(V.tensor_scalar(prb[:], rex[:], rsm[:, 1:2], None, ALU.mult))
                st.wait()
                by_j = prb[:].unsqueeze(1).to_broadcast([P, NE, NE])
                by_e = prb[:].unsqueeze(2).to_broadcast([P, NE, NE])
                st.done(V.tensor_tensor(cmp_[:], by_j, by_e, ALU.is_gt))
                st.done(V.tensor_tensor(eq[:], by_j, by_e, ALU.is_equal))
                st.wait()
                st.done(V.tensor_tensor(eq[:], eq[:], tri, ALU.mult))
                st.wait()
                st.done(V.tensor_tensor(cmp_[:], cmp_[:], eq[:], ALU.add))
                st.wait()
                st.done(V.tensor_reduce(rank[:], cmp_[:], AX.X, ALU.add))
                st.wait()
                st.done(V.scalar_tensor_tensor(out=sel[:], in0=rank[:], scalar=2.0, in1=prb[:], op0=ALU.is_lt, op1=ALU.mult))
                st.wait()
                st.done(V.tensor_reduce(rsm[:, 2:3], sel[:], AX.X, ALU.add))
                st.wait()
                st.done(V.reciprocal(rsm[:, 3:4], rsm[:, 2:3]))
                st.wait()
                st.done(V.tensor_scalar(wgt[:], sel[:], rsm[:, 3:4], 2.0, ALU.mult, ALU.mult))
                st.wait()
                st.done(V.tensor_tensor(mm[:], bank[4][:, NE:NE + P].rearrange("p (e r) -> p e r", e=NE),
                                        wgt[:].unsqueeze(2).to_broadcast([P, NE, RANK]), ALU.mult))
                assert st.n == RT_OPS
                if not isinstance(t, int) or t < NT - 1:
                    x_low(t + 1)
                dve.wait_ge(pe_y0, t)
                dve.wait_ge(xres_ld, t * 16)
                if not isinstance(t, int) or t > 1:
                    dve.wait_ge(x1_st, (t - 1) * 16)
                    dve.wait_ge(pe_x1t, t - 1)
                V.tensor_tensor(x1n[:], bank[3][:], xres[:], ALU.add).then_inc(x1_rdy, 1)
                if not isinstance(t, int) or t < NT:
                    c_low(t)
                table(t)

            l0(1)
            with dve.Fori(2, NT - 1) as t:
                l0(t)
            l0(NT - 1)
            l0(NT)

            with dve.Fori(0, NHALF) as h:
                dve.drain().then_inc(phase, 1)
                dve.wait_ge(phase, 8 * h + 4)
                dve.sem_inc(gate["dve"], 1)
                r0 = h * HALF_ROUNDS + R_HALF
                with dve.Fori(0, 4) as i:
                    prep_low(r0 + i, h * SPLITS + (R_HALF + i), lambda j, part: wq_dst(i, j, part))
                prep_low(r0 + 4, h * SPLITS + (R_HALF + 4), lambda j, part: kv_dst(0, j, part))
                prep_low(r0 + 5, h * SPLITS + (R_HALF + 5), lambda j, part: kv_dst(1, j, part))

                def rotate(g, n, par, u):
                    st = Steps(rope, g * ROPE_OPS + 4 * u)
                    v = 2 if u == 0 else 0
                    c = tab[par][:, v, :].unsqueeze(1).to_broadcast([P, REP, HD])
                    s1 = tab[par][:, v + 1, 0:half].unsqueeze(1).to_broadcast([P, REP, half])
                    s2 = tab[par][:, v + 1, half:HD].unsqueeze(1).to_broadcast([P, REP, half])
                    dve.wait_ge(unit_cp, g * ROPE_UNITS + u + 1)
                    if u == 0:
                        dve.wait_ge(tab_ld[par], (h * LOADS[par] + n + 1) * 16)
                    else:
                        st.wait()
                    st.done(V.tensor_tensor(qkf[par][:, u], qn[:, u], c, ALU.mult))
                    st.done(V.tensor_tensor(qb[:, :, 0:half], qn[:, u, :, half:HD], s1, ALU.mult))
                    st.done(V.tensor_tensor(qb[:, :, half:HD], qn[:, u, :, 0:half], s2, ALU.mult))
                    st.wait()
                    st.done(V.tensor_tensor(qkf[par][:, u], qkf[par][:, u], qb[:], ALU.add))

                def rsqrt(g, par):
                    st = Steps(rope, g * ROPE_OPS + 4 * ROPE_UNITS)
                    dve.wait_ge(unit_ev, g * ROPE_UNITS + ROPE_UNITS)
                    st.wait()
                    st.done(V.tensor_scalar(xs[:], ssq[par][:], EPS, None, ALU.add))
                    st.wait()
                    st.done(V.tensor_scalar(yi[:], xs[:].bitcast(I32), 1, None, ALU.logical_shift_right))
                    st.done(V.tensor_scalar(xh[:], xs[:], -0.5, None, ALU.mult))
                    st.wait()
                    st.done(V.tensor_scalar(yy[:].bitcast(I32), yi[:], -1.0, RSQRT_BITS, ALU.mult, ALU.add))
                    for _ in range(3):
                        st.wait()
                        st.done(V.tensor_tensor(y2[:], yy[:], yy[:], ALU.mult))
                        st.wait()
                        st.done(V.tensor_tensor(y3[:], y2[:], xh[:], ALU.mult))
                        st.wait()
                        st.done(V.scalar_tensor_tensor(out=yy[:], in0=y3[:], scalar=1.5, in1=yy[:], op0=ALU.add, op1=ALU.mult))

                def norm(g, par, part):
                    st = Steps(rope, g * ROPE_OPS + 4 * ROPE_UNITS + 13 + part)
                    if part == 0:
                        st.wait()
                    u0, u1 = (0, 2) if part == 0 else (2, ROPE_UNITS)
                    v = qkf[par][:, u0:u1].rearrange("p u r d -> p (u r) d")
                    st.done(V.tensor_tensor(v, v, yy[:, 4 * u0:4 * u1].unsqueeze(2).to_broadcast([P, 4 * (u1 - u0), HD]), ALU.mult))

                def x_low(g, par):
                    dve.wait_ge(xs_hi, g + 1)
                    V.tensor_tensor(xs2[par][:, 1], xt[par][:], xs2[par][:, 0].bitcast(F32), ALU.subtract).then_inc(xs_lo, 1)

                x_low(h * NT, 0)

                def project(t, n, par, first, last):
                    g = h * NT + t
                    for u in range(ROPE_UNITS):
                        rotate(g, n, par, u)
                        if u == 1 and not last:
                            x_low(g + 1, 1 - par)
                    rsqrt(g, par)
                    norm(g, par, 0)
                    norm(g, par, 1)

                each_tile_2(dve, project)
                dve.drain().then_inc(phase, 1)
                dve.wait_ge(phase, 8 * h + 8)
                dve.sem_inc(gate["dve"], 1)

                with dve.Fori(0, NPAGES // 16) as i:
                    prep(r0 + 6 + i * 2, lambda j: kt_dst(i, j))
                    prep_low(r0 + 7 + i * 2, h * SPLITS + (R_HALF + 6) + i, lambda j, part: wo_dst(i, j, part))
                for j in range(4):
                    dve.wait_ge(prep_ev[j], r0 + HALF_ROUNDS)
                dve.sem_inc(gate["dve"], 1)
                V.memset(pz[:], 0.0).then_inc(pz_zero, 1)

                def gather(n, par, part):
                    pg = regs(DVE_, pages[0:1, bass.ds(n * PG + part * 8, 8)])
                    for i in range(8):
                        ins = V.tensor_copy(kg[par][:, :, part * 8 + i, :],
                                            ktall[:, bass.ds(pg[i], 1)].rearrange("p a h s -> p (a h) s"))
                    if part:
                        ins.then_inc(kg_rdy, 1)

                def key_mask(t, b, free=True):
                    g = h * NT + t
                    if free:
                        dve.wait_ge(ttr, g * NP + (b - 1) * HK2)
                        dve.sem_inc(gate["dve"], 1)
                    V.tensor_scalar(mask[b % 2][:], keyidx[:], seqf[:, bass.ds(t * TB + b, 1)], BIG, ALU.is_ge, ALU.mult).then_inc(mk, 1)

                def least(t, p):
                    g = h * NT + t
                    b = p // HK2
                    if p % HK2 == 0:
                        dve.wait_ge(mk, g * TB + b + 1)
                    dve.wait_ge(s_mm, g * NP + p + 1)
                    dve.sem_inc(gate["dve"], 1)
                    V.tensor_tensor_reduce(out=sm[p % 2][:], in0=bank[p % 2][:], in1=mask[b % 2][:], scale=1.0, scalar=mnew[:, p:p + 1],
                                           op0=ALU.add, op1=ALU.min, accum_out=mp[:, p:p + 1]).then_inc(ttr, 1)

                def out_norm(g, b):
                    c = slice(b * HK2, (b + 1) * HK2)
                    dve.wait_ge(pe_o, g * TB + b + 1)
                    V.tensor_tensor(rsum[:, c], sumc[:, c], sumn[:, c], ALU.add).then_inc(osum, 1)
                    dve.wait_ge(osum, (g * TB + b) * 2 + 1)
                    V.reciprocal(rinv[:, c], rsum[:, c]).then_inc(osum, 1)
                    dve.wait_ge(osum, (g * TB + b) * 2 + 2)
                    V.tensor_tensor(on[:], bank[4 + b % 2][:].rearrange("p (h d) -> p h d", h=HK2),
                                    rinv[:, c].unsqueeze(2).to_broadcast([P, HK2, HD]), ALU.mult).then_inc(on_rdy, 1)

                def ot_low(g, b):
                    dve.wait_ge(ot_hi, g * TB + b + 1)
                    V.tensor_tensor(ots[:, 1, :, b * S:(b + 1) * S], bank[6][:].rearrange("p (h s) -> p h s", s=S),
                                    ots[:, 0, :, b * S:(b + 1) * S].bitcast(F32), ALU.subtract).then_inc(ot_ev, 1)

                def new_least(g, par, free):
                    if free:
                        dve.wait_ge(ttr, g * NP)
                    dve.wait_ge(sn_ev, g + 1)
                    V.tensor_reduce(mnew[:], sn[par][:], AX.X, ALU.min).then_inc(mn, 1)

                def sum_add(g):
                    dve.wait_ge(pe_op, g + 1)
                    dve.wait_ge(a_ld, (g + 1) * 16)
                    V.tensor_tensor(an[:], bank[7][:], an[:], ALU.add).then_inc(op_ev, 1)

                gather(0, 0, 0)
                gather(0, 0, 1)
                gather(1, 1, 0)
                new_least(h * NT, 0, False)
                dve.wait_ge(mn, h * NT + 1)
                dve.sem_inc(gate["dve"], 1)
                key_mask(0, 0, False)
                least(0, 0)

                def attend(t, n, par, first, last):
                    g = h * NT + t
                    for p in range(NP):
                        b = p // HK2
                        if p < NP - 1:
                            least(t, p + 1)
                        elif not last:
                            dve.wait_ge(mn, g + 2)
                            dve.sem_inc(gate["dve"], 1)
                            least(t + 1, 0)
                        if p % 4 == 3 and p >= 7:
                            ot_low(g, (p - 7) // 4)
                        if p == 3 and not first:
                            ot_low(g - 1, TB - 1)
                        if p % 4 == 3 and not (last and b >= TB - 2):
                            gather(t * TB + b + 2, b % 2, 0)
                        if p % 4 == 2 and b < TB - 1:
                            key_mask(t, b + 1, not (first and b == 0))
                        elif p % 4 == 2 and not last:
                            key_mask(t + 1, 0)
                        if p % 4 == 0 and not (last and b == TB - 1):
                            gather(t * TB + b + 1, (b + 1) % 2, 1)
                        if p % 4 == 1 and p > 1:
                            out_norm(g, p // 4 - 1)
                        if p == 1 and not first:
                            out_norm(g - 1, TB - 1)
                        if p == 7 and not first:
                            sum_add(g - 1)
                        if p == NP - 2 and not last:
                            new_least(g + 1, 1 - par, True)

                each_tile(dve, attend)
                out_norm(h * NT + NT - 1, TB - 1)
                ot_low(h * NT + NT - 1, TB - 1)
                sum_add(h * NT + NT - 1)

            dve.drain().then_inc(phase, 1)
            dve.wait_ge(phase, 8 * NHALF + 4)
            for u in range(3 * NI):
                dve.wait_ge(prep_hi, (R_HALF + NHALF * SPLITS) * 4 + u + 1)
                (low, src), high = ffn_dst(u, 1), ffn_dst(u, 0)[0]
                V.tensor_tensor(low, src, high.bitcast(F32), ALU.subtract).then_inc(prep_ev[u % 4], 1)

            def at_low(n):
                for k in range(KC):
                    dve.wait_ge(at_hi, n * KC + k + 1)
                    V.tensor_tensor(at4[:, 1, k, :], bank[6 + k % 2][:], at4[:, 0, k, :].bitcast(F32), ALU.subtract).then_inc(at_ev, 1)

            def ht_low(n, c):
                m = P if c < NI - 1 else ILAST
                dve.wait_ge(ht_hi, n * NI + c + 1)
                V.tensor_tensor(ht[0:m, 1, c, :], sg[c % 2][0:m, :], ht[0:m, 0, c, :].bitcast(F32), ALU.subtract).then_inc(hm, 1)

            at_low(0)

            def group(n, last):
                for c in range(NI):
                    m = P if c < NI - 1 else ILAST
                    dve.wait_ge(silu, n * NI + c + 1)
                    V.tensor_tensor(sg[c % 2][0:m, :], bank[2 + c % 2][0:m, :], sg[c % 2][0:m, :], ALU.mult).then_inc(hmul, 1)
                    if c:
                        ht_low(n, c - 1)
                ht_low(n, NI - 1)
                if not last:
                    at_low(n + 1)
                for i in range(GT):
                    dve.wait_ge(pe_dn, n * GT + i + 1)
                    dve.wait_ge(x1b_ld[i % 2], (n * 2 + i // 2 + 1) * 16)
                    if not isinstance(n, int) or i >= 2:
                        dve.wait_ge(o_st[i % 2], (n * 2 + i // 2) * 16)
                    V.tensor_tensor(ob[i % 2][:], bank[4 + i % 2][:], x1b[i % 2][:], ALU.add).then_inc(out_add, 1)

            group(0, False)
            with dve.Fori(1, NGRP - 1) as n:
                group(n, False)
            group(NGRP - 1, True)


_NAMES = ["x", "itok_B_3_7", "itok_Bx16_0_63", "itok_B_207_1644", "L0_cond_weight", "L0_ffn_base_W", "L0_ffn_router_W",
          "L0_ffn_lora_A", "L0_ffn_lora_B", "L1_cond_Wq", "L1_cond_Wk", "L1_cond_Wv", "L1_cond_Wo", "L1_cond_q_norm_w",
          "L1_cond_k_norm_w", "L1_cond_k_cache", "L1_cond_v_cache", "L1_ffn_codebook"]


def kernel(**inputs):
    import numpy as np
    import concourse.bacc as bacc
    from concourse.bass_utils import run_bass_kernel_spmd

    nc = bacc.Bacc("TRN2", target_bir_lowering=False, num_devices=1, dynamic_dma_scratch_size=4096)
    arrays = {f"in_{n}": np.ascontiguousarray(inputs[n]) for n in _NAMES}
    arrays["idx_all"] = np.concatenate([np.asarray(inputs[f"L1_ffn_idx_{n}"]).reshape(-1) for n in ("gate", "up", "down")]).reshape(P, -1)
    half = HD // 2
    arrays["con_a"] = np.concatenate([np.eye(P), np.tile(np.arange(L), (P, 1))], 1).astype(np.float32)
    invf = (np.float32(1.0) / np.float32(10000.0) ** (np.arange(0, HD, 2, dtype=np.float32) / np.float32(HD))).astype(np.float32)
    tri = (np.arange(NE)[:, None] > np.arange(NE)[None, :]).astype(np.float32).reshape(-1)
    arrays["con_b"] = np.concatenate([np.tile(invf, (P, 1)), (np.arange(P) % S)[:, None], np.tile(tri, (P, 1))], 1).astype(np.float32)
    args = [nc.dram_tensor(n, a.shape, mybir.dt.from_np(a.dtype), kind="ExternalInput").ap() for n, a in arrays.items()]
    out = nc.dram_tensor("out", (64, S, D), F32, kind="ExternalOutput").ap()
    adaln_ffn_kernel(nc, *args, out)
    r = run_bass_kernel_spmd(nc, [arrays], core_ids=[0])
    return r.results[0]["out"]
```
